# Optimizing a Trainium2 kernel written in Bass

```python
import numpy as np
import jax
import jax.numpy as jnp

def _softmax(x, axis=-1):
    return jax.nn.softmax(x, axis=axis)

def _gelu(x):
    return jax.nn.gelu(x, approximate=True)

def _silu(x):
    return jax.nn.silu(x)

def _sigmoid(x):
    return jax.nn.sigmoid(x)

def _layernorm(x, axis=-1, eps=1e-05):
    m = jnp.mean(x, axis=axis, keepdims=True)
    v = jnp.var(x, axis=axis, keepdims=True)
    return (x - m) / jnp.sqrt(v + eps)

def _scatter_add(tgt, idx, src, axis=0):
    return tgt.at[idx].add(src)

def _segment_sum(src, seg, n):
    return jax.ops.segment_sum(src, seg, n)
kernel_name = 'mk_gnn_ffn_d1_gnn_r8_fca882'

def setup_inputs(seed: int=0):
    np.random.seed(seed)
    _w = jnp.asarray

    def _rec_inputs():
        import jax
        import jax.numpy as jnp
        _gk = jax.random.key(seed)
        x = -6.985e-05 + 0.9998 * jax.random.normal(jax.random.fold_in(_gk, 1), (1250, 512), jnp.float32)
        src = jax.random.randint(jax.random.fold_in(_gk, 2), (40000,), 0, 1250, jnp.int32)
        dst = jax.random.randint(jax.random.fold_in(_gk, 3), (40000,), 0, 1250, jnp.int32)
        _o = jnp.argsort(dst, stable=True)
        src = src[_o]
        dst = dst[_o]
        return (x, src, dst)
    x, src, dst = _rec_inputs()

    def _L0_gnn_setup():
        import jax, jax.numpy as jnp
        import numpy as np
        B = 32
        MAXN = 256
        HEADS = 8
        DH = 64
        M = 256
        D = 512
        EPS = 1e-05
        KEPS = 1e-06

        def _batchnorm(x, g, b):
            mu = jnp.mean(x, axis=0)
            var = jnp.mean((x - mu) ** 2, axis=0)
            return (x - mu) * jax.lax.rsqrt(var + EPS) * g + b

        def _forward(x, batch, edge_index, norm1_g, norm1_b, norm2_g, norm2_b, W_conv, b_conv, Wq, Wk, Wv, Wo, proj):
            N = x.shape[0]
            E = edge_index.shape[1]
            h = x
            xn = _batchnorm(x, norm1_g, norm1_b)
            msg = xn[edge_index[0]]
            agg = jax.ops.segment_sum(msg, edge_index[1], num_segments=N)
            deg = jax.ops.segment_sum(jnp.ones((E,), x.dtype), edge_index[1], num_segments=N)
            agg = agg / jnp.maximum(deg, 1.0)[:, None]
            conv_out = jax.nn.relu(agg @ W_conv + b_conv)
            counts = jax.ops.segment_sum(jnp.ones((N,), jnp.int32), batch, num_segments=B)
            offsets = jnp.concatenate([jnp.zeros((1,), jnp.int32), jnp.cumsum(counts)[:-1]])
            pos = jnp.arange(N, dtype=jnp.int32) - offsets[batch]
            h_dense = jnp.zeros((B, MAXN, D), x.dtype).at[batch, pos].set(h)
            mask = jnp.zeros((B, MAXN), bool).at[batch, pos].set(True)

            def heads(t, W):
                return (t @ W).reshape(B, MAXN, HEADS, DH).transpose(0, 2, 1, 3)
            q, k, v = (heads(h_dense, Wq), heads(h_dense, Wk), heads(h_dense, Wv))
            scale = DH ** (-0.25)

            def phi(t, is_query):
                t = t * scale
                u = jnp.einsum('bhnd,md->bhnm', t, proj)
                diag = 0.5 * jnp.sum(t * t, axis=-1, keepdims=True)
                if is_query:
                    m_ = jnp.max(u, axis=-1, keepdims=True)
                else:
                    m_ = jnp.max(u, axis=(-2, -1), keepdims=True)
                return jnp.exp(u - diag - jax.lax.stop_gradient(m_)) / np.sqrt(M) + KEPS
            qf = phi(q, True)
            kf = phi(k, False) * mask[:, None, :, None]
            vm = v * mask[:, None, :, None]
            kv = jnp.einsum('bhnm,bhnd->bhmd', kf, vm)
            z = 1.0 / (jnp.einsum('bhnm,bhm->bhn', qf, kf.sum(axis=2)) + KEPS)
            attn = jnp.einsum('bhnm,bhmd->bhnd', qf, kv) * z[..., None]
            attn = attn.transpose(0, 2, 1, 3).reshape(B, MAXN, D) @ Wo
            h_attn = attn[batch, pos]
            return _batchnorm(conv_out + h_attn + h, norm2_g, norm2_b)
        key = jax.random.key(seed)
        ks = jax.random.split(key, 10)
        sizes = 1024 + np.arange(B) * 131 % 1025
        N = int(sizes.sum())
        E = N * 8
        batch = jnp.asarray(np.repeat(np.arange(B), sizes), dtype=jnp.int32)
        edge_index = jax.random.randint(ks[0], (2, E), 0, N, dtype=jnp.int32)
        s = 1.0 / np.sqrt(D)
        return {'x': jax.random.normal(ks[1], (N, D), jnp.float32), 'batch': batch, 'edge_index': edge_index, 'norm1_g': jnp.ones((D,), jnp.float32), 'norm1_b': jnp.zeros((D,), jnp.float32), 'norm2_g': jnp.ones((D,), jnp.float32), 'norm2_b': jnp.zeros((D,), jnp.float32), 'W_conv': jax.random.normal(ks[2], (D, D), jnp.float32) * s, 'b_conv': jnp.zeros((D,), jnp.float32), 'Wq': jax.random.normal(ks[3], (D, D), jnp.float32) * s, 'Wk': jax.random.normal(ks[4], (D, D), jnp.float32) * s, 'Wv': jax.random.normal(ks[5], (D, D), jnp.float32) * s, 'Wo': jax.random.normal(ks[6], (D, D), jnp.float32) * s, 'proj': jax.random.normal(ks[7], (M, DH), jnp.float32)}
    _L0_gnn_all = _L0_gnn_setup()
    _L0_gnn_in = {k: v for k, v in _L0_gnn_all.items() if k in ('norm1_g', 'norm1_b', 'norm2_g', 'norm2_b', 'W_conv', 'b_conv', 'Wq', 'Wk', 'Wv', 'Wo', 'proj')}
    del _L0_gnn_all

    def _L0_ffn_setup():
        import jax, jax.numpy as jnp
        import numpy as np
        EPS = 1e-05
        NUM_HEADS = 8
        TOP_K = 2
        CAP_FACTOR = 2

        def layernorm(x, g, b):
            m = jnp.mean(x, axis=-1, keepdims=True)
            v = jnp.var(x, axis=-1, keepdims=True)
            return (x - m) * jax.lax.rsqrt(v + EPS) * g + b
        key = jax.random.key(seed)
        ks = jax.random.split(key, 16)
        B, S, H, E, F = (2, 256, 512, 64, 256)
        s = 0.02
        return {'x': jax.random.normal(ks[0], (B, S, H), jnp.float32), 'ln1_g': jnp.ones((H,), jnp.float32), 'ln1_b': jnp.zeros((H,), jnp.float32), 'wq': jax.random.normal(ks[1], (H, H), jnp.float32) * s, 'wk': jax.random.normal(ks[2], (H, H), jnp.float32) * s, 'wv': jax.random.normal(ks[3], (H, H), jnp.float32) * s, 'wo': jax.random.normal(ks[4], (H, H), jnp.float32) * s, 'ln2_g': jnp.ones((H,), jnp.float32), 'ln2_b': jnp.zeros((H,), jnp.float32), 'wr': jax.random.normal(ks[5], (H, E), jnp.float32) * s, 'w1': jax.random.normal(ks[6], (E, H, F), jnp.float32) * s, 'b1': jnp.zeros((E, F), jnp.float32), 'w2': jax.random.normal(ks[7], (E, F, H), jnp.float32) * s, 'b2': jnp.zeros((E, H), jnp.float32)}
    _L0_ffn_all = _L0_ffn_setup()
    _L0_ffn_in = {k: v for k, v in _L0_ffn_all.items() if k in ('ln1_g', 'ln1_b', 'wq', 'wk', 'wv', 'wo', 'ln2_g', 'ln2_b', 'wr', 'w1', 'b1', 'w2', 'b2')}
    del _L0_ffn_all
    return {'x': x, 'src': src, 'dst': dst, 'L0_gnn_norm1_g': _L0_gnn_in['norm1_g'], 'L0_gnn_norm1_b': _L0_gnn_in['norm1_b'], 'L0_gnn_norm2_g': _L0_gnn_in['norm2_g'], 'L0_gnn_norm2_b': _L0_gnn_in['norm2_b'], 'L0_gnn_W_conv': _L0_gnn_in['W_conv'], 'L0_gnn_b_conv': _L0_gnn_in['b_conv'], 'L0_gnn_Wq': _L0_gnn_in['Wq'], 'L0_gnn_Wk': _L0_gnn_in['Wk'], 'L0_gnn_Wv': _L0_gnn_in['Wv'], 'L0_gnn_Wo': _L0_gnn_in['Wo'], 'L0_gnn_proj': _L0_gnn_in['proj'], 'L0_ffn_ln1_g': _L0_ffn_in['ln1_g'], 'L0_ffn_ln1_b': _L0_ffn_in['ln1_b'], 'L0_ffn_wq': _L0_ffn_in['wq'], 'L0_ffn_wk': _L0_ffn_in['wk'], 'L0_ffn_wv': _L0_ffn_in['wv'], 'L0_ffn_wo': _L0_ffn_in['wo'], 'L0_ffn_ln2_g': _L0_ffn_in['ln2_g'], 'L0_ffn_ln2_b': _L0_ffn_in['ln2_b'], 'L0_ffn_wr': _L0_ffn_in['wr'], 'L0_ffn_w1': _L0_ffn_in['w1'], 'L0_ffn_b1': _L0_ffn_in['b1'], 'L0_ffn_w2': _L0_ffn_in['w2'], 'L0_ffn_b2': _L0_ffn_in['b2']}

def reference(x, src, dst, L0_gnn_norm1_g, L0_gnn_norm1_b, L0_gnn_norm2_g, L0_gnn_norm2_b, L0_gnn_W_conv, L0_gnn_b_conv, L0_gnn_Wq, L0_gnn_Wk, L0_gnn_Wv, L0_gnn_Wo, L0_gnn_proj, L0_ffn_ln1_g, L0_ffn_ln1_b, L0_ffn_wq, L0_ffn_wk, L0_ffn_wv, L0_ffn_wo, L0_ffn_ln2_g, L0_ffn_ln2_b, L0_ffn_wr, L0_ffn_w1, L0_ffn_b1, L0_ffn_w2, L0_ffn_b2):
    import jax
    import jax.numpy as jnp

    def _L0_gnn_ref(x, batch, edge_index, norm1_g, norm1_b, norm2_g, norm2_b, W_conv, b_conv, Wq, Wk, Wv, Wo, proj):
        import jax, jax.numpy as jnp
        import numpy as np
        B = 32
        MAXN = 256
        HEADS = 8
        DH = 64
        M = 256
        D = 512
        EPS = 1e-05
        KEPS = 1e-06

        def _batchnorm(x, g, b):
            mu = jnp.mean(x, axis=0)
            var = jnp.mean((x - mu) ** 2, axis=0)
            return (x - mu) * jax.lax.rsqrt(var + EPS) * g + b

        def _forward(x, batch, edge_index, norm1_g, norm1_b, norm2_g, norm2_b, W_conv, b_conv, Wq, Wk, Wv, Wo, proj):
            N = x.shape[0]
            E = edge_index.shape[1]
            h = x
            xn = _batchnorm(x, norm1_g, norm1_b)
            msg = xn[edge_index[0]]
            agg = jax.ops.segment_sum(msg, edge_index[1], num_segments=N)
            deg = jax.ops.segment_sum(jnp.ones((E,), x.dtype), edge_index[1], num_segments=N)
            agg = agg / jnp.maximum(deg, 1.0)[:, None]
            conv_out = jax.nn.relu(agg @ W_conv + b_conv)
            counts = jax.ops.segment_sum(jnp.ones((N,), jnp.int32), batch, num_segments=B)
            offsets = jnp.concatenate([jnp.zeros((1,), jnp.int32), jnp.cumsum(counts)[:-1]])
            pos = jnp.arange(N, dtype=jnp.int32) - offsets[batch]
            h_dense = jnp.zeros((B, MAXN, D), x.dtype).at[batch, pos].set(h)
            mask = jnp.zeros((B, MAXN), bool).at[batch, pos].set(True)

            def heads(t, W):
                return (t @ W).reshape(B, MAXN, HEADS, DH).transpose(0, 2, 1, 3)
            q, k, v = (heads(h_dense, Wq), heads(h_dense, Wk), heads(h_dense, Wv))
            scale = DH ** (-0.25)

            def phi(t, is_query):
                t = t * scale
                u = jnp.einsum('bhnd,md->bhnm', t, proj)
                diag = 0.5 * jnp.sum(t * t, axis=-1, keepdims=True)
                if is_query:
                    m_ = jnp.max(u, axis=-1, keepdims=True)
                else:
                    m_ = jnp.max(u, axis=(-2, -1), keepdims=True)
                return jnp.exp(u - diag - jax.lax.stop_gradient(m_)) / np.sqrt(M) + KEPS
            qf = phi(q, True)
            kf = phi(k, False) * mask[:, None, :, None]
            vm = v * mask[:, None, :, None]
            kv = jnp.einsum('bhnm,bhnd->bhmd', kf, vm)
            z = 1.0 / (jnp.einsum('bhnm,bhm->bhn', qf, kf.sum(axis=2)) + KEPS)
            attn = jnp.einsum('bhnm,bhmd->bhnd', qf, kv) * z[..., None]
            attn = attn.transpose(0, 2, 1, 3).reshape(B, MAXN, D) @ Wo
            h_attn = attn[batch, pos]
            return _batchnorm(conv_out + h_attn + h, norm2_g, norm2_b)
        return _forward(x, batch, edge_index, norm1_g, norm1_b, norm2_g, norm2_b, W_conv, b_conv, Wq, Wk, Wv, Wo, proj)

    def _L0_ffn_ref(x, ln1_g, ln1_b, wq, wk, wv, wo, ln2_g, ln2_b, wr, w1, b1, w2, b2):
        import jax, jax.numpy as jnp
        import numpy as np
        EPS = 1e-05
        NUM_HEADS = 8
        TOP_K = 2
        CAP_FACTOR = 2

        def layernorm(x, g, b):
            m = jnp.mean(x, axis=-1, keepdims=True)
            v = jnp.var(x, axis=-1, keepdims=True)
            return (x - m) * jax.lax.rsqrt(v + EPS) * g + b
        B, S, H = x.shape
        NH = NUM_HEADS
        dh = H // NH
        x1 = layernorm(x, ln1_g, ln1_b)
        q = (x1 @ wq).reshape(B, S, NH, dh)
        k = (x1 @ wk).reshape(B, S, NH, dh)
        v = (x1 @ wv).reshape(B, S, NH, dh)
        scores = jnp.einsum('bqhd,bkhd->bhqk', q, k) * dh ** (-0.5)
        p = jax.nn.softmax(scores, axis=-1)
        attn_out = jnp.einsum('bhqk,bkhd->bqhd', p, v).reshape(B, S, H) @ wo
        x = x + attn_out
        x2 = layernorm(x, ln2_g, ln2_b).reshape(B * S, H)
        T = B * S
        E = wr.shape[1]
        C = CAP_FACTOR * (T * TOP_K // E)
        probs = jax.nn.softmax(x2 @ wr, axis=-1)
        gate_v, gate_i = jax.lax.top_k(probs, TOP_K)
        gate_v = gate_v / jnp.sum(gate_v, axis=-1, keepdims=True)
        ef = gate_i.reshape(-1)
        gf = gate_v.reshape(-1)
        oh = jax.nn.one_hot(ef, E, dtype=x2.dtype)
        pos = jnp.sum((jnp.cumsum(oh, axis=0) - oh) * oh, axis=1).astype(jnp.int32)
        keep = (pos < C).astype(x2.dtype)
        posc = jnp.minimum(pos, C - 1)
        tok = jnp.repeat(x2, TOP_K, axis=0) * keep[:, None]
        buf = jnp.zeros((E, C, H), x2.dtype).at[ef, posc].add(tok)
        h = jax.nn.gelu(jnp.einsum('ech,ehf->ecf', buf, w1) + b1[:, None, :])
        y = jnp.einsum('ecf,efh->ech', h, w2) + b2[:, None, :]
        ys = y[ef, posc] * (gf * keep)[:, None]
        moe_out = ys.reshape(T, TOP_K, H).sum(axis=1).reshape(B, S, H)
        return x + moe_out
    edge_index = jnp.stack([src, dst])
    batch0 = jnp.zeros((1250,), jnp.int32)
    x = x + _L0_gnn_ref(_layernorm(x, axis=-1), batch0, edge_index, L0_gnn_norm1_g, L0_gnn_norm1_b, L0_gnn_norm2_g, L0_gnn_norm2_b, L0_gnn_W_conv, L0_gnn_b_conv, L0_gnn_Wq, L0_gnn_Wk, L0_gnn_Wv, L0_gnn_Wo, L0_gnn_proj)
    x = x + _L0_ffn_ref(_layernorm(x, axis=-1)[None], L0_ffn_ln1_g, L0_ffn_ln1_b, L0_ffn_wq, L0_ffn_wk, L0_ffn_wv, L0_ffn_wo, L0_ffn_ln2_g, L0_ffn_ln2_b, L0_ffn_wr, L0_ffn_w1, L0_ffn_b1, L0_ffn_w2, L0_ffn_b2)[0]
    return x

_drawn_inputs = setup_inputs


def setup_inputs(seed=0):
    import zlib

    import numpy as np

    out = dict(_drawn_inputs(seed))
    spreads = {'L0_gnn_norm1_g': (1.0, 0.6),
     'L0_gnn_norm1_b': (0.0, 0.391),
     'L0_gnn_norm2_g': (1.0, 0.2),
     'L0_gnn_norm2_b': (0.0, 0.1),
     'L0_gnn_b_conv': (0.0, 0.403),
     'L0_ffn_ln1_g': (1.0, 0.6),
     'L0_ffn_ln1_b': (0.0, 0.8),
     'L0_ffn_ln2_g': (1.0, 0.6),
     'L0_ffn_ln2_b': (0.0, 0.681),
     'L0_ffn_b1': (0.0, 2.0),
     'L0_ffn_b2': (0.0, 1.622)}
    factors = {'L0_gnn_Wq': 4.441,
     'L0_gnn_Wk': 5.027,
     'L0_gnn_Wv': 40.584,
     'L0_gnn_Wo': 40.544,
     'L0_gnn_proj': 4.66,
     'L0_ffn_wq': 8.0,
     'L0_ffn_wk': 8.0,
     'L0_ffn_wv': 6.282,
     'L0_ffn_wo': 5.951,
     'L0_ffn_w1': 2.905,
     'L0_ffn_w2': 2.718}
    for name, (base, spread) in spreads.items():
        noise = np.random.default_rng([zlib.crc32(name.encode()), seed]).standard_normal(out[name].shape)
        drawn = base * np.exp(spread * noise) if base else spread * noise
        out[name] = jnp.asarray(drawn.astype(out[name].dtype))
    for name, factor in factors.items():
        out[name] = (out[name] * factor).astype(out[name].dtype)
    return out
```

```python
import numpy as np
import concourse.bass as bass
from concourse import mybir
from contextlib import ExitStack


class Link:

    def __init__(self, eng, sem):
        self.eng, self.sem, self.n = eng, sem, 0

    def __call__(self, ins, base=0):
        self.n += 1
        ins.then_inc(self.sem, 1)
        self.eng.wait_ge(self.sem, base + self.n)


def build(nc, x, src, dst, n1g, n1b, n2g, n2b, w_conv, b_conv, gwq, gwk, gwv, gwo, proj,
          l1g, l1b, fwq, fwk, fwv, fwo, l2g, l2b, wr, w1, b1, w2, b2, out):
    f32, bf16, f16 = mybir.dt.float32, mybir.dt.bfloat16, mybir.dt.float16
    i32, u32 = mybir.dt.int32, mybir.dt.uint32
    ALU, ACT = mybir.AluOpType, mybir.ActivationFunctionType
    AXX = mybir.AxisListType.X
    RMAX = bass.bass_isa.ReduceOp.max

    P = 128
    N, D = x.shape
    E = src.shape[0]
    KD = D // P
    NT = -(-N // P)
    TAIL = N - (NT - 1) * P

    def sz(t):
        return P if t < NT - 1 else TAIL

    HEADS = 8
    DH = D // HEADS
    PAIRS = HEADS // 2
    M = proj.shape[0]
    SEQ = 256
    NQ = SEQ // P
    EPS, KEPS = 1e-5, 1e-6
    NEXP, _, F = w1.shape
    TOPK, CAP = 2, 2 * (N * 2 // NEXP)
    SLOTS = NEXP * CAP
    BN = [(0, 417), (417, 834), (834, N)]
    COLS = [(c, min(c + 512, N)) for c in range(0, N, 512)]

    ROWS = E // P
    LEFT = E - ROWS * P
    PADC = 4
    WIN = 40
    STEP = 32
    ECOLS = PADC + 384
    NB = 4
    U = 2 * NT
    PTS = 3 * U + 2
    FULL = 320

    ctx = ExitStack()
    with ctx:
        def sb(name, shape, dt=f32):
            return ctx.enter_context(nc.sbuf_tensor(name, shape, dt))

        def sem(name):
            return ctx.enter_context(nc.semaphore(name))

        xr = sb("xr", [P, NT, D])
        r2 = sb("r2", [P, NT, D])
        tA = sb("tA", [P, KD, N])
        tB = sb("tB", [P, 4 * N])
        arena = sb("arena", [P, 12500 + 8 * 2048])
        iota16 = sb("iota16", [P, NT * P], f16)
        identf = sb("identf", [P, P])
        tri = sb("tri", [P, P], bf16)
        onesb = sb("onesb", [P, P], bf16)
        onesf = sb("onesf", [P, 1])
        halfblk = sb("halfblk", [P, 2])
        iota64 = sb("iota64", [P, NEXP])
        tokid = sb("tokid", [P, NT], i32)
        zint = sb("zint", [P, SLOTS // P], i32)
        par = sb("par", [P, 28])
        b1T = sb("b1T", [P, P])
        wr_s = sb("wr_s", [P, KD, NEXP])
        b2_s = sb("b2_s", [NEXP, D])
        st = sb("st", [P, NT, 6])
        mv = sb("mv", [P, NT, 2])
        rs = sb("rs", [P, NT])
        bst = sb("bst", [P, KD, 3, 6])
        bmv = sb("bmv", [P, KD, 2])
        ab = sb("ab", [P, 3, KD])
        deg = sb("deg", [P, NT])
        rdeg = sb("rdeg", [P, NT])
        tot = sb("tot", [P, 2])
        flag = sb("flag", [1, 1], i32)
        v8 = sb("v8", [P, NT, 8])
        i8 = sb("i8", [P, NT, 8], u32)
        gk = sb("gk", [P, 8, NT, 2])
        ssum = sb("ssum", [P, NT])
        slot_i = sb("slot_i", [P, NT, 2], i32)
        sidx_i = sb("sidx_i", [P, NT, 2], i32)
        tabr = sb("tabr", [NEXP, CAP], i32)
        tabf = sb("tabf", [NEXP, CAP])
        tabT = sb("tabT", [CAP, NEXP], i32)
        nmx = sb("nmx", [P, 2])
        esum = sb("esum", [P, 2])
        resum = sb("resum", [P, 4])
        arow = sb("arow", [P, 2, P])
        ps = ctx.enter_context(nc.psum_tensor("ps", [P, 8, 512], f32))
        psf = ps[:, :, :].rearrange("p b c -> p (b c)")

        def view(t, off, *dims):
            n = int(np.prod(dims))
            v = t[:, off:off + n]
            if len(dims) == 2:
                v = v.rearrange("p (a b) -> p a b", a=dims[0])
            if len(dims) == 3:
                v = v.rearrange("p (a b c) -> p a b c", a=dims[0], b=dims[1])
            return v

        er_i = arena[:, 0:1024].bitcast(i32).rearrange("p (s b c) -> p s b c", s=2, b=4)
        er_f = view(arena, 1024, 2, 4, P)
        pj = view(arena, 2048, 2, 2, DH)
        b1r = arena[:, 2304:2432]
        prow = arena[0:28, 2432:2560]
        projblk = view(arena, 11400, 2, M)
        qk = view(arena, 0, 2, PAIRS, SEQ)
        vaug = view(arena, 2048, NQ, HEADS, DH + 1)
        qf = view(arena, 3100, NQ, HEADS, M)
        kf = view(arena, 7200, NQ, HEADS, M)
        sq = view(arena, 7200, 2, PAIRS, SEQ)
        qfT = view(tB, 0, 2, M // P, SEQ)
        kv = view(tB, 1024, HEADS, M // P, DH + 1)
        attnrow = view(tB, 2064, NQ, D)
        attnTg = view(tB, 0, KD, SEQ)
        hatt = view(tB, 3088, KD, SEQ)
        dg = view(tB, 4112, 2, NQ, HEADS)
        mk = view(tB, 4150, NQ, HEADS)
        mk8 = tB[:, 4170:4178]
        gmk = tB[:, 4180:4188]
        bk = view(tB, 4190, NQ, HEADS)
        bq = view(tB, 4210, NQ, HEADS)
        zr = view(tB, 4230, 2, 2)
        gw = [view(arena, 12500 + 2048 * i, KD, D) for i in range(4)]
        A = view(arena, 0, NT, N)
        AT = view(arena, 12500, 2, NT, 512)
        wc = view(arena, 22740, KD, D)
        ohs = arena[:, 24788:24788 + NB * 640].bitcast(bf16).rearrange("p (b c) -> p b c", b=NB)
        ohd = arena[:, 27348:27348 + NB * 64].bitcast(bf16).rearrange("p (b c) -> p b c", b=NB)
        ef = view(arena, 27604, 2, ECOLS)
        aggT = view(tB, 0, KD, 512)
        rl = view(tB, 2048, 2, 512)
        nrow = view(arena, 0, NT, D)
        QT = view(arena, 0, 2, N)
        KT = arena[:, 2500:2500 + N]
        V = view(arena, 3750, NT, P)
        Pb = view(arena, 5030, 2, N)
        PT = view(arena, 7530, 2, NT, P)
        wst = view(arena, 10090, 3, KD, P)
        g2row = view(arena, 9024, 2, D)
        wo_s = view(arena, 10090, KD, D)
        attnT = view(tB, 0, KD, N)
        x2T = view(arena, 5120, 2, KD, P)
        lg = view(arena, 6144, NT, NEXP)
        ex = view(arena, 6784, NT, NEXP)
        ohk = [view(arena, 7424 + 640 * k, NT, NEXP) for k in range(2)]
        O = arena[:, 8704:9024].bitcast(bf16).rearrange("p (t e) -> p t e", t=NT)
        posm = view(arena, 9024, NT, NEXP)
        tmp = view(arena, 9664, NT, NEXP)
        G = view(arena, 10304, NT, NEXP)
        GT = tB[0:NEXP, 0:N]
        RW = 8
        ring = [view(arena, 12500 + 2048 * i, 2048) for i in range(RW)]
        ring1 = [r[:, 0:1024].rearrange("p (k f) -> p k f", k=KD) for r in ring]
        ring2 = [r[:, 1024:2048].rearrange("p (k f) -> p k f", k=F // P) for r in ring]
        tAf = tA[:, :, :].rearrange("p k n -> p (k n)")
        XB = 4
        xb = view(tAf, 0, XB, D)
        xT = view(tAf, 2048, 2, KD, CAP)
        hT = view(tAf, 2048 + 624, 2, F // P, CAP)
        ys = view(tAf, 2048 + 624 + 312, 2, D)
        ygat = view(arena, 0, 4, D)

        x2d = nc.dram_tensor("x2d", [N, D], f32).ap()
        tabd = nc.dram_tensor("tabd", [SLOTS, 1], i32).ap()
        yd = nc.dram_tensor("yd", [SLOTS, D], f32).ap()

        names = """x_in edges_in params_in gw_in wc_in wst_in wo_in route_in ln2_in tab_zeroed x2_out tab_scattered
            tab_in out_stored consts pool_link dve_link act_link raw_ready raw_T ef_ready par_T par_ready b1_ready
            var_ready sd_ready h_ready h_T hT_ready bvar_ready bsd_ready xnT_ready xn_T xn_ready
            qk_mm qk_ready v_mm v_ready sq_ready dg_mm u_mm uk_copied uk_maxed uq_bias uq_exp mk_ready gmk_ready
            bk_ready kexp_done kf_ready qf_ready kv_mm kv_ready qfT_mm qfT_ready ga_mm ga_ready ga_T gaT_ready
            ho_mm hatt_ready oh_ready oh_used cnt_ready gcnt_oh_ready gcnt_oh_used gcnt_ready
            tot_ready tot_mm flag_ready An_ready AT_mm AT_act AT_dve agg_mm agg_ready conv_mm rl_ready z_ready
            w_ready w_T x1_ready n1_ready n1_T n1T_raw x1T_ready qpad_ready proj_done
            qkv_act qkv_dve s_mm negmax exp_done p_T pt_dve pt_act
            wo_mm xx_ready x2_ready x2_T x2T_ready lg_mm exs_ready exp_ready O_ready pos_mm idx_ready G_ready G_T GT_ready
            tabf_ready tab_T tabT_ready xT_mm xT_ready l1_mm gelu_done l2_mm y_ready
            b2_mm loop_link acc_ready""".split()
        S = {n: sem(n) for n in names}
        w_in = [sem(f"w_in{i}") for i in range(RW)]
        xb_in = [sem(f"xb_in{i}") for i in range(XB)]
        y_stored = [sem(f"y_stored{i}") for i in range(2)]
        yg_in = [sem(f"yg_in{i}") for i in range(4)]

        block = ctx.enter_context(nc.Block())

        @block.sync
        def _(sp):
            full = (NT - 1) * P
            sp.dma_start(xr[:, 0:NT - 1, :], x[0:full, :].rearrange("(t p) d -> p t d", p=P)).then_inc(S["x_in"], 16)
            sp.dma_start(xr[0:TAIL, NT - 1, :], x[full:N, :]).then_inc(S["x_in"], 16)
            for i, v in enumerate((src, dst)):
                rows = v[0:ROWS * P].rearrange("(r c) -> r c", c=P)
                sp.dma_start(er_i[:, i, 0:2, :], rows[0:2 * P, :].rearrange("(b p) c -> p b c", p=P)).then_inc(S["edges_in"], 16)
                sp.dma_start(er_i[0:ROWS - 2 * P, i, 2, :], rows[2 * P:ROWS, :]).then_inc(S["edges_in"], 16)
                sp.dma_start(er_i[0:1, i, 3, 0:LEFT], v[ROWS * P:E].rearrange("(a n) -> a n", a=1)).then_inc(S["edges_in"], 16)
            for i, v in enumerate((n1g, n1b, n2g, n2b, b_conv, l1g, l1b)):
                sp.dma_start(prow[KD * i:KD * i + KD, :], v.rearrange("(k p) -> k p", p=P)).then_inc(S["params_in"], 16)
            sp.dma_start(b1r[:, :], b1.rearrange("e (h p) -> (e h) p", p=P)).then_inc(S["params_in"], 16)
            for dup in range(2):
                sp.dma_start(pj[:, :, dup, :], proj.rearrange("(t p) d -> p t d", p=P)).then_inc(S["params_in"], 16)
            for i, w in enumerate((gwq, gwk, gwv, gwo)):
                sp.dma_start(gw[i], w.rearrange("(k p) n -> p k n", p=P)).then_inc(S["gw_in"], 16)
            sp.dma_start(wc, w_conv.rearrange("(k p) n -> p k n", p=P)).then_inc(S["wc_in"], 16)
            sp.dma_start(wr_s[:, :, :], wr.rearrange("(k p) n -> p k n", p=P)).then_inc(S["route_in"], 16)
            sp.dma_start(b2_s[:, :], b2).then_inc(S["route_in"], 16)
            sp.wait_ge(S["consts"], 1)
            sp.dma_start(tabd.rearrange("(p c) a -> p (c a)", p=P), zint[:, :]).then_inc(S["tab_zeroed"], 16)
            sp.wait_ge(S["conv_mm"], 3 * KD)

            def load_expert(slot, w1e, w2e):
                sp.dma_start(ring1[slot], w1e).then_inc(w_in[slot], 16)
                sp.dma_start(ring2[slot], w2e).then_inc(w_in[slot], 16)

            w1v = w1.rearrange("e (k p) f -> e p k f", p=P)
            w2v = w2.rearrange("e (k p) n -> e p k n", p=P)
            qv, kvv, vv = (w.rearrange("(k p) n -> p k n", p=P) for w in (fwq, fwk, fwv))
            for e in range(RW):
                load_expert(e, w1v[e], w2v[e])
            with sp.Fori(0, PAIRS) as pr:
                sp.wait_ge(S["proj_done"], pr + 1)
                for i, w in enumerate((qv, kvv, vv)):
                    sp.dma_start(wst[:, i, :, :], w[:, :, bass.ds(pr * P, P)]).then_inc(S["wst_in"], 16)

            sp.wait_ge(S["proj_done"], PAIRS + 1)
            sp.dma_start(wo_s, fwo.rearrange("(k p) n -> p k n", p=P)).then_inc(S["wo_in"], 16)
            sp.wait_ge(S["pt_dve"], PAIRS * (2 * U + 2) + 1)
            sp.dma_start(g2row[:, 0, :], l2g.rearrange("(a n) -> a n", a=1).to_broadcast([P, D])).then_inc(S["ln2_in"], 16)
            sp.dma_start(g2row[:, 1, :], l2b.rearrange("(a n) -> a n", a=1).to_broadcast([P, D])).then_inc(S["ln2_in"], 16)
            for t in range(NT):
                sp.wait_ge(S["x2_ready"], t + 1)
                sp.dma_start(x2d[t * P:t * P + sz(t), :], nrow[0:sz(t), t, :]).then_inc(S["x2_out"], 16)
            sp.wait_ge(S["tab_scattered"], 32 * NT)
            sp.dma_start(tabr[:, :], tabd.rearrange("(e c) a -> e (c a)", c=CAP)).then_inc(S["tab_in"], 16)

            with sp.Fori(0, NEXP // RW - 1) as it:
                for j in range(RW):
                    sp.wait_ge(S["l2_mm"], it * RW + (j + 3))
                    load_expert(j, w1v[bass.ds(it * RW + (j + RW), 1)].rearrange("e p k f -> p (e k) f"),
                                w2v[bass.ds(it * RW + (j + RW), 1)].rearrange("e p k f -> p (e k) f"))
                    sp.wait_ge(S["y_ready"], it * RW + (j + 3))
                    sp.dma_start(yd[bass.ds(it * (RW * CAP) + j * CAP, CAP), :], ys[0:CAP, j % 2, :]).then_inc(y_stored[j % 2], 16)
            for s in range(NEXP - RW, NEXP):
                sp.wait_ge(S["y_ready"], s + 3)
                sp.dma_start(yd[s * CAP:(s + 1) * CAP, :], ys[0:CAP, s % 2, :]).then_inc(y_stored[s % 2], 16)
            for t in range(NT):
                sp.wait_ge(S["acc_ready"], t + 1)
                sp.dma_start(out[t * P:t * P + sz(t), :], xr[0:sz(t), t, :]).then_inc(S["out_stored"], 16)
            sp.wait_ge(S["out_stored"], 16 * NT)

        @block.gpsimd
        def _(pool):
            link = Link(pool, S["pool_link"])
            nc.gpsimd.memset(zint[:, :], 0).then_inc(S["consts"], 1)
            nc.gpsimd.iota(iota16[:, :], pattern=[[1, NT * P]], base=0, channel_multiplier=0,
                           allow_small_or_imprecise_dtypes=True)
            nc.gpsimd.iota(iota64[:, :], pattern=[[1, NEXP]], base=0, channel_multiplier=0,
                           allow_small_or_imprecise_dtypes=True)
            nc.gpsimd.iota(tokid[:, :], pattern=[[P, NT]], base=0, channel_multiplier=1)
            nc.gpsimd.memset(onesb[:, :], 1.0)
            nc.gpsimd.memset(tri[:, :], 1.0)
            link(nc.gpsimd.memset(identf[:, :], 0.0))
            nc.gpsimd.affine_select(out=identf[:, :], in_=identf[:, :], compare_op=ALU.not_equal, fill=1.0, base=0,
                                    pattern=[[-1, P]], channel_multiplier=1)
            nc.gpsimd.affine_select(out=tri[:, :], in_=tri[:, :], compare_op=ALU.is_gt, fill=0.0, base=0,
                                    pattern=[[1, P]], channel_multiplier=-1).then_inc(S["consts"], 1)
            pool.wait_ge(S["mk_ready"], 1)
            nc.gpsimd.partition_all_reduce(gmk, mk8, P, RMAX).then_inc(S["gmk_ready"], 1)
            pool.wait_ge(S["n1_T"], NT)
            nc.gpsimd.memset(QT[64:128, 0, :], 0.0)
            nc.gpsimd.memset(QT[0:64, 1, :], 0.0).then_inc(S["qpad_ready"], 1)
            pool.wait_ge(S["idx_ready"], 1)
            pool.wait_ge(S["tab_zeroed"], 16)
            for t in range(NT):
                for k in range(TOPK):
                    nc.gpsimd.indirect_dma_start(
                        out=tabd, out_offset=bass.IndirectOffsetOnAxis(ap=sidx_i[0:sz(t), t, k:k + 1], axis=0),
                        in_=tokid[0:sz(t), t:t + 1], in_offset=None,
                        bounds_check=SLOTS - 1, oob_is_err=False).then_inc(S["tab_scattered"], 16)
            pool.wait_ge(S["tabT_ready"], 1)
            pool.wait_ge(S["x2_out"], 16 * NT)
            for e in range(NEXP):
                if e >= XB:
                    pool.wait_ge(S["xT_mm"], e - XB + 1)
                nc.gpsimd.indirect_dma_start(
                    out=xb[0:CAP, e % XB, :], out_offset=None, in_=x2d,
                    in_offset=bass.IndirectOffsetOnAxis(ap=tabT[:, e:e + 1], axis=0)).then_inc(xb_in[e % XB], 16)
            for k in range(2):
                pool.wait_ge(y_stored[k], 16 * (NEXP // 2) + 16)
            for t in range(NT):
                for k in range(TOPK):
                    n = t * TOPK + k
                    if n >= 4:
                        pool.wait_ge(S["acc_ready"], (n - 4) // TOPK + 1)
                    nc.gpsimd.indirect_dma_start(
                        out=ygat[0:sz(t), n % 4, :], out_offset=None, in_=yd,
                        in_offset=bass.IndirectOffsetOnAxis(ap=slot_i[0:sz(t), t, k:k + 1], axis=0)).then_inc(yg_in[n % 4], 16)

        @block.scalar
        def _(act):
            act_ = nc.scalar.activation
            act.wait_ge(S["var_ready"], 1)
            act_(rs[:, :], rs[:, :], ACT.Sqrt).then_inc(S["sd_ready"], 1)
            for t in range(NT):
                act.wait_ge(S["h_T"], t + 1)
                act_(tA[:, :, t * P:t * P + sz(t)], ps[:, 2 + t % 2, :].rearrange("p (k c) -> p k c", k=KD)[:, :, 0:sz(t)],
                     ACT.Copy).then_inc(S["hT_ready"], 1)
            act.wait_ge(S["bvar_ready"], 1)
            act_(ab[:, 0, :], ab[:, 0, :], ACT.Sqrt).then_inc(S["bsd_ready"], 1)
            for t in range(NT):
                act.wait_ge(S["xn_T"], t + 1)
                act_(r2[0:sz(t), t, :], ps[0:sz(t), 2 + t % 2, :], ACT.Copy).then_inc(S["xn_ready"], 1)

            for p in range(PAIRS):
                act.wait_ge(S["qk_mm"], p + 1)
                act_(qk[:, :, p, :], ps[:, p % 2, :].rearrange("p (s c) -> p s c", s=2), ACT.Copy,
                     scale=float(DH) ** -0.25).then_inc(S["qk_ready"], 1)
            act.wait_ge(S["qk_ready"], PAIRS)
            act_(sq, qk, ACT.Square).then_inc(S["sq_ready"], 1)
            act.wait_ge(S["dg_mm"], 1)
            for u in range(NQ * PAIRS):
                nt, p = divmod(u, PAIRS)
                act.wait_ge(S["u_mm"], u + 1)
                act_(kf[:, nt, 2 * p:2 * p + 2, :], ps[:, 5 + u % 3, :].rearrange("p (h m) -> p h m", h=2),
                     ACT.Copy).then_inc(S["uk_copied"], 1)
            for u in range(NQ * PAIRS):
                nt, p = divmod(u, PAIRS)
                act.wait_ge(S["uq_bias"], u + 1)
                for h in range(2):
                    act_(qf[:, nt, 2 * p + h, :], ps[:, 5 + (u + 8) % 3, h * M:(h + 1) * M], ACT.Exp,
                         bias=bq[:, nt, 2 * p + h:2 * p + h + 1]).then_inc(S["uq_exp"], 1)
            act.wait_ge(S["bk_ready"], 1)
            act.wait_ge(S["uk_copied"], NQ * PAIRS)
            for nt in range(NQ):
                for h in range(HEADS):
                    act_(kf[:, nt, h, :], kf[:, nt, h, :], ACT.Exp, bias=bk[:, nt, h:h + 1]).then_inc(S["kexp_done"], 1)
            for h in range(HEADS):
                act.wait_ge(S["qfT_mm"], h + 1)
                if h >= 2:
                    act.wait_ge(S["ga_mm"], h - 1)
                act_(qfT[:, h % 2, :, :], ps[:, 4 + h % 2, :].rearrange("p (m n) -> p m n", m=M // P),
                     ACT.Copy).then_inc(S["qfT_ready"], 1)
            for b in range(2):
                act.wait_ge(S["ga_T"], b + 1)
                act_(attnTg[:, 2 * b:2 * b + 2, :], ps[:, b, :].rearrange("p (k n) -> p k n", k=2), ACT.Copy).then_inc(S["gaT_ready"], 1)
            for b in range(2):
                act.wait_ge(S["ho_mm"], b + 1)
                act_(hatt[:, 2 * b:2 * b + 2, :], ps[:, 2 + b, :].rearrange("p (k n) -> p k n", k=2), ACT.Copy).then_inc(S["hatt_ready"], 1)

            for t in range(NT):
                act.wait_ge(S["oh_used"], NB + (t + 1) * WIN)
                b = 1536 * (t % 2)
                act_(A[:, t, :], psf[:, b:b + N], ACT.Copy, accum_out=deg[:, t:t + 1]).then_inc(S["cnt_ready"], 1)
            act.wait_ge(S["flag_ready"], 1)
            total = act.value_load(flag[0:1, 0:1], min_val=0, max_val=E)
            with act.If(total < E):
                for t in range(NT):
                    act.wait_ge(S["gcnt_oh_used"], NB + (t + 1) * FULL)
                    b = 1536 * (t % 2)
                    act_(A[:, t, :], psf[:, b:b + N], ACT.Copy, accum_out=deg[:, t:t + 1]).then_inc(S["gcnt_ready"], 1)
            for c, (c0, c1) in enumerate(COLS):
                cn = c1 - c0
                for kt in range(1, NT, 2):
                    act.wait_ge(S["AT_mm"], c * NT + kt + 1)
                    if c == 2 and kt == 1:
                        act.wait_ge(S["agg_mm"], KD)
                    act_(AT[0:sz(kt), c % 2, kt, 0:cn], ps[0:sz(kt), kt % 2, 0:cn], ACT.Copy).then_inc(S["AT_act"], 1)
                for fo in range(KD):
                    n = c * KD + fo
                    act.wait_ge(S["conv_mm"], n + 1)
                    if n >= 2:
                        act.wait_ge(S["z_ready"], n - 1)
                    act_(rl[:, n % 2, 0:cn], ps[:, 6 + n % 2, 0:cn], ACT.Relu,
                         bias=par[:, 4 * KD + fo:4 * KD + fo + 1]).then_inc(S["rl_ready"], 1)
            act.wait_ge(S["bvar_ready"], 2)
            act_(ab[:, 0, :], ab[:, 0, :], ACT.Sqrt).then_inc(S["bsd_ready"], 1)
            for r in range(2):
                act.wait_ge(S["var_ready"], 2 + r)
                act_(rs[:, :], rs[:, :], ACT.Sqrt).then_inc(S["sd_ready"], 1)
            for t in range(NT):
                act.wait_ge(S["n1_T"], t + 1)
                act_(tA[:, :, t * P:t * P + sz(t)], ps[:, 2 + t % 2, :].rearrange("p (k c) -> p k c", k=KD)[:, :, 0:sz(t)],
                     ACT.Copy).then_inc(S["n1T_raw"], 1)

            with act.Fori(0, PAIRS) as pr:
                act.wait_ge(S["proj_done"], pr + 2)
                for h in range(2):
                    half = slice(h * DH, (h + 1) * DH)
                    act_(QT[half, h, :], psf[half, 0:N], ACT.Copy, scale=float(DH) ** -0.5).then_inc(S["qkv_act"], 1)
                act_(V[:, 0:4, :], ps[:, 6, :].rearrange("p (t c) -> p t c", t=4), ACT.Copy).then_inc(S["qkv_act"], 1)
                act_(V[:, 8, :], ps[:, 2, 256:384], ACT.Copy).then_inc(S["qkv_act"], 1)
                act_(V[0:TAIL, 9, :], ps[0:TAIL, 2, 384:512], ACT.Copy).then_inc(S["qkv_act"], 1)

                def exp_unit(i):
                    qt = sz(i // 2)
                    act.wait_ge(S["negmax"], pr * U + (i + 1))
                    if i >= 2:
                        act.wait_ge(S["p_T"], pr * PTS + 3 * (i - 1))
                    act_(Pb[0:qt, i % 2, :], psf[0:qt, 1536 * (i % 2):1536 * (i % 2) + N], ACT.Exp,
                         bias=nmx[0:qt, i % 2:i % 2 + 1],
                         accum_out=esum[0:qt, i % 2:i % 2 + 1]).then_inc(S["exp_done"], 1)

                exp_unit(0)
                for i in range(U):
                    if i + 1 < U:
                        exp_unit(i + 1)
                    act.wait_ge(S["p_T"], pr * PTS + 3 * i + 2)
                    act_(PT[:, i % 2, 4:8, 0:sz(i // 2)],
                         ps[:, 6 + (3 * i + 1) % 2, :].rearrange("p (t c) -> p t c", t=4)[:, :, 0:sz(i // 2)],
                         ACT.Copy).then_inc(S["pt_act"], 1)

            act.wait_ge(S["var_ready"], 4)
            act_(rs[:, :], rs[:, :], ACT.Sqrt).then_inc(S["sd_ready"], 1)
            for t in range(NT):
                act.wait_ge(S["x2_T"], t + 1)
                if t >= 2:
                    act.wait_ge(S["lg_mm"], t - 1)
                act_(x2T[:, t % 2, :, 0:sz(t)], ps[:, 2 + t % 2, :].rearrange("p (k c) -> p k c", k=KD)[:, :, 0:sz(t)],
                     ACT.Copy).then_inc(S["x2T_ready"], 1)
            act.wait_ge(S["exs_ready"], 1)
            act_(ex, ex, ACT.Exp)
            act_(gk[:, 0, :, :], gk[:, 0, :, :], ACT.Exp).then_inc(S["exp_ready"], 1)
            for c, (c0, c1) in enumerate(COLS):
                act.wait_ge(S["G_T"], c + 1)
                act_(GT[:, c0:c1], ps[0:NEXP, c, 0:c1 - c0], ACT.Copy).then_inc(S["GT_ready"], 1)
            with act.Fori(0, NEXP // 2) as it:
                for j in range(2):
                    act.wait_ge(S["l1_mm"], it * 2 + (j + 1))
                    act.wait_ge(S["l2_mm"], it * 2 + (j + 1))
                    for f in range(F // P):
                        last = act_(hT[:, j, f, :], ps[:, 2 + j, f * P:f * P + CAP], ACT.Gelu_apprx_tanh,
                                    bias=b1T[:, bass.ds(it * 4 + (2 * j + f), 1)])
                    last.then_inc(S["gelu_done"], 1)

        @block.vector
        def _(dve):
            V_ = nc.vector
            link = Link(dve, S["dve_link"])
            V_.memset(mv[:, :, :], 1.0)
            V_.memset(er_f, -1.0)
            V_.memset(ef[:, :, 0:PADC], -1.0)
            V_.memset(onesf[:, :], 1.0)
            link(V_.memset(halfblk[:, :], 0.0))
            V_.memset(halfblk[0:64, 0:1], 0.5)
            V_.memset(halfblk[64:128, 1:2], 0.5)
            V_.memset(projblk, 0.0)
            dve.wait_ge(S["edges_in"], 96)
            V_.tensor_copy(er_f[:, :, 0:2, :], er_i[:, :, 0:2, :])
            V_.tensor_copy(er_f[0:ROWS - 2 * P, :, 2, :], er_i[0:ROWS - 2 * P, :, 2, :])
            V_.tensor_copy(er_f[0:1, :, 3, 0:LEFT], er_i[0:1, :, 3, 0:LEFT]).then_inc(S["raw_ready"], 1)

            def layer_norm_stats(rows, n):
                for t in range(NT):
                    last = V_.bn_stats(st[0:sz(t), t, :], rows[0:sz(t), t, :])
                link(last)
                for t in range(NT):
                    last = V_.bn_aggr(mv[0:sz(t), t, :], st[0:sz(t), t, :])
                link(last)
                V_.tensor_scalar(rs[:, :], mv[:, :, 1], EPS, None, ALU.add).then_inc(S["var_ready"], 1)
                dve.wait_ge(S["sd_ready"], n)
                link(V_.reciprocal(rs[:, :], rs[:, :]))

            def batch_norm_affine(first, g0, b0):
                for k in range(KD):
                    for i, (c0, c1) in enumerate(BN):
                        last = V_.bn_stats(bst[:, k, i, :], tA[:, k, c0:c1])
                link(last)
                for k in range(KD):
                    last = V_.bn_aggr(bmv[:, k, :], bst[:, k, :, :].rearrange("p a b -> p (a b)"))
                link(last)
                V_.tensor_scalar(ab[:, 0, :], bmv[:, :, 1], EPS, None, ALU.add).then_inc(S["bvar_ready"], 1)
                dve.wait_ge(S["bsd_ready"], first)
                link(V_.reciprocal(ab[:, 0, :], ab[:, 0, :]))
                link(V_.tensor_tensor(ab[:, 1, :], ab[:, 0, :], par[:, g0:g0 + KD], ALU.mult))
                link(V_.tensor_tensor(ab[:, 2, :], bmv[:, :, 0], ab[:, 1, :], ALU.mult))
                link(V_.tensor_tensor(ab[:, 2, :], par[:, b0:b0 + KD], ab[:, 2, :], ALU.subtract))

            dve.wait_ge(S["x_in"], 32)
            layer_norm_stats(xr, 1)
            for t in range(NT):
                V_.tensor_scalar(r2[0:sz(t), t, :], xr[0:sz(t), t, :], mv[0:sz(t), t, 0:1], rs[0:sz(t), t:t + 1],
                                 ALU.subtract, ALU.mult).then_inc(S["h_ready"], 1)
            dve.wait_ge(S["raw_T"], 1)
            link(V_.tensor_copy(ef[:, :, PADC:PADC + 384], ps[:, 0:2, 0:384]))
            V_.tensor_copy(ef[:, :, PADC + ROWS:PADC + ROWS + 1], ps[:, 0:2, 384:385]).then_inc(S["ef_ready"], 1)
            dve.wait_ge(S["par_T"], 1)
            V_.tensor_copy(par[:, :], ps[:, 4, 0:28])
            V_.tensor_copy(b1T[:, :], ps[:, 4, 128:256])
            V_.tensor_copy(projblk[0:64, 0, :], ps[0:64, 5, 0:M])
            link(V_.tensor_copy(projblk[64:128, 1, :], ps[64:128, 5, 0:M]))
            V_.memset(tot[:, :], 0.0).then_inc(S["par_ready"], 1)
            dve.wait_ge(S["hT_ready"], NT)
            batch_norm_affine(1, 0, KD)
            for k in range(KD):
                V_.tensor_scalar(tB[:, k * N:(k + 1) * N], tA[:, k, :], ab[:, 1, k:k + 1], ab[:, 2, k:k + 1],
                                 ALU.mult, ALU.add).then_inc(S["xnT_ready"], 1)
            V_.memset(vaug[:, :, :, DH:DH + 1], 1.0)
            for nt in range(NQ):
                dve.wait_ge(S["v_mm"], nt + 1)
                V_.tensor_copy(vaug[:, nt, :, 0:DH], ps[:, 2 + nt, :].rearrange("p (h d) -> p h d", h=HEADS)).then_inc(S["v_ready"], 1)
            dve.wait_ge(S["dg_mm"], 1)
            link(V_.tensor_copy(dg, ps[:, 4, 0:2 * NQ * HEADS].rearrange("p (s n h) -> p s n h", s=2, n=NQ)))
            for u in range(NQ * PAIRS):
                nt, p = divmod(u, PAIRS)
                dve.wait_ge(S["uk_copied"], u + 1)
                V_.tensor_reduce(mk[:, nt, 2 * p:2 * p + 2], kf[:, nt, 2 * p:2 * p + 2, :], AXX, ALU.max).then_inc(S["uk_maxed"], 1)
            dve.wait_ge(S["uk_maxed"], NQ * PAIRS)
            V_.tensor_tensor(mk8, mk[:, 0, :], mk[:, 1, :], ALU.max).then_inc(S["mk_ready"], 1)
            for u in range(NQ * PAIRS):
                nt, p = divmod(u, PAIRS)
                dve.wait_ge(S["u_mm"], NQ * PAIRS + u + 1)
                link(V_.tensor_reduce(bq[:, nt, 2 * p:2 * p + 2], ps[:, 5 + (u + 8) % 3, :].rearrange("p (h m) -> p h m", h=2),
                                      AXX, ALU.max))
                V_.scalar_tensor_tensor(bq[:, nt, 2 * p:2 * p + 2], bq[:, nt, 2 * p:2 * p + 2], -1.0, dg[:, 0, nt, 2 * p:2 * p + 2],
                                        ALU.mult, ALU.subtract).then_inc(S["uq_bias"], 1)
            dve.wait_ge(S["gmk_ready"], 1)
            for nt in range(NQ):
                last = V_.scalar_tensor_tensor(bk[:, nt, :], gmk, -1.0, dg[:, 1, nt, :], ALU.mult, ALU.subtract)
            last.then_inc(S["bk_ready"], 1)
            dve.wait_ge(S["uq_exp"], NQ * HEADS)
            V_.tensor_scalar(qf, qf, 1.0 / float(np.sqrt(M)), KEPS, ALU.mult, ALU.add).then_inc(S["qf_ready"], 1)
            dve.wait_ge(S["kexp_done"], NQ * HEADS)
            V_.tensor_scalar(kf, kf, 1.0 / float(np.sqrt(M)), KEPS, ALU.mult, ALU.add).then_inc(S["kf_ready"], 1)
            for b in range(4):
                dve.wait_ge(S["kv_mm"], b + 1)
                V_.tensor_copy(kv[:, 2 * b:2 * b + 2, :, :], ps[:, b, :].rearrange("p (h m c) -> p h m c", h=2, m=2)[:, :, :, 0:DH + 1])\
                  .then_inc(S["kv_ready"], 1)
            for h in range(HEADS):
                dve.wait_ge(S["ga_mm"], h + 1)
                o = ps[:, 6 + h % 2, 0:256].rearrange("p (n c) -> p n c", n=NQ)
                link(V_.tensor_scalar(zr[:, h % 2, :], o[:, :, DH], KEPS, None, ALU.add))
                link(V_.reciprocal(zr[:, h % 2, :], zr[:, h % 2, :]))
                for nt in range(NQ):
                    last = V_.tensor_scalar(attnrow[:, nt, h * DH:(h + 1) * DH], o[:, nt, 0:DH], zr[:, h % 2, nt:nt + 1],
                                            None, ALU.mult)
                last.then_inc(S["ga_ready"], 1)

            with dve.Fori(0, NT // 2) as tp:
                for tt in range(2):
                    for i in range(WIN):
                        s = tt * WIN + i
                        col = tp * (2 * STEP) + (tt * STEP + i)
                        dve.wait_ge(S["oh_used"], tp * (2 * WIN) + (s + 1))
                        V_.tensor_scalar(ohs[:, i % NB, 0:N], iota16[:, 0:N], ef[:, 0, bass.ds(col, 1)], None, ALU.is_equal)
                        V_.tensor_scalar(ohd[:, i % NB, :], iota16[:, bass.ds(tp * (2 * P) + tt * P, P)],
                                         ef[:, 1, bass.ds(col, 1)], None, ALU.is_equal).then_inc(S["oh_ready"], 1)
            dve.wait_ge(S["cnt_ready"], NT + 2)
            V_.tensor_reduce(tot[:, 0:1], deg[:, :], AXX, ALU.add).then_inc(S["tot_ready"], 1)
            dve.wait_ge(S["tot_mm"], 1)
            V_.tensor_copy(flag[0:1, 0:1], ps[0:1, 7, 0:1]).then_inc(S["flag_ready"], 1)
            dve.wait_ge(S["flag_ready"], 1)
            total = dve.value_load(flag[0:1, 0:1], min_val=0, max_val=E)
            with dve.If(total < E):
                with dve.Fori(0, NT) as t:
                    with dve.Fori(0, FULL // NB) as g:
                        for j in range(NB):
                            dve.wait_ge(S["gcnt_oh_used"], t * FULL + g * NB + (j + 1))
                            V_.tensor_scalar(ohs[:, j, 0:N], iota16[:, 0:N], ef[:, 0, bass.ds(g * NB + (PADC + j), 1)], None, ALU.is_equal)
                            V_.tensor_scalar(ohd[:, j, :], iota16[:, bass.ds(t * P, P)],
                                             ef[:, 1, bass.ds(g * NB + (PADC + j), 1)], None, ALU.is_equal).then_inc(S["gcnt_oh_ready"], 1)
                dve.wait_ge(S["gcnt_ready"], NT + 2)
            link(V_.tensor_scalar(rdeg[:, :], deg[:, :], 1.0, None, ALU.max))
            link(V_.reciprocal(rdeg[:, :], rdeg[:, :]))
            for t in range(NT):
                V_.tensor_scalar(A[:, t, :], A[:, t, :], rdeg[:, t:t + 1], None, ALU.mult).then_inc(S["An_ready"], 1)
            for c, (c0, c1) in enumerate(COLS):
                cn = c1 - c0
                for kt in range(0, NT, 2):
                    dve.wait_ge(S["AT_mm"], c * NT + kt + 1)
                    V_.tensor_copy(AT[0:sz(kt), c % 2, kt, 0:cn], ps[0:sz(kt), kt % 2, 0:cn]).then_inc(S["AT_dve"], 1)
                for k in range(KD):
                    dve.wait_ge(S["agg_mm"], c * KD + k + 1)
                    if c >= 1 and k == 0:
                        dve.wait_ge(S["conv_mm"], c * KD)
                    V_.tensor_copy(aggT[:, k, 0:cn], ps[:, 2 + k, 0:cn]).then_inc(S["agg_ready"], 1)
                for fo in range(KD):
                    n = c * KD + fo
                    dve.wait_ge(S["rl_ready"], n + 1)
                    a0 = SEQ if c == 0 else 0
                    if c == 0:
                        dve.wait_ge(S["hatt_ready"], 2)
                        link(V_.tensor_tensor(rl[:, n % 2, 0:SEQ], rl[:, n % 2, 0:SEQ], hatt[:, fo, :], ALU.add))
                        V_.tensor_tensor(tA[:, fo, 0:SEQ], rl[:, n % 2, 0:SEQ], tA[:, fo, 0:SEQ], ALU.add)
                    V_.scalar_tensor_tensor(tA[:, fo, c0 + a0:c1], rl[:, n % 2, a0:cn], hatt[:, fo, SEQ - 1:SEQ],
                                            tA[:, fo, c0 + a0:c1], ALU.add, ALU.add).then_inc(S["z_ready"], 1)
            dve.wait_ge(S["z_ready"], 3 * KD)
            batch_norm_affine(2, 2 * KD, 3 * KD)
            for k in range(KD):
                V_.tensor_scalar(tA[:, k, :], tA[:, k, :], ab[:, 1, k:k + 1], ab[:, 2, k:k + 1],
                                 ALU.mult, ALU.add).then_inc(S["w_ready"], 1)
            for t in range(NT):
                dve.wait_ge(S["w_T"], t + 1)
                last = V_.tensor_tensor(xr[0:sz(t), t, :], xr[0:sz(t), t, :], ps[0:sz(t), t % 2, :], ALU.add)
                last.then_inc(S["x1_ready"], 1)
            dve.wait_ge(S["x1_ready"], NT)
            layer_norm_stats(xr, 2)
            for t in range(NT):
                last = V_.tensor_scalar(r2[0:sz(t), t, :], xr[0:sz(t), t, :], mv[0:sz(t), t, 0:1], rs[0:sz(t), t:t + 1],
                                        ALU.subtract, ALU.mult)
            link(last)
            layer_norm_stats(r2, 3)
            for t in range(NT):
                V_.tensor_scalar(nrow[0:sz(t), t, :], r2[0:sz(t), t, :], mv[0:sz(t), t, 0:1], rs[0:sz(t), t:t + 1],
                                 ALU.subtract, ALU.mult).then_inc(S["n1_ready"], 1)
            dve.wait_ge(S["n1T_raw"], NT)
            for k in range(KD):
                V_.tensor_scalar(tA[:, k, :], tA[:, k, :], par[:, 5 * KD + k:5 * KD + k + 1], par[:, 6 * KD + k:6 * KD + k + 1],
                                 ALU.mult, ALU.add).then_inc(S["x1T_ready"], 1)

            with dve.Fori(0, PAIRS) as pr:
                dve.wait_ge(S["proj_done"], pr + 2)
                V_.tensor_copy(KT, psf[:, 1536:1536 + N]).then_inc(S["qkv_dve"], 1)
                V_.tensor_copy(V[:, 4:8, :], ps[:, 7, :].rearrange("p (t c) -> p t c", t=4)).then_inc(S["qkv_dve"], 1)

                def neg_max(i):
                    qt = sz(i // 2)
                    dve.wait_ge(S["s_mm"], pr * U + (i + 1))
                    if i >= 2:
                        dve.wait_ge(S["exp_done"], pr * U + (i - 1))
                    V_.tensor_reduce(nmx[0:qt, i % 2:i % 2 + 1], psf[0:qt, 1536 * (i % 2):1536 * (i % 2) + N], AXX, ALU.max,
                                     negate=True).then_inc(S["negmax"], 1)

                def last_bank(i):
                    dve.wait_ge(S["p_T"], pr * PTS + (3 * i + 3 if i < U else 2 * U + i + 1))
                    bank = 6 + (3 * i + 2 if i < U else 2 * U + i) % 2
                    last = None
                    if i < U:
                        qt = sz(i // 2)
                        V_.tensor_copy(PT[:, i % 2, 8, 0:qt], ps[:, bank, 0:qt])
                        last = V_.tensor_copy(PT[0:TAIL, i % 2, 9, 0:qt], ps[0:TAIL, bank, P:P + qt])
                    if 1 <= i <= U:
                        n = i - 1
                        qt = sz(n // 2)
                        dve.wait_ge(S["loop_link"], pr * U + i)
                        last = V_.tensor_scalar(arow[0:qt, (n // 2) % 2, (n % 2) * DH:(n % 2 + 1) * DH],
                                                ps[0:qt, bank, 256:256 + DH], resum[0:qt, n % 4:n % 4 + 1], None, ALU.mult)
                    if i >= 3 and i % 2:
                        t = (i - 3) // 2
                        last = V_.tensor_copy(attnT[:, bass.ds(pr, 1), t * P:t * P + sz(t)].rearrange("p a n -> p (a n)"),
                                              ps[:, bank, 320:320 + sz(t)])
                    last.then_inc(S["pt_dve"], 1)

                neg_max(0)
                neg_max(1)
                for i in range(U + 3):
                    if i >= 1:
                        last_bank(i - 1)
                    if i < U:
                        qt = sz(i // 2)
                        dve.wait_ge(S["p_T"], pr * PTS + (3 * i + 1))
                        V_.tensor_copy(PT[:, i % 2, 0:4, 0:qt],
                                       ps[:, 6 + i % 2, :].rearrange("p (t c) -> p t c", t=4)[:, :, 0:qt]).then_inc(S["pt_dve"], 1)
                        dve.wait_ge(S["exp_done"], pr * U + (i + 1))
                        V_.reciprocal(resum[0:qt, i % 4:i % 4 + 1], esum[0:qt, i % 2:i % 2 + 1]).then_inc(S["loop_link"], 1)
                    if i + 2 < U:
                        neg_max(i + 2)

            for t in range(NT):
                dve.wait_ge(S["wo_mm"], t + 1)
                last = V_.tensor_tensor(r2[0:sz(t), t, :], r2[0:sz(t), t, :], ps[0:sz(t), t % 2, :], ALU.add)
                last.then_inc(S["xx_ready"], 1)
            dve.wait_ge(S["xx_ready"], NT)
            layer_norm_stats(r2, 4)
            dve.wait_ge(S["ln2_in"], 32)
            for t in range(NT):
                n = nrow[0:sz(t), t, :]
                link(V_.tensor_scalar(n, r2[0:sz(t), t, :], mv[0:sz(t), t, 0:1], rs[0:sz(t), t:t + 1],
                                      ALU.subtract, ALU.mult))
                link(V_.tensor_tensor(n, n, g2row[0:sz(t), 0, :], ALU.mult))
                V_.tensor_tensor(n, n, g2row[0:sz(t), 1, :], ALU.add).then_inc(S["x2_ready"], 1)
            dve.wait_ge(S["lg_mm"], NT)
            link(V_.memset(lg[:, NT - 1, :], 0.0))
            V_.tensor_copy(lg[:, 0:8, :], ps[:, 4, :].rearrange("p (t e) -> p t e", t=8))
            V_.tensor_copy(lg[:, 8, :], ps[:, 5, 0:NEXP])
            link(V_.tensor_copy(lg[0:TAIL, 9, :], ps[0:TAIL, 5, NEXP:2 * NEXP]))
            for t in range(NT):
                last = V_.max(v8[:, t, :], lg[:, t, :])
            link(last)
            for t in range(NT):
                V_.max_index(i8[:, t, :], v8[:, t, :], lg[:, t, :])
                last = V_.tensor_scalar(ex[:, t, :], lg[:, t, :], v8[:, t, 0:1], None, ALU.subtract)
                last = V_.tensor_scalar(gk[:, 0, t, :], v8[:, t, 0:2], v8[:, t, 0:1], None, ALU.subtract)
            last.then_inc(S["exs_ready"], 1)
            dve.wait_ge(S["exs_ready"], 1)
            link(V_.tensor_copy(gk[:, 1, :, :], i8[:, :, 0:2]))
            for t in range(NT):
                for k in range(2):
                    last = V_.tensor_scalar(ohk[k][:, t, :], iota64[:, :], gk[:, 1, t, k:k + 1], None, ALU.is_equal)
            link(last)
            V_.tensor_tensor(O, ohk[0], ohk[1], ALU.add).then_inc(S["O_ready"], 1)
            dve.wait_ge(S["exp_ready"], 1)
            link(V_.tensor_reduce(ssum[:, :], ex, AXX, ALU.add))
            link(V_.reciprocal(ssum[:, :], ssum[:, :]))
            for k in range(2):
                last = V_.tensor_tensor(gk[:, 2, :, k], gk[:, 0, :, k], ssum[:, :], ALU.mult)
            link(last)
            link(V_.tensor_tensor(gk[:, 3, :, 0], gk[:, 2, :, 0], gk[:, 2, :, 1], ALU.add))
            link(V_.reciprocal(gk[:, 3, :, 0], gk[:, 3, :, 0]))
            for k in range(2):
                last = V_.tensor_tensor(gk[:, 4, :, k], gk[:, 2, :, k], gk[:, 3, :, 0], ALU.mult)
            link(last)
            dve.wait_ge(S["pos_mm"], 1)
            V_.tensor_copy(posm[:, 0:8, :], ps[:, 6, :].rearrange("p (t e) -> p t e", t=8))
            V_.tensor_copy(posm[:, 8, :], ps[:, 7, 0:NEXP])
            link(V_.tensor_copy(posm[:, 9, :], ps[:, 7, NEXP:2 * NEXP]))
            for k in range(2):
                link(V_.tensor_tensor(tmp, posm, ohk[k], ALU.mult))
                link(V_.tensor_reduce(gk[:, 5, :, k], tmp, AXX, ALU.add))
            link(V_.tensor_scalar(gk[:, 6, :, :], gk[:, 5, :, :], float(CAP), None, ALU.is_lt))
            link(V_.tensor_scalar(gk[:, 5, :, :], gk[:, 5, :, :], float(CAP - 1), None, ALU.min))
            link(V_.scalar_tensor_tensor(gk[:, 5, :, :], gk[:, 1, :, :], float(CAP), gk[:, 5, :, :], ALU.mult, ALU.add))
            link(V_.tensor_copy(slot_i[:, :, :], gk[:, 5, :, :]))
            link(V_.tensor_scalar(gk[:, 7, :, :], gk[:, 6, :, :], -65536.0, 65536.0, ALU.mult, ALU.add))
            link(V_.tensor_tensor(gk[:, 7, :, :], gk[:, 7, :, :], gk[:, 5, :, :], ALU.add))
            V_.tensor_copy(sidx_i[:, :, :], gk[:, 7, :, :]).then_inc(S["idx_ready"], 1)
            link(V_.tensor_tensor(gk[:, 4, :, :], gk[:, 4, :, :], gk[:, 6, :, :], ALU.mult))
            for t in range(NT):
                last = V_.tensor_scalar(tmp[:, t, :], ohk[0][:, t, :], gk[:, 4, t, 0:1], None, ALU.mult)
            link(last)
            for t in range(NT):
                last = V_.scalar_tensor_tensor(G[:, t, :], ohk[1][:, t, :], gk[:, 4, t, 1:2], tmp[:, t, :], ALU.mult, ALU.add)
            last.then_inc(S["G_ready"], 1)
            dve.wait_ge(S["tab_in"], 16)
            V_.tensor_copy(tabf[:, :], tabr[:, :]).then_inc(S["tabf_ready"], 1)
            dve.wait_ge(S["tab_T"], 1)
            V_.tensor_copy(tabT[:, :], ps[0:CAP, 3, 0:NEXP]).then_inc(S["tabT_ready"], 1)

            def xT_copy(j, n):
                dve.wait_ge(S["xT_mm"], n)
                V_.tensor_copy(xT[:, j, :, :], ps[:, j, :].rearrange("p (k c) -> p k c", k=KD)[:, :, 0:CAP]).then_inc(S["xT_ready"], 1)

            def y_copy(j, n, stored):
                dve.wait_ge(S["l2_mm"], n + 2)
                dve.wait_ge(y_stored[j], stored)
                V_.tensor_copy(ys[0:CAP, j, :], ps[0:CAP, 4 + j, :]).then_inc(S["y_ready"], 1)

            xT_copy(0, 1)
            xT_copy(1, 2)
            with dve.Fori(0, NEXP // 2 - 1) as it:
                for j in range(2):
                    xT_copy(j, it * 2 + (j + 3))
                    y_copy(j, it * 2 + (j + 1), it * 16 + 16)
            for j in range(2):
                y_copy(j, NEXP - 1 + j, 16 * (NEXP // 2))
            for t in range(NT):
                last = V_.tensor_tensor(xr[0:sz(t), t, :], xr[0:sz(t), t, :], r2[0:sz(t), t, :], ALU.add)
            link(last)
            for t in range(NT):
                dve.wait_ge(S["b2_mm"], t + 1)
                xo = xr[0:sz(t), t, :]
                link(V_.tensor_tensor(xo, xo, ps[0:sz(t), 6 + t % 2, :], ALU.add))
                for k in range(2):
                    n = t * 2 + k
                    dve.wait_ge(yg_in[n % 4], 16 * (n // 4 + 1))
                    last = V_.scalar_tensor_tensor(xo, ygat[0:sz(t), n % 4, :], gk[0:sz(t), 4, t, k:k + 1], xo, ALU.mult, ALU.add)
                    if k == 0:
                        link(last)
                last.then_inc(S["acc_ready"], 1)

        @block.tensor
        def _(pe):
            mm, tr = nc.tensor.matmul, nc.tensor.transpose
            pe.sem_inc(S["oh_used"], NB)
            pe.sem_inc(S["proj_done"], 1)
            pe.sem_inc(S["pt_dve"], 1)
            pe.sem_inc(S["cnt_ready"], 2)
            pe.sem_inc(S["gcnt_ready"], 2)
            pe.sem_inc(S["gcnt_oh_used"], NB)
            pe.sem_inc(S["l2_mm"], 2)
            pe.sem_inc(S["y_ready"], 2)
            pe.sem_inc(y_stored[0], 16)
            pe.sem_inc(y_stored[1], 16)
            pe.wait_ge(S["consts"], 2)
            pe.wait_ge(S["raw_ready"], 1)
            for s in range(2):
                for b in range(3):
                    tr(ps[:, s, b * P:(b + 1) * P], er_f[:, s, b, :], identf[:, :])
                last = tr(ps[:, s, 384:385], er_f[0:1, s, 3, :], identf[0:1, 0:1])
            last.then_inc(S["raw_T"], 1)
            pe.wait_ge(S["params_in"], 160)
            tr(ps[:, 4, 0:28], prow[:, :], identf[0:28, 0:28])
            tr(ps[:, 4, 128:256], b1r[:, :], identf[:, :])
            for t in range(2):
                last = tr(ps[:, 5, t * P:(t + 1) * P], pj[:, t, :, :].rearrange("p a d -> p (a d)"), identf[:, :])
            last.then_inc(S["par_T"], 1)

            def rows_to_T(rows, ready, done, freed, bank):
                for t in range(NT):
                    pe.wait_ge(S[ready], t + 1)
                    if t >= 2:
                        pe.wait_ge(S[freed], t - 1)
                    for k in range(KD):
                        last = tr(ps[:, bank + t % 2, k * P:k * P + sz(t)], rows[0:sz(t), t, k * P:(k + 1) * P],
                                  identf[0:sz(t), 0:sz(t)])
                    last.then_inc(S[done], 1)

            def T_to_rows(cols, done, freed, bank):
                for t in range(NT):
                    if t >= 2:
                        pe.wait_ge(S[freed], t - 1)
                    for k in range(KD):
                        last = tr(ps[0:sz(t), bank + t % 2, k * P:(k + 1) * P], cols(k, t), identf[:, :])
                    last.then_inc(S[done], 1)

            rows_to_T(r2, "h_ready", "h_T", "hT_ready", 2)
            pe.wait_ge(S["xnT_ready"], KD)
            pe.wait_ge(S["hT_ready"], NT)
            T_to_rows(lambda k, t: tB[:, k * N + t * P:k * N + t * P + sz(t)], "xn_T", "xn_ready", 2)

            pe.wait_ge(S["ef_ready"], 1)
            pe.wait_ge(S["par_ready"], 1)
            pe.wait_ge(S["gw_in"], 64)
            pe.wait_ge(S["xn_ready"], NT)
            for p in range(PAIRS):
                if p >= 2:
                    pe.wait_ge(S["qk_ready"], p - 1)
                for s in range(2):
                    for k in range(KD):
                        last = mm(ps[:, p % 2, s * SEQ:(s + 1) * SEQ], gw[s][:, k, p * P:(p + 1) * P], tA[:, k, 0:SEQ],
                                  start=(k == 0), stop=(k == KD - 1))
                last.then_inc(S["qk_mm"], 1)
            for nt in range(NQ):
                for k in range(KD):
                    last = mm(ps[:, 2 + nt, :], tA[:, k, nt * P:(nt + 1) * P], gw[2][:, k, :], start=(k == 0), stop=(k == KD - 1))
                last.then_inc(S["v_mm"], 1)
            pe.wait_ge(S["sq_ready"], 1)
            for s in range(2):
                for nt in range(NQ):
                    for p in range(PAIRS):
                        c = (s * NQ + nt) * HEADS + 2 * p
                        last = mm(ps[:, 4, c:c + 2], sq[:, s, p, nt * P:(nt + 1) * P], halfblk[:, :], start=True, stop=True)
            last.then_inc(S["dg_mm"], 1)
            for u in range(2 * NQ * PAIRS):
                s, r = divmod(u, NQ * PAIRS)
                nt, p = divmod(r, PAIRS)
                if u >= 3:
                    v = u - 3
                    if v < NQ * PAIRS:
                        pe.wait_ge(S["uk_copied"], v + 1)
                    else:
                        pe.wait_ge(S["uq_exp"], 2 * (v - NQ * PAIRS + 1))
                mm(ps[:, 5 + u % 3, :], qk[:, 1 - s, p, nt * P:(nt + 1) * P], projblk.rearrange("p a m -> p (a m)"),
                   start=True, stop=True).then_inc(S["u_mm"], 1)
            pe.wait_ge(S["v_ready"], NQ)
            pe.wait_ge(S["kf_ready"], 1)
            for h in range(HEADS):
                for m in range(M // P):
                    c = ((h % 2) * 2 + m) * P
                    for nt in range(NQ):
                        last = mm(ps[:, h // 2, c:c + DH + 1], kf[:, nt, h, m * P:(m + 1) * P], vaug[:, nt, h, :],
                                  start=(nt == 0), stop=(nt == NQ - 1))
                if h % 2:
                    last.then_inc(S["kv_mm"], 1)
            pe.wait_ge(S["qf_ready"], 1)

            def q_features_T(h):
                if h >= 2:
                    pe.wait_ge(S["qfT_ready"], h - 1)
                for m in range(M // P):
                    for nt in range(NQ):
                        last = tr(ps[:, 4 + h % 2, m * SEQ + nt * P:m * SEQ + (nt + 1) * P], qf[:, nt, h, m * P:(m + 1) * P],
                                  identf[:, :])
                last.then_inc(S["qfT_mm"], 1)

            pe.wait_ge(S["uq_exp"], 2 * NQ * PAIRS)
            q_features_T(0)
            for h in range(HEADS):
                if h + 1 < HEADS:
                    q_features_T(h + 1)
                pe.wait_ge(S["qfT_ready"], h + 1)
                pe.wait_ge(S["kv_ready"], h // 2 + 1)
                if h >= 2:
                    pe.wait_ge(S["ga_ready"], h - 1)
                for nt in range(NQ):
                    for m in range(M // P):
                        last = mm(ps[:, 6 + h % 2, nt * P:nt * P + DH + 1], qfT[:, h % 2, m, nt * P:(nt + 1) * P], kv[:, h, m, :],
                                  start=(m == 0), stop=(m == M // P - 1))
                last.then_inc(S["ga_mm"], 1)
            pe.wait_ge(S["kv_ready"], 4)
            pe.wait_ge(S["ga_ready"], HEADS)
            for k in range(KD):
                for nt in range(NQ):
                    last = tr(ps[:, k // 2, (k % 2) * SEQ + nt * P:(k % 2) * SEQ + (nt + 1) * P], attnrow[:, nt, k * P:(k + 1) * P],
                              identf[:, :])
                if k % 2:
                    last.then_inc(S["ga_T"], 1)
            pe.wait_ge(S["gaT_ready"], 2)
            for fo in range(KD):
                for k in range(KD):
                    last = mm(ps[:, 2 + fo // 2, (fo % 2) * SEQ:(fo % 2 + 1) * SEQ], gw[3][:, k, fo * P:(fo + 1) * P],
                              attnTg[:, k, :], start=(k == 0), stop=(k == KD - 1))
                if fo % 2:
                    last.then_inc(S["ho_mm"], 1)
            pe.wait_ge(S["hatt_ready"], 2)

            def count_chunk(b, i, first, last_chunk, used):
                for c0, c1 in COLS:
                    last = mm(ps[:, b + c0 // 512, 0:c1 - c0], ohd[:, i, :], ohs[:, i, c0:c1], start=first, stop=last_chunk)
                last.then_inc(S[used], 1)
                return last

            with pe.Fori(0, NT // 2) as tp:
                for tt in range(2):
                    pe.wait_ge(S["cnt_ready"], tp * 2 + (tt + 1))
                    for i in range(WIN):
                        pe.wait_ge(S["oh_ready"], tp * (2 * WIN) + (tt * WIN + i + 1))
                        count_chunk(3 * tt, i % NB, i == 0, i == WIN - 1, "oh_used")
            pe.wait_ge(S["tot_ready"], 1)
            mm(ps[0:1, 7, 0:1], onesf[:, :], tot[:, 0:1], start=True, stop=True).then_inc(S["tot_mm"], 1)
            pe.wait_ge(S["flag_ready"], 1)
            total = pe.value_load(flag[0:1, 0:1], min_val=0, max_val=E)
            with pe.If(total < E):
                with pe.Fori(0, NT // 2) as tp:
                    for tt in range(2):
                        pe.wait_ge(S["gcnt_ready"], tp * 2 + (tt + 1))

                        def group(done, first=False, final=False):
                            for j in range(NB):
                                pe.wait_ge(S["gcnt_oh_ready"], done + (j + 1))
                                count_chunk(3 * tt, j, first and j == 0, final and j == NB - 1, "gcnt_oh_used")

                        start = tp * (2 * FULL) + tt * FULL
                        group(start, first=True)
                        with pe.Fori(1, FULL // NB - 1) as g:
                            group(start + g * NB)
                        group(start + (FULL - NB), final=True)

            pe.wait_ge(S["An_ready"], NT)
            pe.wait_ge(S["wc_in"], 16)
            for c, (c0, c1) in enumerate(COLS):
                cn = c1 - c0
                tiles = range(4 * c, min(4 * c + 4, NT))
                for kt in range(NT):
                    n = c * NT + kt
                    if n >= 2:
                        pe.wait_ge(S["AT_dve"] if kt % 2 == 0 else S["AT_act"], (n - 2) // 2 + 1)
                    for t in tiles:
                        last = tr(ps[0:sz(kt), kt % 2, (t - 4 * c) * P:(t - 4 * c) * P + sz(t)],
                                  A[0:sz(t), t, kt * P:kt * P + sz(kt)], identf[0:sz(t), 0:sz(t)])
                    last.then_inc(S["AT_mm"], 1)
                pe.wait_ge(S["AT_dve"], (c + 1) * NT // 2)
                pe.wait_ge(S["AT_act"], (c + 1) * NT // 2)
                for k in range(KD):
                    if c >= 1:
                        pe.wait_ge(S["agg_ready"], (c - 1) * KD + k + 1)
                    for kt in range(NT):
                        last = mm(ps[:, 2 + k, 0:cn], r2[0:sz(kt), kt, k * P:(k + 1) * P], AT[0:sz(kt), c % 2, kt, 0:cn],
                                  start=(kt == 0), stop=(kt == NT - 1))
                    last.then_inc(S["agg_mm"], 1)
                pe.wait_ge(S["agg_ready"], (c + 1) * KD)
                for fo in range(KD):
                    n = c * KD + fo
                    if n >= 2:
                        pe.wait_ge(S["rl_ready"], n - 1)
                    for k in range(KD):
                        last = mm(ps[:, 6 + n % 2, 0:cn], wc[:, k, fo * P:(fo + 1) * P], aggT[:, k, 0:cn],
                                  start=(k == 0), stop=(k == KD - 1))
                    last.then_inc(S["conv_mm"], 1)
            pe.wait_ge(S["w_ready"], KD)
            T_to_rows(lambda k, t: tA[:, k, t * P:t * P + sz(t)], "w_T", "x1_ready", 0)
            rows_to_T(nrow, "n1_ready", "n1_T", "n1T_raw", 2)
            pe.wait_ge(S["x1T_ready"], KD)
            pe.wait_ge(S["rl_ready"], 3 * KD)

            pe.wait_ge(S["qpad_ready"], 1)
            with pe.Fori(0, PAIRS) as pr:
                pe.wait_ge(S["wst_in"], pr * 48 + 48)
                pe.wait_ge(S["pt_dve"], pr * (2 * U + 2) + 1)
                for i, b0 in ((0, 0), (1, 3)):
                    for c, (c0, c1) in enumerate(COLS):
                        for k in range(KD):
                            mm(ps[:, b0 + c, 0:c1 - c0], wst[:, i, k, :], tA[:, k, c0:c1], start=(k == 0), stop=(k == KD - 1))
                for t in range(NT):
                    bank, col = (6 + t // 4, (t % 4) * P) if t < 8 else (2, 256 + (t - 8) * P)
                    for k in range(KD):
                        last = mm(ps[0:sz(t), bank, col:col + P], tA[:, k, t * P:t * P + sz(t)], wst[:, 2, k, :],
                                  start=(k == 0), stop=(k == KD - 1))
                last.then_inc(S["proj_done"], 1)
                pe.wait_ge(S["qkv_act"], pr * 5 + 5)
                pe.wait_ge(S["qkv_dve"], pr * 2 + 2)

                def scores(i):
                    t, h = divmod(i, 2)
                    if i >= 2:
                        pe.wait_ge(S["exp_done"], pr * U + (i - 1))
                    for c, (c0, c1) in enumerate(COLS):
                        last = mm(ps[0:sz(t), 3 * (i % 2) + c, 0:c1 - c0], QT[:, h, t * P:t * P + sz(t)], KT[:, c0:c1], start=True, stop=True)
                    last.then_inc(S["s_mm"], 1)

                def bank_free(n):
                    n -= 2
                    if n >= 0:
                        m, r = divmod(n, 3)
                        if n >= 3 * U:
                            pe.wait_ge(S["pt_dve"], pr * (2 * U + 2) + (2 * U + 2 + n - 3 * U))
                        elif r == 1:
                            pe.wait_ge(S["pt_act"], pr * U + (m + 1))
                        else:
                            pe.wait_ge(S["pt_dve"], pr * (2 * U + 2) + (2 * m + r // 2 + 2))

                def weights_T(i, parts):
                    t = i // 2
                    if i < U:
                        pe.wait_ge(S["exp_done"], pr * U + (i + 1))
                    for g in parts:
                        n = 3 * i + g if i < U else 2 * U + i
                        bank_free(n)
                        if i < U:
                            for kt in range(4 * g, min(4 * g + 4, NT)):
                                last = tr(ps[0:sz(kt), 6 + n % 2, (kt % 4) * P:(kt % 4) * P + sz(t)],
                                          Pb[0:sz(t), i % 2, kt * P:kt * P + sz(kt)], identf[0:sz(t), 0:sz(t)])
                        if g == 2 and 1 <= i <= U:
                            m, h = divmod(i - 1, 2)
                            pe.wait_ge(S["pt_dve"], pr * (2 * U + 2) + (2 * i + 1))
                            pe.wait_ge(S["pt_act"], pr * U + i)
                            for kt in range(NT):
                                last = mm(ps[0:sz(m), 6 + n % 2, 256:256 + DH], PT[0:sz(kt), (i - 1) % 2, kt, 0:sz(m)],
                                          V[0:sz(kt), kt, h * DH:(h + 1) * DH], start=(kt == 0), stop=(kt == NT - 1))
                        if g == 2 and i >= 3 and i % 2:
                            r = (i - 3) // 2
                            pe.wait_ge(S["pt_dve"], pr * (2 * U + 2) + (2 * i + 1 if i <= U else 2 * U + 2))
                            last = tr(ps[:, 6 + n % 2, 320:320 + sz(r)], arow[0:sz(r), r % 2, :], identf[0:sz(r), 0:sz(r)])
                        last.then_inc(S["p_T"], 1)

                scores(0)
                scores(1)
                for i in range(U + 2):
                    if i < U:
                        weights_T(i, (0,))
                    if i + 2 < U:
                        scores(i + 2)
                    weights_T(i, (1, 2) if i < U else (2,))

            pe.wait_ge(S["wo_in"], 16)
            pe.wait_ge(S["pt_dve"], PAIRS * (2 * U + 2) + 1)
            for t in range(NT):
                if t >= 2:
                    pe.wait_ge(S["xx_ready"], t - 1)
                for k in range(KD):
                    last = mm(ps[0:sz(t), t % 2, :], attnT[:, k, t * P:t * P + sz(t)], wo_s[:, k, :],
                              start=(k == 0), stop=(k == KD - 1))
                last.then_inc(S["wo_mm"], 1)
            pe.wait_ge(S["route_in"], 32)
            for t in range(NT + 1):
                if t < NT:
                    pe.wait_ge(S["x2_ready"], t + 1)
                    if t >= 2:
                        pe.wait_ge(S["x2T_ready"], t - 1)
                    for k in range(KD):
                        last = tr(ps[:, 2 + t % 2, k * P:k * P + sz(t)], nrow[0:sz(t), t, k * P:(k + 1) * P],
                                  identf[0:sz(t), 0:sz(t)])
                    last.then_inc(S["x2_T"], 1)
                if t >= 1:
                    r = t - 1
                    pe.wait_ge(S["x2T_ready"], r + 1)
                    for k in range(KD):
                        last = mm(ps[0:sz(r), 4 + r // 8, (r % 8) * NEXP:(r % 8 + 1) * NEXP], x2T[:, r % 2, k, 0:sz(r)],
                                  wr_s[:, k, :], start=(k == 0), stop=(k == KD - 1))
                    last.then_inc(S["lg_mm"], 1)
            pe.wait_ge(S["O_ready"], 1)
            for t in range(NT):
                o = ps[:, 6 + t // 8, (t % 8) * NEXP:(t % 8 + 1) * NEXP]
                for r in range(t):
                    mm(o, onesb[:, :], O[:, r, :], start=(r == 0), stop=False)
                last = mm(o, tri[:, :], O[:, t, :], start=(t == 0), stop=True)
            last.then_inc(S["pos_mm"], 1)
            pe.wait_ge(S["G_ready"], 1)
            for t in range(NT):
                last = tr(ps[0:NEXP, t // 4, (t % 4) * P:(t % 4) * P + sz(t)], G[0:sz(t), t, :], identf[0:sz(t), 0:sz(t)])
                if t % 4 == 3 or t == NT - 1:
                    last.then_inc(S["G_T"], 1)
            pe.wait_ge(S["tabf_ready"], 1)
            tr(ps[0:CAP, 3, 0:NEXP], tabf[:, :], identf[0:NEXP, 0:NEXP]).then_inc(S["tab_T"], 1)
            pe.wait_ge(S["GT_ready"], 3)
            pe.wait_ge(S["tabT_ready"], 1)


            def gathered_T(j, arrived, jj):
                pe.wait_ge(xb_in[j], arrived)
                for k in range(KD):
                    last = tr(ps[:, jj, k * P:k * P + CAP], xb[0:CAP, j, k * P:(k + 1) * P], identf[0:CAP, 0:CAP])
                last.then_inc(S["xT_mm"], 1)

            def layer1(slot, arrived, n):
                pe.wait_ge(w_in[slot], arrived)
                pe.wait_ge(S["xT_ready"], n)
                for f in range(F // P):
                    for k in range(KD):
                        last = mm(ps[:, 2 + slot % 2, f * P:f * P + CAP], ring1[slot][:, k, f * P:(f + 1) * P], xT[:, slot % 2, k, :],
                                  start=(k == 0), stop=(k == KD - 1))
                last.then_inc(S["l1_mm"], 1)

            def layer2(slot, n):
                pe.wait_ge(S["gelu_done"], n)
                for f in range(F // P):
                    last = mm(ps[0:CAP, 4 + slot % 2, :], hT[:, slot % 2, f, :], ring2[slot][:, f, :],
                              start=(f == 0), stop=(f == F // P - 1))
                last.then_inc(S["l2_mm"], 1)

            gathered_T(0, 16, 0)
            layer1(0, 32, 1)
            gathered_T(1, 16, 1)
            with pe.Fori(0, NEXP // RW - 1) as it:
                for j in range(RW):
                    layer1((j + 1) % RW, it * 32 + (32 if j + 1 < RW else 64), it * RW + (j + 2))
                    gathered_T((j + 2) % XB, it * 32 + 16 * ((j + 2) // XB + 1), j % 2)
                    pe.wait_ge(S["y_ready"], it * RW + (j + 1))
                    layer2(j, it * RW + (j + 1))
            for s in range(NEXP - RW, NEXP):
                if s + 1 < NEXP:
                    layer1((s + 1) % RW, 32 * ((s + 1) // RW + 1), s + 2)
                if s + 2 < NEXP:
                    gathered_T((s + 2) % XB, 16 * ((s + 2) // XB + 1), s % 2)
                pe.wait_ge(S["y_ready"], s + 1)
                layer2(s % RW, s + 1)
            for t in range(NT):
                if t >= 2:
                    pe.wait_ge(S["acc_ready"], t - 1)
                mm(ps[0:sz(t), 6 + t % 2, :], GT[:, t * P:t * P + sz(t)], b2_s[:, :], start=True, stop=True).then_inc(S["b2_mm"], 1)


_INS = ["x", "src", "dst", "L0_gnn_norm1_g", "L0_gnn_norm1_b", "L0_gnn_norm2_g", "L0_gnn_norm2_b", "L0_gnn_W_conv",
        "L0_gnn_b_conv", "L0_gnn_Wq", "L0_gnn_Wk", "L0_gnn_Wv", "L0_gnn_Wo", "L0_gnn_proj", "L0_ffn_ln1_g", "L0_ffn_ln1_b",
        "L0_ffn_wq", "L0_ffn_wk", "L0_ffn_wv", "L0_ffn_wo", "L0_ffn_ln2_g", "L0_ffn_ln2_b", "L0_ffn_wr", "L0_ffn_w1",
        "L0_ffn_b1", "L0_ffn_w2", "L0_ffn_b2"]


def kernel(**inputs):
    import numpy as _np
    import concourse.bacc as _bacc
    from concourse import mybir as _mybir
    from concourse.bass_utils import run_bass_kernel_spmd as _run

    nc = _bacc.Bacc("TRN2", target_bir_lowering=False, num_devices=1)
    arrays, args = {}, []
    for name in _INS:
        a = _np.ascontiguousarray(inputs[name])
        arrays[f"in_{name}"] = a
        args.append(nc.dram_tensor(f"in_{name}", a.shape, _mybir.dt.from_np(a.dtype), kind="ExternalInput").ap())
    args.append(nc.dram_tensor("out_0", (1250, 512), _mybir.dt.float32, kind="ExternalOutput").ap())
    build(nc, *args)
    r = _run(nc, [arrays], core_ids=[0])
    return r.results[0]["out_0"]
```

```python
import numpy as np
import concourse.bass as bass
from concourse import mybir
from contextlib import ExitStack


class Link:

    def __init__(self, eng, sem):
        self.eng, self.sem, self.n = eng, sem, 0

    def __call__(self, ins, base=0):
        self.n += 1
        ins.then_inc(self.sem, 1)
        self.eng.wait_ge(self.sem, base + self.n)


def build(nc, x, src, dst, n1g, n1b, n2g, n2b, w_conv, b_conv, gwq, gwk, gwv, gwo, proj,
          l1g, l1b, fwq, fwk, fwv, fwo, l2g, l2b, wr, w1, b1, w2, b2, out):
    f32, bf16, f16 = mybir.dt.float32, mybir.dt.bfloat16, mybir.dt.float16
    i32, u32 = mybir.dt.int32, mybir.dt.uint32
    ALU, ACT = mybir.AluOpType, mybir.ActivationFunctionType
    AXX = mybir.AxisListType.X
    RMAX = bass.bass_isa.ReduceOp.max

    P = 128
    N, D = x.shape
    E = src.shape[0]
    KD = D // P
    NT = -(-N // P)
    TAIL = N - (NT - 1) * P

    def sz(t):
        return P if t < NT - 1 else TAIL

    HEADS = 8
    DH = D // HEADS
    PAIRS = HEADS // 2
    M = proj.shape[0]
    SEQ = 256
    NQ = SEQ // P
    EPS, KEPS = 1e-5, 1e-6
    NEXP, _, F = w1.shape
    TOPK, CAP = 2, 2 * (N * 2 // NEXP)
    SLOTS = NEXP * CAP
    BN = [(0, 417), (417, 834), (834, N)]
    COLS = [(c, min(c + 512, N)) for c in range(0, N, 512)]

    ROWS = E // P
    LEFT = E - ROWS * P
    PADC = 4
    WT = 50
    WN = N // WT
    WK = NT * WT
    WIN = 18
    PAIRC = 2 * WT * E // N // P
    FIRST = 3
    ODD = PAIRC // 2 + 1
    MG = 5
    ECOLS = PADC + 384
    NB = 6
    CREDIT = 4 * WIN
    EXACT = 256
    U = 2 * NT
    PTS = 3 * U + 2
    FULL = 318

    ctx = ExitStack()
    with ctx:
        def sb(name, shape, dt=f32):
            return ctx.enter_context(nc.sbuf_tensor(name, shape, dt))

        def sem(name):
            return ctx.enter_context(nc.semaphore(name))

        xr = sb("xr", [P, NT, D])
        r2 = sb("r2", [P, NT, D])
        tA = sb("tA", [P, KD, N])
        tB = sb("tB", [P, 4 * N])
        arena = sb("arena", [P, 12500 + 8 * 2048])
        iota16 = sb("iota16", [P, 512], f16)
        identf = sb("identf", [P, P])
        tri = sb("tri", [P, P], bf16)
        onesb = sb("onesb", [P, P], bf16)
        onesf = sb("onesf", [P, 1])
        halfblk = sb("halfblk", [P, 2])
        iota64 = sb("iota64", [P, NEXP])
        tokid = sb("tokid", [P, NT], i32)
        zint = sb("zint", [P, SLOTS // P], i32)
        par = sb("par", [P, 28])
        b1T = sb("b1T", [P, P])
        wr_s = sb("wr_s", [P, KD, NEXP])
        b2_s = sb("b2_s", [NEXP, D])
        st = sb("st", [P, NT, 6])
        mv = sb("mv", [P, NT, 2])
        rs = sb("rs", [P, NT])
        bst = sb("bst", [P, KD, 3, 6])
        bmv = sb("bmv", [P, KD, 2])
        ab = sb("ab", [P, 3, KD])
        tot = sb("tot", [P, 2])
        flag = sb("flag", [1, 1], i32)
        v8 = sb("v8", [P, NT, 8])
        i8 = sb("i8", [P, NT, 8], u32)
        gk = sb("gk", [P, 8, NT, 2])
        ssum = sb("ssum", [P, NT])
        slot_i = sb("slot_i", [P, NT, 2], i32)
        sidx_i = sb("sidx_i", [P, NT, 2], i32)
        tabr = sb("tabr", [NEXP, CAP], i32)
        tabf = sb("tabf", [NEXP, CAP])
        tabT = sb("tabT", [CAP, NEXP], i32)
        nmx = sb("nmx", [P, 2])
        esum = sb("esum", [P, 2])
        resum = sb("resum", [P, 4])
        arow = sb("arow", [P, 2, P])
        ps = ctx.enter_context(nc.psum_tensor("ps", [P, 8, 512], f32))
        psf = ps[:, :, :].rearrange("p b c -> p (b c)")

        def view(t, off, *dims):
            n = int(np.prod(dims))
            v = t[:, off:off + n]
            if len(dims) == 2:
                v = v.rearrange("p (a b) -> p a b", a=dims[0])
            if len(dims) == 3:
                v = v.rearrange("p (a b c) -> p a b c", a=dims[0], b=dims[1])
            return v

        er_i = arena[:, 0:1024].bitcast(i32).rearrange("p (s b c) -> p s b c", s=2, b=4)
        er_f = view(arena, 1024, 2, 4, P)
        pj = view(arena, 2048, 2, 2, DH)
        b1r = arena[:, 2304:2432]
        prow = arena[0:28, 2432:2560]
        projblk = view(arena, 11400, 2, M)
        qk = view(arena, 0, 2, PAIRS, SEQ)
        vaug = view(arena, 2048, NQ, HEADS, DH + 1)
        qf = view(arena, 3100, NQ, HEADS, M)
        kf = view(arena, 7200, NQ, HEADS, M)
        sq = view(arena, 7200, 2, PAIRS, SEQ)
        qfT = view(tB, 0, 2, M // P, SEQ)
        kv = view(tB, 1024, HEADS, M // P, DH + 1)
        attnrow = view(tB, 2064, NQ, D)
        attnTg = view(tB, 0, KD, SEQ)
        hatt = view(tB, 3088, KD, SEQ)
        dg = view(tB, 4112, 2, NQ, HEADS)
        mk = view(tB, 4150, NQ, HEADS)
        mk8 = tB[:, 4170:4178]
        gmk = tB[:, 4180:4188]
        bk = view(tB, 4190, NQ, HEADS)
        bq = view(tB, 4210, NQ, HEADS)
        zr = view(tB, 4230, 2, 2)
        gw = [view(arena, 12500 + 2048 * i, KD, D) for i in range(4)]
        AT = [arena[:, 6250 * i:6250 * i + 6250].bitcast(bf16).rearrange("p (a n) -> p a n", a=NT) for i in range(2)]
        xs = [arena[:, 12500 + 2560 * i:12500 + 2560 * (i + 1)].bitcast(bf16).rearrange("p (t d) -> p t d", t=NT) for i in range(3)]
        key = arena[:, 20692:20692 + WN * WIN]
        efa = arena[:, 21142:21142 + ECOLS]
        tk = arena[:, 21530:21530 + WN * WIN]
        wfirst = arena[:, 21980:21980 + WN]
        wc = view(arena, 22740, KD, D)
        ohm = arena[:, 24788:24788 + 2 * PAIRC * 64].bitcast(bf16).rearrange("p (b c) -> p b c", b=2 * PAIRC)
        rdegB = arena[:, 24788:24788 + N]
        ef = view(arena, 24788 + 2 * PAIRC * 64, 2, ECOLS)
        em = arena[:, 22010:22010 + ECOLS // 2].bitcast(f16)
        ei = [arena[:, 400 * i:400 * i + ECOLS].bitcast(i32) for i in range(3)]
        ohs = tB[:, 1536:1536 + NB * WK // 2].bitcast(bf16).rearrange("p (b c) -> p b c", b=NB)
        aggT = view(tB, 0, KD, 512)
        rl = view(tB, 2048, 2, 512)
        nrow = view(arena, 0, NT, D)
        QT = view(arena, 0, 2, N)
        KT = arena[:, 2500:2500 + N]
        V = view(arena, 3750, NT, P)
        Pb = view(arena, 5030, 2, N)
        PT = view(arena, 7530, 2, NT, P)
        wst = view(arena, 10090, 3, KD, P)
        g2row = view(arena, 9024, 2, D)
        wo_s = view(arena, 10090, KD, D)
        attnT = view(tB, 0, KD, N)
        x2T = view(arena, 5120, 2, KD, P)
        lg = view(arena, 6144, NT, NEXP)
        ex = view(arena, 6784, NT, NEXP)
        ohk = [view(arena, 7424 + 640 * k, NT, NEXP) for k in range(2)]
        O = arena[:, 8704:9024].bitcast(bf16).rearrange("p (t e) -> p t e", t=NT)
        posm = view(arena, 9024, NT, NEXP)
        tmp = view(arena, 9664, NT, NEXP)
        G = view(arena, 10304, NT, NEXP)
        GT = tB[0:NEXP, 0:N]
        RW = 8
        ring = [view(arena, 12500 + 2048 * i, 2048) for i in range(RW)]
        ring1 = [r[:, 0:1024].rearrange("p (k f) -> p k f", k=KD) for r in ring]
        ring2 = [r[:, 1024:2048].rearrange("p (k f) -> p k f", k=F // P) for r in ring]
        tAf = tA[:, :, :].rearrange("p k n -> p (k n)")
        XB = 4
        xb = view(tAf, 0, XB, D)
        xT = view(tAf, 2048, 2, KD, CAP)
        hT = view(tAf, 2048 + 624, 2, F // P, CAP)
        ys = view(tAf, 2048 + 624 + 312, 2, D)
        ygat = view(arena, 0, 4, D)

        x2d = nc.dram_tensor("x2d", [N, D], f32).ap()
        tabd = nc.dram_tensor("tabd", [SLOTS, 1], i32).ap()
        yd = nc.dram_tensor("yd", [SLOTS, D], f32).ap()

        names = """x_in edges_in params_in gw_in wc_in wst_in wo_in route_in ln2_in tab_zeroed x2_out tab_scattered
            tab_in out_stored consts pool_link dve_link act_link raw_ready raw_T ef_ready par_T par_ready b1_ready
            var_ready sd_ready h_ready h_T hT_ready bvar_ready bsd_ready xnT_ready xn_T xn_ready
            qk_mm qk_ready v_mm v_ready sq_ready dg_mm u_mm uk_copied uk_maxed uq_bias uq_exp mk_ready gmk_ready
            bk_ready kexp_done kf_ready qf_ready kv_mm kv_ready qfT_mm qfT_ready ga_mm ga_ready ga_T gaT_ready
            ho_mm hatt_ready wbase_ready ohm_ready oh_ready oh_used cnt_ready gcnt_oh_ready gcnt_oh_used gcnt_hi gcnt_link gcnt_ready
            xs_hi xs_rest xs_mid xs_ready deg_mm flag_ready rdeg_ready agg_mm agg_ready conv_mm rl_ready z_ready
            w_ready w_T x1_ready n1_ready n1_T n1T_raw x1T_ready qpad_ready proj_done
            qkv_act qkv_dve s_mm negmax exp_done p_T pt_dve pt_act
            wo_mm xx_ready x2_ready x2_T x2T_ready lg_mm exs_ready exp_ready O_ready pos_mm idx_ready G_ready G_T GT_ready
            tabf_ready tab_T tabT_ready xT_mm xT_ready l1_mm gelu_done l2_mm y_ready
            b2_mm loop_link acc_ready""".split()
        S = {n: sem(n) for n in names}
        w_in = [sem(f"w_in{i}") for i in range(RW)]
        xb_in = [sem(f"xb_in{i}") for i in range(XB)]
        y_stored = [sem(f"y_stored{i}") for i in range(2)]
        yg_in = [sem(f"yg_in{i}") for i in range(4)]

        block = ctx.enter_context(nc.Block())

        @block.sync
        def _(sp):
            full = (NT - 1) * P
            sp.dma_start(xr[:, 0:NT - 1, :], x[0:full, :].rearrange("(t p) d -> p t d", p=P)).then_inc(S["x_in"], 16)
            sp.dma_start(xr[0:TAIL, NT - 1, :], x[full:N, :]).then_inc(S["x_in"], 16)
            for i, v in enumerate((src, dst)):
                rows = v[0:ROWS * P].rearrange("(r c) -> r c", c=P)
                sp.dma_start(er_i[:, i, 0:2, :], rows[0:2 * P, :].rearrange("(b p) c -> p b c", p=P)).then_inc(S["edges_in"], 16)
                sp.dma_start(er_i[0:ROWS - 2 * P, i, 2, :], rows[2 * P:ROWS, :]).then_inc(S["edges_in"], 16)
                sp.dma_start(er_i[0:1, i, 3, 0:LEFT], v[ROWS * P:E].rearrange("(a n) -> a n", a=1)).then_inc(S["edges_in"], 16)
            for i, v in enumerate((n1g, n1b, n2g, n2b, b_conv, l1g, l1b)):
                sp.dma_start(prow[KD * i:KD * i + KD, :], v.rearrange("(k p) -> k p", p=P)).then_inc(S["params_in"], 16)
            sp.dma_start(b1r[:, :], b1.rearrange("e (h p) -> (e h) p", p=P)).then_inc(S["params_in"], 16)
            for dup in range(2):
                sp.dma_start(pj[:, :, dup, :], proj.rearrange("(t p) d -> p t d", p=P)).then_inc(S["params_in"], 16)
            for i, w in enumerate((gwq, gwk, gwv, gwo)):
                sp.dma_start(gw[i], w.rearrange("(k p) n -> p k n", p=P)).then_inc(S["gw_in"], 16)
            sp.dma_start(wc, w_conv.rearrange("(k p) n -> p k n", p=P)).then_inc(S["wc_in"], 16)
            sp.dma_start(wr_s[:, :, :], wr.rearrange("(k p) n -> p k n", p=P)).then_inc(S["route_in"], 16)
            sp.dma_start(b2_s[:, :], b2).then_inc(S["route_in"], 16)
            sp.wait_ge(S["consts"], 1)
            sp.dma_start(tabd.rearrange("(p c) a -> p (c a)", p=P), zint[:, :]).then_inc(S["tab_zeroed"], 16)
            sp.wait_ge(S["conv_mm"], 3 * KD)

            def load_expert(slot, w1e, w2e):
                sp.dma_start(ring1[slot], w1e).then_inc(w_in[slot], 16)
                sp.dma_start(ring2[slot], w2e).then_inc(w_in[slot], 16)

            w1v = w1.rearrange("e (k p) f -> e p k f", p=P)
            w2v = w2.rearrange("e (k p) n -> e p k n", p=P)
            qv, kvv, vv = (w.rearrange("(k p) n -> p k n", p=P) for w in (fwq, fwk, fwv))
            for e in range(RW):
                load_expert(e, w1v[e], w2v[e])
            with sp.Fori(0, PAIRS) as pr:
                sp.wait_ge(S["proj_done"], pr + 1)
                for i, w in enumerate((qv, kvv, vv)):
                    sp.dma_start(wst[:, i, :, :], w[:, :, bass.ds(pr * P, P)]).then_inc(S["wst_in"], 16)

            sp.wait_ge(S["proj_done"], PAIRS + 1)
            sp.dma_start(wo_s, fwo.rearrange("(k p) n -> p k n", p=P)).then_inc(S["wo_in"], 16)
            sp.wait_ge(S["pt_dve"], PAIRS * (2 * U + 2) + 1)
            sp.dma_start(g2row[:, 0, :], l2g.rearrange("(a n) -> a n", a=1).to_broadcast([P, D])).then_inc(S["ln2_in"], 16)
            sp.dma_start(g2row[:, 1, :], l2b.rearrange("(a n) -> a n", a=1).to_broadcast([P, D])).then_inc(S["ln2_in"], 16)
            for t in range(NT):
                sp.wait_ge(S["x2_ready"], t + 1)
                sp.dma_start(x2d[t * P:t * P + sz(t), :], nrow[0:sz(t), t, :]).then_inc(S["x2_out"], 16)
            sp.wait_ge(S["tab_scattered"], 32 * NT)
            sp.dma_start(tabr[:, :], tabd.rearrange("(e c) a -> e (c a)", c=CAP)).then_inc(S["tab_in"], 16)

            with sp.Fori(0, NEXP // RW - 1) as it:
                for j in range(RW):
                    sp.wait_ge(S["l2_mm"], it * RW + (j + 3))
                    load_expert(j, w1v[bass.ds(it * RW + (j + RW), 1)].rearrange("e p k f -> p (e k) f"),
                                w2v[bass.ds(it * RW + (j + RW), 1)].rearrange("e p k f -> p (e k) f"))
                    sp.wait_ge(S["y_ready"], it * RW + (j + 3))
                    sp.dma_start(yd[bass.ds(it * (RW * CAP) + j * CAP, CAP), :], ys[0:CAP, j % 2, :]).then_inc(y_stored[j % 2], 16)
            for s in range(NEXP - RW, NEXP):
                sp.wait_ge(S["y_ready"], s + 3)
                sp.dma_start(yd[s * CAP:(s + 1) * CAP, :], ys[0:CAP, s % 2, :]).then_inc(y_stored[s % 2], 16)
            for t in range(NT):
                sp.wait_ge(S["acc_ready"], t + 1)
                sp.dma_start(out[t * P:t * P + sz(t), :], xr[0:sz(t), t, :]).then_inc(S["out_stored"], 16)
            sp.wait_ge(S["out_stored"], 16 * NT)

        @block.gpsimd
        def _(pool):
            link = Link(pool, S["pool_link"])
            nc.gpsimd.memset(zint[:, :], 0).then_inc(S["consts"], 1)
            nc.gpsimd.iota(tk, pattern=[[WT, WN], [0, WIN]], base=0, channel_multiplier=0,
                           allow_small_or_imprecise_dtypes=True)
            nc.gpsimd.iota(wfirst, pattern=[[WT, WN]], base=0, channel_multiplier=0,
                           allow_small_or_imprecise_dtypes=True).then_inc(S["wbase_ready"], 1)
            nc.gpsimd.iota(iota16[:, :], pattern=[[1, 512]], base=0, channel_multiplier=0,
                           allow_small_or_imprecise_dtypes=True)
            nc.gpsimd.iota(iota64[:, :], pattern=[[1, NEXP]], base=0, channel_multiplier=0,
                           allow_small_or_imprecise_dtypes=True)
            nc.gpsimd.iota(tokid[:, :], pattern=[[P, NT]], base=0, channel_multiplier=1)
            nc.gpsimd.memset(onesb[:, :], 1.0)
            nc.gpsimd.memset(tri[:, :], 1.0)
            link(nc.gpsimd.memset(identf[:, :], 0.0))
            nc.gpsimd.affine_select(out=identf[:, :], in_=identf[:, :], compare_op=ALU.not_equal, fill=1.0, base=0,
                                    pattern=[[-1, P]], channel_multiplier=1)
            nc.gpsimd.affine_select(out=tri[:, :], in_=tri[:, :], compare_op=ALU.is_gt, fill=0.0, base=0,
                                    pattern=[[1, P]], channel_multiplier=-1).then_inc(S["consts"], 1)
            pool.wait_ge(S["mk_ready"], 1)
            nc.gpsimd.partition_all_reduce(gmk, mk8, P, RMAX).then_inc(S["gmk_ready"], 1)
            def split_tile(t, part):
                x = r2[0:sz(t), t, :]
                if part == 0:
                    pool.wait_ge(S["xs_hi"], t + 1)
                    nc.gpsimd.tensor_tensor(x, x, xs[0][0:sz(t), t, :], ALU.subtract).then_inc(S["xs_rest"], 1)
                else:
                    pool.wait_ge(S["xs_mid"], t + 1)
                    nc.gpsimd.tensor_tensor(xs[2][0:sz(t), t, :], x, xs[1][0:sz(t), t, :], ALU.subtract).then_inc(S["xs_ready"], 1)

            for part in range(2):
                for t in range(NT):
                    split_tile(t, part)
            pool.wait_ge(S["n1_T"], NT)
            nc.gpsimd.memset(QT[64:128, 0, :], 0.0)
            nc.gpsimd.memset(QT[0:64, 1, :], 0.0).then_inc(S["qpad_ready"], 1)
            pool.wait_ge(S["idx_ready"], 1)
            pool.wait_ge(S["tab_zeroed"], 16)
            for t in range(NT):
                for k in range(TOPK):
                    nc.gpsimd.indirect_dma_start(
                        out=tabd, out_offset=bass.IndirectOffsetOnAxis(ap=sidx_i[0:sz(t), t, k:k + 1], axis=0),
                        in_=tokid[0:sz(t), t:t + 1], in_offset=None,
                        bounds_check=SLOTS - 1, oob_is_err=False).then_inc(S["tab_scattered"], 16)
            pool.wait_ge(S["tabT_ready"], 1)
            pool.wait_ge(S["x2_out"], 16 * NT)
            for e in range(NEXP):
                if e >= XB:
                    pool.wait_ge(S["xT_mm"], e - XB + 1)
                nc.gpsimd.indirect_dma_start(
                    out=xb[0:CAP, e % XB, :], out_offset=None, in_=x2d,
                    in_offset=bass.IndirectOffsetOnAxis(ap=tabT[:, e:e + 1], axis=0)).then_inc(xb_in[e % XB], 16)
            for k in range(2):
                pool.wait_ge(y_stored[k], 16 * (NEXP // 2) + 16)
            for t in range(NT):
                for k in range(TOPK):
                    n = t * TOPK + k
                    if n >= 4:
                        pool.wait_ge(S["acc_ready"], (n - 4) // TOPK + 1)
                    nc.gpsimd.indirect_dma_start(
                        out=ygat[0:sz(t), n % 4, :], out_offset=None, in_=yd,
                        in_offset=bass.IndirectOffsetOnAxis(ap=slot_i[0:sz(t), t, k:k + 1], axis=0)).then_inc(yg_in[n % 4], 16)

        @block.scalar
        def _(act):
            act_ = nc.scalar.activation
            act.wait_ge(S["var_ready"], 1)
            act_(rs[:, :], rs[:, :], ACT.Sqrt).then_inc(S["sd_ready"], 1)
            for t in range(NT):
                act.wait_ge(S["h_T"], t + 1)
                act_(tA[:, :, t * P:t * P + sz(t)], ps[:, 2 + t % 2, :].rearrange("p (k c) -> p k c", k=KD)[:, :, 0:sz(t)],
                     ACT.Copy).then_inc(S["hT_ready"], 1)
            act.wait_ge(S["bvar_ready"], 1)
            act_(ab[:, 0, :], ab[:, 0, :], ACT.Sqrt).then_inc(S["bsd_ready"], 1)
            for t in range(NT):
                act.wait_ge(S["xn_T"], t + 1)
                act_(r2[0:sz(t), t, :], ps[0:sz(t), 2 + t % 2, :], ACT.Copy).then_inc(S["xn_ready"], 1)

            for p in range(PAIRS):
                act.wait_ge(S["qk_mm"], p + 1)
                act_(qk[:, :, p, :], ps[:, p % 2, :].rearrange("p (s c) -> p s c", s=2), ACT.Copy,
                     scale=float(DH) ** -0.25).then_inc(S["qk_ready"], 1)
            act.wait_ge(S["qk_ready"], PAIRS)
            act_(sq, qk, ACT.Square).then_inc(S["sq_ready"], 1)
            act.wait_ge(S["dg_mm"], 1)
            for u in range(NQ * PAIRS):
                nt, p = divmod(u, PAIRS)
                act.wait_ge(S["u_mm"], u + 1)
                act_(kf[:, nt, 2 * p:2 * p + 2, :], ps[:, 5 + u % 3, :].rearrange("p (h m) -> p h m", h=2),
                     ACT.Copy).then_inc(S["uk_copied"], 1)
            for u in range(NQ * PAIRS):
                nt, p = divmod(u, PAIRS)
                act.wait_ge(S["uq_bias"], u + 1)
                for h in range(2):
                    act_(qf[:, nt, 2 * p + h, :], ps[:, 5 + (u + 8) % 3, h * M:(h + 1) * M], ACT.Exp,
                         bias=bq[:, nt, 2 * p + h:2 * p + h + 1]).then_inc(S["uq_exp"], 1)
            act.wait_ge(S["bk_ready"], 1)
            act.wait_ge(S["uk_copied"], NQ * PAIRS)
            for nt in range(NQ):
                for h in range(HEADS):
                    act_(kf[:, nt, h, :], kf[:, nt, h, :], ACT.Exp, bias=bk[:, nt, h:h + 1]).then_inc(S["kexp_done"], 1)
            for h in range(HEADS):
                act.wait_ge(S["qfT_mm"], h + 1)
                if h >= 2:
                    act.wait_ge(S["ga_mm"], h - 1)
                act_(qfT[:, h % 2, :, :], ps[:, 4 + h % 2, :].rearrange("p (m n) -> p m n", m=M // P),
                     ACT.Copy).then_inc(S["qfT_ready"], 1)
            for b in range(2):
                act.wait_ge(S["ga_T"], b + 1)
                act_(attnTg[:, 2 * b:2 * b + 2, :], ps[:, b, :].rearrange("p (k n) -> p k n", k=2), ACT.Copy).then_inc(S["gaT_ready"], 1)
            for b in range(2):
                act.wait_ge(S["ho_mm"], b + 1)
                act_(hatt[:, 2 * b:2 * b + 2, :], ps[:, 2 + b, :].rearrange("p (k n) -> p k n", k=2), ACT.Copy).then_inc(S["hatt_ready"], 1)

            for part in range(2):
                for t in range(NT):
                    act.wait_ge(S["xs_rest"] if part else S["hatt_ready"], t + 1 if part else 2)
                    act_(xs[part][0:sz(t), t, :], r2[0:sz(t), t, :], ACT.Copy).then_inc(S["xs_mid"] if part else S["xs_hi"], 1)
            with act.Fori(0, WN // 4) as it:
                for w in range(4):
                    act.wait_ge(S["oh_used"], it * (4 * WIN) + ((w + 1) * WIN + CREDIT))
                    act_(AT[0][:, :, bass.ds(it * (4 * WT) + w * WT, WT)], ps[:, 4 + w, 0:WK].rearrange("p (a n) -> p a n", a=NT),
                         ACT.Copy).then_inc(S["cnt_ready"], 1)
            act.wait_ge(S["oh_used"], WN * WIN + CREDIT)
            act_(AT[0][:, :, N - WT:N], ps[:, 4, 0:WK].rearrange("p (a n) -> p a n", a=NT), ACT.Copy).then_inc(S["cnt_ready"], 1)
            act.wait_ge(S["flag_ready"], 1)
            total = act.value_load(flag[0:1, 0:1], min_val=0, max_val=E)
            with act.If(total < E):
                with act.Fori(0, WN) as w:
                    act.wait_ge(S["gcnt_oh_used"], w * FULL + (NB + FULL))
                    act_(AT[0][:, :, bass.ds(w * WT, WT)], ps[:, 4, 0:WK].rearrange("p (a n) -> p a n", a=NT),
                         ACT.Copy).then_inc(S["gcnt_hi"], 1)
            for c, (c0, c1) in enumerate(COLS):
                cn = c1 - c0
                for fo in range(KD):
                    n = c * KD + fo
                    act.wait_ge(S["conv_mm"], n + 1)
                    if n >= 2:
                        act.wait_ge(S["z_ready"], n - 1)
                    act_(rl[:, n % 2, 0:cn], ps[:, 7 - 7 * (n % 2), 0:cn], ACT.Relu,
                         bias=par[:, 4 * KD + fo:4 * KD + fo + 1]).then_inc(S["rl_ready"], 1)
            act.wait_ge(S["bvar_ready"], 2)
            act_(ab[:, 0, :], ab[:, 0, :], ACT.Sqrt).then_inc(S["bsd_ready"], 1)
            for r in range(2):
                act.wait_ge(S["var_ready"], 2 + r)
                act_(rs[:, :], rs[:, :], ACT.Sqrt).then_inc(S["sd_ready"], 1)
            for t in range(NT):
                act.wait_ge(S["n1_T"], t + 1)
                act_(tA[:, :, t * P:t * P + sz(t)], ps[:, 2 + t % 2, :].rearrange("p (k c) -> p k c", k=KD)[:, :, 0:sz(t)],
                     ACT.Copy).then_inc(S["n1T_raw"], 1)

            with act.Fori(0, PAIRS) as pr:
                act.wait_ge(S["proj_done"], pr + 2)
                for h in range(2):
                    half = slice(h * DH, (h + 1) * DH)
                    act_(QT[half, h, :], psf[half, 0:N], ACT.Copy, scale=float(DH) ** -0.5).then_inc(S["qkv_act"], 1)
                act_(V[:, 0:4, :], ps[:, 6, :].rearrange("p (t c) -> p t c", t=4), ACT.Copy).then_inc(S["qkv_act"], 1)
                act_(V[:, 8, :], ps[:, 2, 256:384], ACT.Copy).then_inc(S["qkv_act"], 1)
                act_(V[0:TAIL, 9, :], ps[0:TAIL, 2, 384:512], ACT.Copy).then_inc(S["qkv_act"], 1)

                def exp_unit(i):
                    qt = sz(i // 2)
                    act.wait_ge(S["negmax"], pr * U + (i + 1))
                    if i >= 2:
                        act.wait_ge(S["p_T"], pr * PTS + 3 * (i - 1))
                    act_(Pb[0:qt, i % 2, :], psf[0:qt, 1536 * (i % 2):1536 * (i % 2) + N], ACT.Exp,
                         bias=nmx[0:qt, i % 2:i % 2 + 1],
                         accum_out=esum[0:qt, i % 2:i % 2 + 1]).then_inc(S["exp_done"], 1)

                exp_unit(0)
                for i in range(U):
                    if i + 1 < U:
                        exp_unit(i + 1)
                    act.wait_ge(S["p_T"], pr * PTS + 3 * i + 2)
                    act_(PT[:, i % 2, 4:8, 0:sz(i // 2)],
                         ps[:, 6 + (3 * i + 1) % 2, :].rearrange("p (t c) -> p t c", t=4)[:, :, 0:sz(i // 2)],
                         ACT.Copy).then_inc(S["pt_act"], 1)

            act.wait_ge(S["var_ready"], 4)
            act_(rs[:, :], rs[:, :], ACT.Sqrt).then_inc(S["sd_ready"], 1)
            for t in range(NT):
                act.wait_ge(S["x2_T"], t + 1)
                if t >= 2:
                    act.wait_ge(S["lg_mm"], t - 1)
                act_(x2T[:, t % 2, :, 0:sz(t)], ps[:, 2 + t % 2, :].rearrange("p (k c) -> p k c", k=KD)[:, :, 0:sz(t)],
                     ACT.Copy).then_inc(S["x2T_ready"], 1)
            act.wait_ge(S["exs_ready"], 1)
            act_(ex, ex, ACT.Exp)
            act_(gk[:, 0, :, :], gk[:, 0, :, :], ACT.Exp).then_inc(S["exp_ready"], 1)
            for c, (c0, c1) in enumerate(COLS):
                act.wait_ge(S["G_T"], c + 1)
                act_(GT[:, c0:c1], ps[0:NEXP, c, 0:c1 - c0], ACT.Copy).then_inc(S["GT_ready"], 1)
            with act.Fori(0, NEXP // 2) as it:
                for j in range(2):
                    act.wait_ge(S["l1_mm"], it * 2 + (j + 1))
                    act.wait_ge(S["l2_mm"], it * 2 + (j + 1))
                    for f in range(F // P):
                        last = act_(hT[:, j, f, :], ps[:, 2 + j, f * P:f * P + CAP], ACT.Gelu_apprx_tanh,
                                    bias=b1T[:, bass.ds(it * 4 + (2 * j + f), 1)])
                    last.then_inc(S["gelu_done"], 1)

        @block.vector
        def _(dve):
            V_ = nc.vector
            link = Link(dve, S["dve_link"])
            V_.memset(mv[:, :, :], 1.0)
            V_.memset(er_f, -1.0)
            V_.memset(ef[:, :, 0:PADC], -1.0)
            V_.memset(onesf[:, :], 1.0)
            link(V_.memset(halfblk[:, :], 0.0))
            V_.memset(halfblk[0:64, 0:1], 0.5)
            V_.memset(halfblk[64:128, 1:2], 0.5)
            V_.memset(projblk, 0.0)
            dve.wait_ge(S["edges_in"], 96)
            V_.tensor_copy(er_f[:, :, 0:2, :], er_i[:, :, 0:2, :])
            V_.tensor_copy(er_f[0:ROWS - 2 * P, :, 2, :], er_i[0:ROWS - 2 * P, :, 2, :])
            V_.tensor_copy(er_f[0:1, :, 3, 0:LEFT], er_i[0:1, :, 3, 0:LEFT]).then_inc(S["raw_ready"], 1)

            def layer_norm_stats(rows, n):
                for t in range(NT):
                    last = V_.bn_stats(st[0:sz(t), t, :], rows[0:sz(t), t, :])
                link(last)
                for t in range(NT):
                    last = V_.bn_aggr(mv[0:sz(t), t, :], st[0:sz(t), t, :])
                link(last)
                V_.tensor_scalar(rs[:, :], mv[:, :, 1], EPS, None, ALU.add).then_inc(S["var_ready"], 1)
                dve.wait_ge(S["sd_ready"], n)
                link(V_.reciprocal(rs[:, :], rs[:, :]))

            def batch_norm_affine(first, g0, b0):
                for k in range(KD):
                    for i, (c0, c1) in enumerate(BN):
                        last = V_.bn_stats(bst[:, k, i, :], tA[:, k, c0:c1])
                link(last)
                for k in range(KD):
                    last = V_.bn_aggr(bmv[:, k, :], bst[:, k, :, :].rearrange("p a b -> p (a b)"))
                link(last)
                V_.tensor_scalar(ab[:, 0, :], bmv[:, :, 1], EPS, None, ALU.add).then_inc(S["bvar_ready"], 1)
                dve.wait_ge(S["bsd_ready"], first)
                link(V_.reciprocal(ab[:, 0, :], ab[:, 0, :]))
                link(V_.tensor_tensor(ab[:, 1, :], ab[:, 0, :], par[:, g0:g0 + KD], ALU.mult))
                link(V_.tensor_tensor(ab[:, 2, :], bmv[:, :, 0], ab[:, 1, :], ALU.mult))
                link(V_.tensor_tensor(ab[:, 2, :], par[:, b0:b0 + KD], ab[:, 2, :], ALU.subtract))

            dve.wait_ge(S["x_in"], 32)
            layer_norm_stats(xr, 1)
            for t in range(NT):
                V_.tensor_scalar(r2[0:sz(t), t, :], xr[0:sz(t), t, :], mv[0:sz(t), t, 0:1], rs[0:sz(t), t:t + 1],
                                 ALU.subtract, ALU.mult).then_inc(S["h_ready"], 1)
            dve.wait_ge(S["raw_T"], 1)
            link(V_.tensor_copy(ef[:, :, PADC:PADC + 384], ps[:, 0:2, 0:384]))
            link(V_.tensor_copy(ef[:, :, PADC + ROWS:PADC + ROWS + 1], ps[:, 0:2, 384:385]))
            link(V_.tensor_copy(ei[0], ef[:, 0, :]))
            V_.tensor_scalar(ei[1], ei[0], 7, None, ALU.arith_shift_right)
            link(V_.tensor_scalar(ei[2], ei[0], 127, None, ALU.bitwise_and))
            V_.tensor_copy(efa, ei[1])
            V_.tensor_copy(em, ei[2])
            link(V_.tensor_copy(ef[:, 0, :], ei[2]))
            link(V_.scalar_tensor_tensor(efa, efa, float(WT), ef[:, 1, :], ALU.mult, ALU.add))
            V_.memset(tot[:, :], 0.0).then_inc(S["ef_ready"], 1)
            dve.wait_ge(S["wbase_ready"], 1)

            def windows(v, odd):
                c = PADC - FIRST + (ODD if odd else 0)
                n = (WN + 1 - odd) // 2
                return v[:, c:c + PAIRC * n].rearrange("p (w c) -> p w c", w=n)[:, :, 0:WIN]

            def outside(k, t, link, base=0):
                link(V_.tensor_scalar(t, t, (WT - 1) / 2.0, None, ALU.subtract), base)
                link(V_.tensor_tensor(t, t, t, ALU.mult), base)
                link(V_.tensor_scalar(t, t, WT * WT / 4.0, 4096.0, ALU.is_gt, ALU.mult), base)
                return V_.tensor_tensor(k, k, t, ALU.add)

            keyv, tkv = (v.rearrange("p (w c) -> p w c", w=WN) for v in (key, tk))
            for q in range(2):
                last = V_.tensor_tensor(keyv[:, q::2, :], windows(efa, q), tkv[:, q::2, :], ALU.subtract)
            link(last)
            for q in range(2):
                last = V_.tensor_tensor(tkv[:, q::2, :], windows(ef[:, 1, :], q), tkv[:, q::2, :], ALU.subtract)
            link(last)
            link(outside(key, tk, link))
            dve.wait_ge(S["par_T"], 1)
            V_.tensor_copy(par[:, :], ps[:, 4, 0:28])
            V_.tensor_copy(b1T[:, :], ps[:, 4, 128:256])
            V_.tensor_copy(projblk[0:64, 0, :], ps[0:64, 5, 0:M])
            V_.tensor_copy(projblk[64:128, 1, :], ps[64:128, 5, 0:M]).then_inc(S["par_ready"], 1)
            dve.wait_ge(S["hT_ready"], NT)
            batch_norm_affine(1, 0, KD)
            for k in range(KD):
                V_.tensor_scalar(tB[:, k * N:(k + 1) * N], tA[:, k, :], ab[:, 1, k:k + 1], ab[:, 2, k:k + 1],
                                 ALU.mult, ALU.add).then_inc(S["xnT_ready"], 1)
            V_.memset(vaug[:, :, :, DH:DH + 1], 1.0)
            for nt in range(NQ):
                dve.wait_ge(S["v_mm"], nt + 1)
                V_.tensor_copy(vaug[:, nt, :, 0:DH], ps[:, 2 + nt, :].rearrange("p (h d) -> p h d", h=HEADS)).then_inc(S["v_ready"], 1)
            dve.wait_ge(S["dg_mm"], 1)
            link(V_.tensor_copy(dg, ps[:, 4, 0:2 * NQ * HEADS].rearrange("p (s n h) -> p s n h", s=2, n=NQ)))
            for u in range(NQ * PAIRS):
                nt, p = divmod(u, PAIRS)
                dve.wait_ge(S["uk_copied"], u + 1)
                V_.tensor_reduce(mk[:, nt, 2 * p:2 * p + 2], kf[:, nt, 2 * p:2 * p + 2, :], AXX, ALU.max).then_inc(S["uk_maxed"], 1)
            dve.wait_ge(S["uk_maxed"], NQ * PAIRS)
            V_.tensor_tensor(mk8, mk[:, 0, :], mk[:, 1, :], ALU.max).then_inc(S["mk_ready"], 1)
            for u in range(NQ * PAIRS):
                nt, p = divmod(u, PAIRS)
                dve.wait_ge(S["u_mm"], NQ * PAIRS + u + 1)
                link(V_.tensor_reduce(bq[:, nt, 2 * p:2 * p + 2], ps[:, 5 + (u + 8) % 3, :].rearrange("p (h m) -> p h m", h=2),
                                      AXX, ALU.max))
                V_.scalar_tensor_tensor(bq[:, nt, 2 * p:2 * p + 2], bq[:, nt, 2 * p:2 * p + 2], -1.0, dg[:, 0, nt, 2 * p:2 * p + 2],
                                        ALU.mult, ALU.subtract).then_inc(S["uq_bias"], 1)
            dve.wait_ge(S["gmk_ready"], 1)
            for nt in range(NQ):
                last = V_.scalar_tensor_tensor(bk[:, nt, :], gmk, -1.0, dg[:, 1, nt, :], ALU.mult, ALU.subtract)
            last.then_inc(S["bk_ready"], 1)
            dve.wait_ge(S["uq_exp"], NQ * HEADS)
            V_.tensor_scalar(qf, qf, 1.0 / float(np.sqrt(M)), KEPS, ALU.mult, ALU.add).then_inc(S["qf_ready"], 1)
            dve.wait_ge(S["kexp_done"], NQ * HEADS)
            V_.tensor_scalar(kf, kf, 1.0 / float(np.sqrt(M)), KEPS, ALU.mult, ALU.add).then_inc(S["kf_ready"], 1)
            for b in range(4):
                dve.wait_ge(S["kv_mm"], b + 1)
                V_.tensor_copy(kv[:, 2 * b:2 * b + 2, :, :], ps[:, b, :].rearrange("p (h m c) -> p h m c", h=2, m=2)[:, :, :, 0:DH + 1])\
                  .then_inc(S["kv_ready"], 1)
            for h in range(HEADS):
                dve.wait_ge(S["ga_mm"], h + 1)
                o = ps[:, 6 + h % 2, 0:256].rearrange("p (n c) -> p n c", n=NQ)
                link(V_.tensor_scalar(zr[:, h % 2, :], o[:, :, DH], KEPS, None, ALU.add))
                link(V_.reciprocal(zr[:, h % 2, :], zr[:, h % 2, :]))
                for nt in range(NQ):
                    last = V_.tensor_scalar(attnrow[:, nt, h * DH:(h + 1) * DH], o[:, nt, 0:DH], zr[:, h % 2, nt:nt + 1],
                                            None, ALU.mult)
                last.then_inc(S["ga_ready"], 1)

            dve.wait_ge(S["ga_T"], 2)

            def m_onehots(block, g, col):
                nc.vector.tensor_tensor(
                    ohm[:, block * PAIRC + g * MG:block * PAIRC + (g + 1) * MG, :],
                    iota16[:, 0:P].rearrange("p (a c) -> p a c", a=1).to_broadcast([P, MG, P]),
                    em[:, bass.ds(col + g * MG, MG)].rearrange("p (a c) -> p a c", c=1).to_broadcast([P, MG, P]),
                    ALU.is_equal).then_inc(S["ohm_ready"], MG)

            def window_onehots(odd, block, step, col=None):
                for i in range(WIN):
                    dve.wait_ge(S["oh_used"], step + (i + 1 - NB + CREDIT))
                    V_.tensor_scalar(ohs[:, i % NB, :], iota16[:, 0:WK], key[:, bass.ds(step + i, 1)], None,
                                     ALU.is_equal).then_inc(S["oh_ready"], 1)
                    if col is not None and not odd and i in (6, 10, 14):
                        m_onehots(1 - block, (i - 6) // 4 + 2, col + PAIRC)
                    if col is not None and odd and i in (8, 13):
                        m_onehots(block, (i - 8) // 5, col + 2 * PAIRC)

            for g in range(PAIRC // MG + 2):
                m_onehots(g // (PAIRC // MG), g % (PAIRC // MG), PADC - FIRST + PAIRC * (g // (PAIRC // MG)))
            with dve.Fori(0, WN // 4) as it:
                for w in range(4):
                    window_onehots(w % 2, w // 2, it * (4 * WIN) + w * WIN,
                                   it * (2 * PAIRC) + ((w // 2) * PAIRC + PADC - FIRST))
            window_onehots(0, 0, (WN - 1) * WIN)
            dve.wait_ge(S["deg_mm"], 1)
            V_.tensor_reduce(tot[:, 0:1], psf[:, 0:N], AXX, ALU.add)
            link(V_.tensor_reduce(tot[:, 1:2], psf[:, 0:N], AXX, ALU.max))
            V_.scalar_tensor_tensor(flag[0:1, 0:1], tot[0:1, 1:2], float(EXACT), tot[0:1, 0:1], ALU.is_lt, ALU.mult)\
              .then_inc(S["flag_ready"], 1)
            dve.wait_ge(S["flag_ready"], 1)
            total = dve.value_load(flag[0:1, 0:1], min_val=0, max_val=E)
            with dve.If(total < E):
                glink = Link(dve, S["gcnt_link"])
                with dve.Fori(0, WN) as w:
                    for v, o in ((efa, key), (ef[:, 1, :], tk)):
                        last = V_.tensor_scalar(o[:, 0:FULL], v[:, PADC:PADC + FULL], wfirst[:, bass.ds(w, 1)], None, ALU.subtract)
                    glink(last, base=w * 5)
                    glink(outside(key[:, 0:FULL], tk[:, 0:FULL], glink, base=w * 5), base=w * 5)

                    def one_hots(g):
                        for j in range(NB):
                            dve.wait_ge(S["gcnt_oh_used"], w * FULL + g * NB + (j + 1))
                            V_.tensor_scalar(ohm[:, j, :], iota16[:, 0:P], ef[:, 0, bass.ds(g * NB + (PADC + j), 1)], None, ALU.is_equal)
                            V_.tensor_scalar(ohs[:, j, :], iota16[:, 0:WK], key[:, bass.ds(g * NB + j, 1)],
                                             None, ALU.is_equal).then_inc(S["gcnt_oh_ready"], 1)

                    one_hots(0)
                    with dve.Fori(1, FULL // NB) as g:
                        one_hots(g)
                    dve.wait_ge(S["gcnt_hi"], w + 1)
                    V_.tensor_tensor(AT[1][:, :, bass.ds(w * WT, WT)], ps[:, 4, 0:WK].rearrange("p (a n) -> p a n", a=NT),
                                     AT[0][:, :, bass.ds(w * WT, WT)], ALU.subtract).then_inc(S["gcnt_ready"], 1)
                dve.wait_ge(S["deg_mm"], 2)
            V_.tensor_scalar(rdegB, psf[:, 0:N], 1.0, None, ALU.max).then_inc(S["rdeg_ready"], 1)
            dve.wait_ge(S["rdeg_ready"], 1)
            V_.reciprocal(rdegB, rdegB).then_inc(S["rdeg_ready"], 1)
            dve.wait_ge(S["rdeg_ready"], 2)
            for c, (c0, c1) in enumerate(COLS):
                cn = c1 - c0
                for k in range(KD):
                    dve.wait_ge(S["agg_mm"], c * KD + k + 1)
                    if c >= 1 and k == 0:
                        dve.wait_ge(S["conv_mm"], c * KD)
                    V_.tensor_tensor(aggT[:, k, 0:cn], ps[:, 3 + k, 0:cn], rdegB[:, c0:c1], ALU.mult).then_inc(S["agg_ready"], 1)
                for fo in range(KD):
                    n = c * KD + fo
                    dve.wait_ge(S["rl_ready"], n + 1)
                    a0 = SEQ if c == 0 else 0
                    if c == 0:
                        dve.wait_ge(S["hatt_ready"], 2)
                        link(V_.tensor_tensor(rl[:, n % 2, 0:SEQ], rl[:, n % 2, 0:SEQ], hatt[:, fo, :], ALU.add))
                        V_.tensor_tensor(tA[:, fo, 0:SEQ], rl[:, n % 2, 0:SEQ], tA[:, fo, 0:SEQ], ALU.add)
                    V_.scalar_tensor_tensor(tA[:, fo, c0 + a0:c1], rl[:, n % 2, a0:cn], hatt[:, fo, SEQ - 1:SEQ],
                                            tA[:, fo, c0 + a0:c1], ALU.add, ALU.add).then_inc(S["z_ready"], 1)
            dve.wait_ge(S["z_ready"], 3 * KD)
            batch_norm_affine(2, 2 * KD, 3 * KD)
            for k in range(KD):
                V_.tensor_scalar(tA[:, k, :], tA[:, k, :], ab[:, 1, k:k + 1], ab[:, 2, k:k + 1],
                                 ALU.mult, ALU.add).then_inc(S["w_ready"], 1)
            for t in range(NT):
                dve.wait_ge(S["w_T"], t + 1)
                last = V_.tensor_tensor(xr[0:sz(t), t, :], xr[0:sz(t), t, :], ps[0:sz(t), t % 2, :], ALU.add)
                last.then_inc(S["x1_ready"], 1)
            dve.wait_ge(S["x1_ready"], NT)
            layer_norm_stats(xr, 2)
            for t in range(NT):
                last = V_.tensor_scalar(r2[0:sz(t), t, :], xr[0:sz(t), t, :], mv[0:sz(t), t, 0:1], rs[0:sz(t), t:t + 1],
                                        ALU.subtract, ALU.mult)
            link(last)
            layer_norm_stats(r2, 3)
            for t in range(NT):
                V_.tensor_scalar(nrow[0:sz(t), t, :], r2[0:sz(t), t, :], mv[0:sz(t), t, 0:1], rs[0:sz(t), t:t + 1],
                                 ALU.subtract, ALU.mult).then_inc(S["n1_ready"], 1)
            dve.wait_ge(S["n1T_raw"], NT)
            for k in range(KD):
                V_.tensor_scalar(tA[:, k, :], tA[:, k, :], par[:, 5 * KD + k:5 * KD + k + 1], par[:, 6 * KD + k:6 * KD + k + 1],
                                 ALU.mult, ALU.add).then_inc(S["x1T_ready"], 1)

            with dve.Fori(0, PAIRS) as pr:
                dve.wait_ge(S["proj_done"], pr + 2)
                V_.tensor_copy(KT, psf[:, 1536:1536 + N]).then_inc(S["qkv_dve"], 1)
                V_.tensor_copy(V[:, 4:8, :], ps[:, 7, :].rearrange("p (t c) -> p t c", t=4)).then_inc(S["qkv_dve"], 1)

                def neg_max(i):
                    qt = sz(i // 2)
                    dve.wait_ge(S["s_mm"], pr * U + (i + 1))
                    if i >= 2:
                        dve.wait_ge(S["exp_done"], pr * U + (i - 1))
                    V_.tensor_reduce(nmx[0:qt, i % 2:i % 2 + 1], psf[0:qt, 1536 * (i % 2):1536 * (i % 2) + N], AXX, ALU.max,
                                     negate=True).then_inc(S["negmax"], 1)

                def last_bank(i):
                    dve.wait_ge(S["p_T"], pr * PTS + (3 * i + 3 if i < U else 2 * U + i + 1))
                    bank = 6 + (3 * i + 2 if i < U else 2 * U + i) % 2
                    last = None
                    if i < U:
                        qt = sz(i // 2)
                        V_.tensor_copy(PT[:, i % 2, 8, 0:qt], ps[:, bank, 0:qt])
                        last = V_.tensor_copy(PT[0:TAIL, i % 2, 9, 0:qt], ps[0:TAIL, bank, P:P + qt])
                    if 1 <= i <= U:
                        n = i - 1
                        qt = sz(n // 2)
                        dve.wait_ge(S["loop_link"], pr * U + i)
                        last = V_.tensor_scalar(arow[0:qt, (n // 2) % 2, (n % 2) * DH:(n % 2 + 1) * DH],
                                                ps[0:qt, bank, 256:256 + DH], resum[0:qt, n % 4:n % 4 + 1], None, ALU.mult)
                    if i >= 3 and i % 2:
                        t = (i - 3) // 2
                        last = V_.tensor_copy(attnT[:, bass.ds(pr, 1), t * P:t * P + sz(t)].rearrange("p a n -> p (a n)"),
                                              ps[:, bank, 320:320 + sz(t)])
                    last.then_inc(S["pt_dve"], 1)

                neg_max(0)
                neg_max(1)
                for i in range(U + 3):
                    if i >= 1:
                        last_bank(i - 1)
                    if i < U:
                        qt = sz(i // 2)
                        dve.wait_ge(S["p_T"], pr * PTS + (3 * i + 1))
                        V_.tensor_copy(PT[:, i % 2, 0:4, 0:qt],
                                       ps[:, 6 + i % 2, :].rearrange("p (t c) -> p t c", t=4)[:, :, 0:qt]).then_inc(S["pt_dve"], 1)
                        dve.wait_ge(S["exp_done"], pr * U + (i + 1))
                        V_.reciprocal(resum[0:qt, i % 4:i % 4 + 1], esum[0:qt, i % 2:i % 2 + 1]).then_inc(S["loop_link"], 1)
                    if i + 2 < U:
                        neg_max(i + 2)

            for t in range(NT):
                dve.wait_ge(S["wo_mm"], t + 1)
                last = V_.tensor_tensor(r2[0:sz(t), t, :], r2[0:sz(t), t, :], ps[0:sz(t), t % 2, :], ALU.add)
                last.then_inc(S["xx_ready"], 1)
            dve.wait_ge(S["xx_ready"], NT)
            layer_norm_stats(r2, 4)
            dve.wait_ge(S["ln2_in"], 32)
            for t in range(NT):
                n = nrow[0:sz(t), t, :]
                link(V_.tensor_scalar(n, r2[0:sz(t), t, :], mv[0:sz(t), t, 0:1], rs[0:sz(t), t:t + 1],
                                      ALU.subtract, ALU.mult))
                link(V_.tensor_tensor(n, n, g2row[0:sz(t), 0, :], ALU.mult))
                V_.tensor_tensor(n, n, g2row[0:sz(t), 1, :], ALU.add).then_inc(S["x2_ready"], 1)
            dve.wait_ge(S["lg_mm"], NT)
            link(V_.memset(lg[:, NT - 1, :], 0.0))
            V_.tensor_copy(lg[:, 0:8, :], ps[:, 4, :].rearrange("p (t e) -> p t e", t=8))
            V_.tensor_copy(lg[:, 8, :], ps[:, 5, 0:NEXP])
            link(V_.tensor_copy(lg[0:TAIL, 9, :], ps[0:TAIL, 5, NEXP:2 * NEXP]))
            for t in range(NT):
                last = V_.max(v8[:, t, :], lg[:, t, :])
            link(last)
            for t in range(NT):
                V_.max_index(i8[:, t, :], v8[:, t, :], lg[:, t, :])
                last = V_.tensor_scalar(ex[:, t, :], lg[:, t, :], v8[:, t, 0:1], None, ALU.subtract)
                last = V_.tensor_scalar(gk[:, 0, t, :], v8[:, t, 0:2], v8[:, t, 0:1], None, ALU.subtract)
            last.then_inc(S["exs_ready"], 1)
            dve.wait_ge(S["exs_ready"], 1)
            link(V_.tensor_copy(gk[:, 1, :, :], i8[:, :, 0:2]))
            for t in range(NT):
                for k in range(2):
                    last = V_.tensor_scalar(ohk[k][:, t, :], iota64[:, :], gk[:, 1, t, k:k + 1], None, ALU.is_equal)
            link(last)
            V_.tensor_tensor(O, ohk[0], ohk[1], ALU.add).then_inc(S["O_ready"], 1)
            dve.wait_ge(S["exp_ready"], 1)
            link(V_.tensor_reduce(ssum[:, :], ex, AXX, ALU.add))
            link(V_.reciprocal(ssum[:, :], ssum[:, :]))
            for k in range(2):
                last = V_.tensor_tensor(gk[:, 2, :, k], gk[:, 0, :, k], ssum[:, :], ALU.mult)
            link(last)
            link(V_.tensor_tensor(gk[:, 3, :, 0], gk[:, 2, :, 0], gk[:, 2, :, 1], ALU.add))
            link(V_.reciprocal(gk[:, 3, :, 0], gk[:, 3, :, 0]))
            for k in range(2):
                last = V_.tensor_tensor(gk[:, 4, :, k], gk[:, 2, :, k], gk[:, 3, :, 0], ALU.mult)
            link(last)
            dve.wait_ge(S["pos_mm"], 1)
            V_.tensor_copy(posm[:, 0:8, :], ps[:, 6, :].rearrange("p (t e) -> p t e", t=8))
            V_.tensor_copy(posm[:, 8, :], ps[:, 7, 0:NEXP])
            link(V_.tensor_copy(posm[:, 9, :], ps[:, 7, NEXP:2 * NEXP]))
            for k in range(2):
                link(V_.tensor_tensor(tmp, posm, ohk[k], ALU.mult))
                link(V_.tensor_reduce(gk[:, 5, :, k], tmp, AXX, ALU.add))
            link(V_.tensor_scalar(gk[:, 6, :, :], gk[:, 5, :, :], float(CAP), None, ALU.is_lt))
            link(V_.tensor_scalar(gk[:, 5, :, :], gk[:, 5, :, :], float(CAP - 1), None, ALU.min))
            link(V_.scalar_tensor_tensor(gk[:, 5, :, :], gk[:, 1, :, :], float(CAP), gk[:, 5, :, :], ALU.mult, ALU.add))
            link(V_.tensor_copy(slot_i[:, :, :], gk[:, 5, :, :]))
            link(V_.tensor_scalar(gk[:, 7, :, :], gk[:, 6, :, :], -65536.0, 65536.0, ALU.mult, ALU.add))
            link(V_.tensor_tensor(gk[:, 7, :, :], gk[:, 7, :, :], gk[:, 5, :, :], ALU.add))
            V_.tensor_copy(sidx_i[:, :, :], gk[:, 7, :, :]).then_inc(S["idx_ready"], 1)
            link(V_.tensor_tensor(gk[:, 4, :, :], gk[:, 4, :, :], gk[:, 6, :, :], ALU.mult))
            for t in range(NT):
                last = V_.tensor_scalar(tmp[:, t, :], ohk[0][:, t, :], gk[:, 4, t, 0:1], None, ALU.mult)
            link(last)
            for t in range(NT):
                last = V_.scalar_tensor_tensor(G[:, t, :], ohk[1][:, t, :], gk[:, 4, t, 1:2], tmp[:, t, :], ALU.mult, ALU.add)
            last.then_inc(S["G_ready"], 1)
            dve.wait_ge(S["tab_in"], 16)
            V_.tensor_copy(tabf[:, :], tabr[:, :]).then_inc(S["tabf_ready"], 1)
            dve.wait_ge(S["tab_T"], 1)
            V_.tensor_copy(tabT[:, :], ps[0:CAP, 3, 0:NEXP]).then_inc(S["tabT_ready"], 1)

            def xT_copy(j, n):
                dve.wait_ge(S["xT_mm"], n)
                V_.tensor_copy(xT[:, j, :, :], ps[:, j, :].rearrange("p (k c) -> p k c", k=KD)[:, :, 0:CAP]).then_inc(S["xT_ready"], 1)

            def y_copy(j, n, stored):
                dve.wait_ge(S["l2_mm"], n + 2)
                dve.wait_ge(y_stored[j], stored)
                V_.tensor_copy(ys[0:CAP, j, :], ps[0:CAP, 4 + j, :]).then_inc(S["y_ready"], 1)

            xT_copy(0, 1)
            xT_copy(1, 2)
            with dve.Fori(0, NEXP // 2 - 1) as it:
                for j in range(2):
                    xT_copy(j, it * 2 + (j + 3))
                    y_copy(j, it * 2 + (j + 1), it * 16 + 16)
            for j in range(2):
                y_copy(j, NEXP - 1 + j, 16 * (NEXP // 2))
            for t in range(NT):
                last = V_.tensor_tensor(xr[0:sz(t), t, :], xr[0:sz(t), t, :], r2[0:sz(t), t, :], ALU.add)
            link(last)
            for t in range(NT):
                dve.wait_ge(S["b2_mm"], t + 1)
                xo = xr[0:sz(t), t, :]
                link(V_.tensor_tensor(xo, xo, ps[0:sz(t), 6 + t % 2, :], ALU.add))
                for k in range(2):
                    n = t * 2 + k
                    dve.wait_ge(yg_in[n % 4], 16 * (n // 4 + 1))
                    last = V_.scalar_tensor_tensor(xo, ygat[0:sz(t), n % 4, :], gk[0:sz(t), 4, t, k:k + 1], xo, ALU.mult, ALU.add)
                    if k == 0:
                        link(last)
                last.then_inc(S["acc_ready"], 1)

        @block.tensor
        def _(pe):
            mm, tr = nc.tensor.matmul, nc.tensor.transpose
            pe.sem_inc(S["oh_used"], CREDIT)
            pe.sem_inc(S["proj_done"], 1)
            pe.sem_inc(S["pt_dve"], 1)
            pe.sem_inc(S["cnt_ready"], 4)
            pe.sem_inc(S["gcnt_ready"], 1)
            pe.sem_inc(S["gcnt_oh_used"], NB)
            pe.sem_inc(S["l2_mm"], 2)
            pe.sem_inc(S["y_ready"], 2)
            pe.sem_inc(y_stored[0], 16)
            pe.sem_inc(y_stored[1], 16)
            pe.wait_ge(S["consts"], 2)
            pe.wait_ge(S["raw_ready"], 1)
            for s in range(2):
                for b in range(3):
                    tr(ps[:, s, b * P:(b + 1) * P], er_f[:, s, b, :], identf[:, :])
                last = tr(ps[:, s, 384:385], er_f[0:1, s, 3, :], identf[0:1, 0:1])
            last.then_inc(S["raw_T"], 1)
            pe.wait_ge(S["params_in"], 160)
            tr(ps[:, 4, 0:28], prow[:, :], identf[0:28, 0:28])
            tr(ps[:, 4, 128:256], b1r[:, :], identf[:, :])
            for t in range(2):
                last = tr(ps[:, 5, t * P:(t + 1) * P], pj[:, t, :, :].rearrange("p a d -> p (a d)"), identf[:, :])
            last.then_inc(S["par_T"], 1)

            def rows_to_T(rows, ready, done, freed, bank):
                for t in range(NT):
                    pe.wait_ge(S[ready], t + 1)
                    if t >= 2:
                        pe.wait_ge(S[freed], t - 1)
                    for k in range(KD):
                        last = tr(ps[:, bank + t % 2, k * P:k * P + sz(t)], rows[0:sz(t), t, k * P:(k + 1) * P],
                                  identf[0:sz(t), 0:sz(t)])
                    last.then_inc(S[done], 1)

            def T_to_rows(cols, done, freed, bank):
                for t in range(NT):
                    if t >= 2:
                        pe.wait_ge(S[freed], t - 1)
                    for k in range(KD):
                        last = tr(ps[0:sz(t), bank + t % 2, k * P:(k + 1) * P], cols(k, t), identf[:, :])
                    last.then_inc(S[done], 1)

            rows_to_T(r2, "h_ready", "h_T", "hT_ready", 2)
            pe.wait_ge(S["xnT_ready"], KD)
            pe.wait_ge(S["hT_ready"], NT)
            T_to_rows(lambda k, t: tB[:, k * N + t * P:k * N + t * P + sz(t)], "xn_T", "xn_ready", 2)

            pe.wait_ge(S["ef_ready"], 1)
            pe.wait_ge(S["par_ready"], 1)
            pe.wait_ge(S["gw_in"], 64)
            pe.wait_ge(S["xn_ready"], NT)
            for p in range(PAIRS):
                if p >= 2:
                    pe.wait_ge(S["qk_ready"], p - 1)
                for s in range(2):
                    for k in range(KD):
                        last = mm(ps[:, p % 2, s * SEQ:(s + 1) * SEQ], gw[s][:, k, p * P:(p + 1) * P], tA[:, k, 0:SEQ],
                                  start=(k == 0), stop=(k == KD - 1))
                last.then_inc(S["qk_mm"], 1)
            for nt in range(NQ):
                for k in range(KD):
                    last = mm(ps[:, 2 + nt, :], tA[:, k, nt * P:(nt + 1) * P], gw[2][:, k, :], start=(k == 0), stop=(k == KD - 1))
                last.then_inc(S["v_mm"], 1)
            pe.wait_ge(S["sq_ready"], 1)
            for s in range(2):
                for nt in range(NQ):
                    for p in range(PAIRS):
                        c = (s * NQ + nt) * HEADS + 2 * p
                        last = mm(ps[:, 4, c:c + 2], sq[:, s, p, nt * P:(nt + 1) * P], halfblk[:, :], start=True, stop=True)
            last.then_inc(S["dg_mm"], 1)
            for u in range(2 * NQ * PAIRS):
                s, r = divmod(u, NQ * PAIRS)
                nt, p = divmod(r, PAIRS)
                if u >= 3:
                    v = u - 3
                    if v < NQ * PAIRS:
                        pe.wait_ge(S["uk_copied"], v + 1)
                    else:
                        pe.wait_ge(S["uq_exp"], 2 * (v - NQ * PAIRS + 1))
                mm(ps[:, 5 + u % 3, :], qk[:, 1 - s, p, nt * P:(nt + 1) * P], projblk.rearrange("p a m -> p (a m)"),
                   start=True, stop=True).then_inc(S["u_mm"], 1)
            pe.wait_ge(S["v_ready"], NQ)
            pe.wait_ge(S["kf_ready"], 1)
            for h in range(HEADS):
                for m in range(M // P):
                    c = ((h % 2) * 2 + m) * P
                    for nt in range(NQ):
                        last = mm(ps[:, h // 2, c:c + DH + 1], kf[:, nt, h, m * P:(m + 1) * P], vaug[:, nt, h, :],
                                  start=(nt == 0), stop=(nt == NQ - 1))
                if h % 2:
                    last.then_inc(S["kv_mm"], 1)
            pe.wait_ge(S["qf_ready"], 1)

            def q_features_T(h):
                if h >= 2:
                    pe.wait_ge(S["qfT_ready"], h - 1)
                for m in range(M // P):
                    for nt in range(NQ):
                        last = tr(ps[:, 4 + h % 2, m * SEQ + nt * P:m * SEQ + (nt + 1) * P], qf[:, nt, h, m * P:(m + 1) * P],
                                  identf[:, :])
                last.then_inc(S["qfT_mm"], 1)

            pe.wait_ge(S["uq_exp"], 2 * NQ * PAIRS)
            q_features_T(0)
            for h in range(HEADS):
                if h + 1 < HEADS:
                    q_features_T(h + 1)
                pe.wait_ge(S["qfT_ready"], h + 1)
                pe.wait_ge(S["kv_ready"], h // 2 + 1)
                if h >= 2:
                    pe.wait_ge(S["ga_ready"], h - 1)
                for nt in range(NQ):
                    for m in range(M // P):
                        last = mm(ps[:, 6 + h % 2, nt * P:nt * P + DH + 1], qfT[:, h % 2, m, nt * P:(nt + 1) * P], kv[:, h, m, :],
                                  start=(m == 0), stop=(m == M // P - 1))
                last.then_inc(S["ga_mm"], 1)
            pe.wait_ge(S["kv_ready"], 4)
            pe.wait_ge(S["ga_ready"], HEADS)
            for k in range(KD):
                for nt in range(NQ):
                    last = tr(ps[:, k // 2, (k % 2) * SEQ + nt * P:(k % 2) * SEQ + (nt + 1) * P], attnrow[:, nt, k * P:(k + 1) * P],
                              identf[:, :])
                if k % 2:
                    last.then_inc(S["ga_T"], 1)
            pe.wait_ge(S["gaT_ready"], 2)
            for fo in range(KD):
                for k in range(KD):
                    last = mm(ps[:, 2 + fo // 2, (fo % 2) * SEQ:(fo % 2 + 1) * SEQ], gw[3][:, k, fo * P:(fo + 1) * P],
                              attnTg[:, k, :], start=(k == 0), stop=(k == KD - 1))
                if fo % 2:
                    last.then_inc(S["ho_mm"], 1)
            pe.wait_ge(S["hatt_ready"], 2)

            def window(odd, block, g0, w0, wv):
                pe.wait_ge(S["cnt_ready"], wv + 1)
                for i in range(WIN):
                    j = i + ODD * odd
                    if not odd or j >= WIN:
                        pe.wait_ge(S["ohm_ready"], g0 + (j + 1))
                    pe.wait_ge(S["oh_ready"], w0 + (i + 1))
                    mm(ps[:, 4 + 2 * block + odd, 0:WK], ohm[:, (block * PAIRC + j) % (2 * PAIRC), :], ohs[:, i % NB, :],
                       start=(i == 0), stop=(i == WIN - 1)).then_inc(S["oh_used"], 1)

            with pe.Fori(0, WN // 4) as it:
                for w in range(4):
                    window(w % 2, w // 2, it * (2 * PAIRC) + (w // 2) * PAIRC, it * (4 * WIN) + w * WIN, it * 4 + w)
            window(0, 0, (WN // 2) * PAIRC, (WN - 1) * WIN, WN - 1)

            def degrees(parts):
                for c0, c1 in COLS:
                    n = len(parts) * NT
                    for i in range(n):
                        last = mm(ps[:, c0 // 512, 0:c1 - c0], onesb[:, :], parts[i // NT][:, i % NT, c0:c1],
                                  start=(i == 0), stop=(i == n - 1))
                last.then_inc(S["deg_mm"], 1)

            pe.wait_ge(S["cnt_ready"], WN + 4)
            degrees(AT[0:1])
            pe.wait_ge(S["flag_ready"], 1)
            total = pe.value_load(flag[0:1, 0:1], min_val=0, max_val=E)

            def aggregate(parts):
                steps = [(a, x, kt) for a in parts for x in xs for kt in range(NT)]
                for c, (c0, c1) in enumerate(COLS):
                    cn = c1 - c0
                    for k in range(KD):
                        if c >= 1:
                            pe.wait_ge(S["agg_ready"], (c - 1) * KD + k + 1)
                        for i, (a, x, kt) in enumerate(steps):
                            last = mm(ps[:, 3 + k, 0:cn], x[0:sz(kt), kt, k * P:(k + 1) * P], a[0:sz(kt), kt, c0:c1],
                                      start=(i == 0), stop=(i == len(steps) - 1))
                        last.then_inc(S["agg_mm"], 1)
                    pe.wait_ge(S["agg_ready"], (c + 1) * KD)
                    for fo in range(KD):
                        n = c * KD + fo
                        if n >= 2:
                            pe.wait_ge(S["rl_ready"], n - 1)
                        for k in range(KD):
                            last = mm(ps[:, 7 - 7 * (n % 2), 0:cn], wc[:, k, fo * P:(fo + 1) * P], aggT[:, k, 0:cn],
                                      start=(k == 0), stop=(k == KD - 1))
                        last.then_inc(S["conv_mm"], 1)

            pe.wait_ge(S["xs_ready"], NT)
            pe.wait_ge(S["wc_in"], 16)
            with pe.If(total >= E):
                aggregate(AT[0:1])
            with pe.If(total < E):
                with pe.Fori(0, WN) as w:
                    pe.wait_ge(S["gcnt_ready"], w + 1)

                    def group(done, first=False, final=False):
                        for j in range(NB):
                            pe.wait_ge(S["gcnt_oh_ready"], done + (j + 1))
                            mm(ps[:, 4, 0:WK], ohm[:, j, :], ohs[:, j, :], start=first and j == 0,
                               stop=final and j == NB - 1).then_inc(S["gcnt_oh_used"], 1)

                    start = w * FULL
                    group(start, first=True)
                    with pe.Fori(1, FULL // NB - 1) as g:
                        group(start + g * NB)
                    group(start + (FULL - NB), final=True)
                pe.wait_ge(S["gcnt_ready"], WN + 1)
                degrees(AT)
                aggregate(AT)
            pe.wait_ge(S["w_ready"], KD)
            T_to_rows(lambda k, t: tA[:, k, t * P:t * P + sz(t)], "w_T", "x1_ready", 0)
            rows_to_T(nrow, "n1_ready", "n1_T", "n1T_raw", 2)
            pe.wait_ge(S["x1T_ready"], KD)
            pe.wait_ge(S["rl_ready"], 3 * KD)

            pe.wait_ge(S["qpad_ready"], 1)
            with pe.Fori(0, PAIRS) as pr:
                pe.wait_ge(S["wst_in"], pr * 48 + 48)
                pe.wait_ge(S["pt_dve"], pr * (2 * U + 2) + 1)
                for i, b0 in ((0, 0), (1, 3)):
                    for c, (c0, c1) in enumerate(COLS):
                        for k in range(KD):
                            mm(ps[:, b0 + c, 0:c1 - c0], wst[:, i, k, :], tA[:, k, c0:c1], start=(k == 0), stop=(k == KD - 1))
                for t in range(NT):
                    bank, col = (6 + t // 4, (t % 4) * P) if t < 8 else (2, 256 + (t - 8) * P)
                    for k in range(KD):
                        last = mm(ps[0:sz(t), bank, col:col + P], tA[:, k, t * P:t * P + sz(t)], wst[:, 2, k, :],
                                  start=(k == 0), stop=(k == KD - 1))
                last.then_inc(S["proj_done"], 1)
                pe.wait_ge(S["qkv_act"], pr * 5 + 5)
                pe.wait_ge(S["qkv_dve"], pr * 2 + 2)

                def scores(i):
                    t, h = divmod(i, 2)
                    if i >= 2:
                        pe.wait_ge(S["exp_done"], pr * U + (i - 1))
                    for c, (c0, c1) in enumerate(COLS):
                        last = mm(ps[0:sz(t), 3 * (i % 2) + c, 0:c1 - c0], QT[:, h, t * P:t * P + sz(t)], KT[:, c0:c1], start=True, stop=True)
                    last.then_inc(S["s_mm"], 1)

                def bank_free(n):
                    n -= 2
                    if n >= 0:
                        m, r = divmod(n, 3)
                        if n >= 3 * U:
                            pe.wait_ge(S["pt_dve"], pr * (2 * U + 2) + (2 * U + 2 + n - 3 * U))
                        elif r == 1:
                            pe.wait_ge(S["pt_act"], pr * U + (m + 1))
                        else:
                            pe.wait_ge(S["pt_dve"], pr * (2 * U + 2) + (2 * m + r // 2 + 2))

                def weights_T(i, parts):
                    t = i // 2
                    if i < U:
                        pe.wait_ge(S["exp_done"], pr * U + (i + 1))
                    for g in parts:
                        n = 3 * i + g if i < U else 2 * U + i
                        bank_free(n)
                        if i < U:
                            for kt in range(4 * g, min(4 * g + 4, NT)):
                                last = tr(ps[0:sz(kt), 6 + n % 2, (kt % 4) * P:(kt % 4) * P + sz(t)],
                                          Pb[0:sz(t), i % 2, kt * P:kt * P + sz(kt)], identf[0:sz(t), 0:sz(t)])
                        if g == 2 and 1 <= i <= U:
                            m, h = divmod(i - 1, 2)
                            pe.wait_ge(S["pt_dve"], pr * (2 * U + 2) + (2 * i + 1))
                            pe.wait_ge(S["pt_act"], pr * U + i)
                            for kt in range(NT):
                                last = mm(ps[0:sz(m), 6 + n % 2, 256:256 + DH], PT[0:sz(kt), (i - 1) % 2, kt, 0:sz(m)],
                                          V[0:sz(kt), kt, h * DH:(h + 1) * DH], start=(kt == 0), stop=(kt == NT - 1))
                        if g == 2 and i >= 3 and i % 2:
                            r = (i - 3) // 2
                            pe.wait_ge(S["pt_dve"], pr * (2 * U + 2) + (2 * i + 1 if i <= U else 2 * U + 2))
                            last = tr(ps[:, 6 + n % 2, 320:320 + sz(r)], arow[0:sz(r), r % 2, :], identf[0:sz(r), 0:sz(r)])
                        last.then_inc(S["p_T"], 1)

                scores(0)
                scores(1)
                for i in range(U + 2):
                    if i < U:
                        weights_T(i, (0,))
                    if i + 2 < U:
                        scores(i + 2)
                    weights_T(i, (1, 2) if i < U else (2,))

            pe.wait_ge(S["wo_in"], 16)
            pe.wait_ge(S["pt_dve"], PAIRS * (2 * U + 2) + 1)
            for t in range(NT):
                if t >= 2:
                    pe.wait_ge(S["xx_ready"], t - 1)
                for k in range(KD):
                    last = mm(ps[0:sz(t), t % 2, :], attnT[:, k, t * P:t * P + sz(t)], wo_s[:, k, :],
                              start=(k == 0), stop=(k == KD - 1))
                last.then_inc(S["wo_mm"], 1)
            pe.wait_ge(S["route_in"], 32)
            for t in range(NT + 1):
                if t < NT:
                    pe.wait_ge(S["x2_ready"], t + 1)
                    if t >= 2:
                        pe.wait_ge(S["x2T_ready"], t - 1)
                    for k in range(KD):
                        last = tr(ps[:, 2 + t % 2, k * P:k * P + sz(t)], nrow[0:sz(t), t, k * P:(k + 1) * P],
                                  identf[0:sz(t), 0:sz(t)])
                    last.then_inc(S["x2_T"], 1)
                if t >= 1:
                    r = t - 1
                    pe.wait_ge(S["x2T_ready"], r + 1)
                    for k in range(KD):
                        last = mm(ps[0:sz(r), 4 + r // 8, (r % 8) * NEXP:(r % 8 + 1) * NEXP], x2T[:, r % 2, k, 0:sz(r)],
                                  wr_s[:, k, :], start=(k == 0), stop=(k == KD - 1))
                    last.then_inc(S["lg_mm"], 1)
            pe.wait_ge(S["O_ready"], 1)
            for t in range(NT):
                o = ps[:, 6 + t // 8, (t % 8) * NEXP:(t % 8 + 1) * NEXP]
                for r in range(t):
                    mm(o, onesb[:, :], O[:, r, :], start=(r == 0), stop=False)
                last = mm(o, tri[:, :], O[:, t, :], start=(t == 0), stop=True)
            last.then_inc(S["pos_mm"], 1)
            pe.wait_ge(S["G_ready"], 1)
            for t in range(NT):
                last = tr(ps[0:NEXP, t // 4, (t % 4) * P:(t % 4) * P + sz(t)], G[0:sz(t), t, :], identf[0:sz(t), 0:sz(t)])
                if t % 4 == 3 or t == NT - 1:
                    last.then_inc(S["G_T"], 1)
            pe.wait_ge(S["tabf_ready"], 1)
            tr(ps[0:CAP, 3, 0:NEXP], tabf[:, :], identf[0:NEXP, 0:NEXP]).then_inc(S["tab_T"], 1)
            pe.wait_ge(S["GT_ready"], 3)
            pe.wait_ge(S["tabT_ready"], 1)


            def gathered_T(j, arrived, jj):
                pe.wait_ge(xb_in[j], arrived)
                for k in range(KD):
                    last = tr(ps[:, jj, k * P:k * P + CAP], xb[0:CAP, j, k * P:(k + 1) * P], identf[0:CAP, 0:CAP])
                last.then_inc(S["xT_mm"], 1)

            def layer1(slot, arrived, n):
                pe.wait_ge(w_in[slot], arrived)
                pe.wait_ge(S["xT_ready"], n)
                for f in range(F // P):
                    for k in range(KD):
                        last = mm(ps[:, 2 + slot % 2, f * P:f * P + CAP], ring1[slot][:, k, f * P:(f + 1) * P], xT[:, slot % 2, k, :],
                                  start=(k == 0), stop=(k == KD - 1))
                last.then_inc(S["l1_mm"], 1)

            def layer2(slot, n):
                pe.wait_ge(S["gelu_done"], n)
                for f in range(F // P):
                    last = mm(ps[0:CAP, 4 + slot % 2, :], hT[:, slot % 2, f, :], ring2[slot][:, f, :],
                              start=(f == 0), stop=(f == F // P - 1))
                last.then_inc(S["l2_mm"], 1)

            gathered_T(0, 16, 0)
            layer1(0, 32, 1)
            gathered_T(1, 16, 1)
            with pe.Fori(0, NEXP // RW - 1) as it:
                for j in range(RW):
                    layer1((j + 1) % RW, it * 32 + (32 if j + 1 < RW else 64), it * RW + (j + 2))
                    gathered_T((j + 2) % XB, it * 32 + 16 * ((j + 2) // XB + 1), j % 2)
                    pe.wait_ge(S["y_ready"], it * RW + (j + 1))
                    layer2(j, it * RW + (j + 1))
            for s in range(NEXP - RW, NEXP):
                if s + 1 < NEXP:
                    layer1((s + 1) % RW, 32 * ((s + 1) // RW + 1), s + 2)
                if s + 2 < NEXP:
                    gathered_T((s + 2) % XB, 16 * ((s + 2) // XB + 1), s % 2)
                pe.wait_ge(S["y_ready"], s + 1)
                layer2(s % RW, s + 1)
            for t in range(NT):
                if t >= 2:
                    pe.wait_ge(S["acc_ready"], t - 1)
                mm(ps[0:sz(t), 6 + t % 2, :], GT[:, t * P:t * P + sz(t)], b2_s[:, :], start=True, stop=True).then_inc(S["b2_mm"], 1)


_INS = ["x", "src", "dst", "L0_gnn_norm1_g", "L0_gnn_norm1_b", "L0_gnn_norm2_g", "L0_gnn_norm2_b", "L0_gnn_W_conv",
        "L0_gnn_b_conv", "L0_gnn_Wq", "L0_gnn_Wk", "L0_gnn_Wv", "L0_gnn_Wo", "L0_gnn_proj", "L0_ffn_ln1_g", "L0_ffn_ln1_b",
        "L0_ffn_wq", "L0_ffn_wk", "L0_ffn_wv", "L0_ffn_wo", "L0_ffn_ln2_g", "L0_ffn_ln2_b", "L0_ffn_wr", "L0_ffn_w1",
        "L0_ffn_b1", "L0_ffn_w2", "L0_ffn_b2"]


def kernel(**inputs):
    import numpy as _np
    import concourse.bacc as _bacc
    from concourse import mybir as _mybir
    from concourse.bass_utils import run_bass_kernel_spmd as _run

    nc = _bacc.Bacc("TRN2", target_bir_lowering=False, num_devices=1)
    arrays, args = {}, []
    for name in _INS:
        a = _np.ascontiguousarray(inputs[name])
        arrays[f"in_{name}"] = a
        args.append(nc.dram_tensor(f"in_{name}", a.shape, _mybir.dt.from_np(a.dtype), kind="ExternalInput").ap())
    args.append(nc.dram_tensor("out_0", (1250, 512), _mybir.dt.float32, kind="ExternalOutput").ap())
    build(nc, *args)
    r = _run(nc, [arrays], core_ids=[0])
    return r.results[0]["out_0"]
```

```python
import numpy as np
import concourse.bass as bass
from concourse import mybir
from contextlib import ExitStack


class Link:

    def __init__(self, eng, sem):
        self.eng, self.sem, self.n = eng, sem, 0

    def __call__(self, ins, base=0):
        self.n += 1
        ins.then_inc(self.sem, 1)
        self.eng.wait_ge(self.sem, base + self.n)


def build(nc, x, src, dst, n1g, n1b, n2g, n2b, w_conv, b_conv, gwq, gwk, gwv, gwo, proj,
          l1g, l1b, fwq, fwk, fwv, fwo, l2g, l2b, wr, w1, b1, w2, b2, out):
    f32, bf16, f16 = mybir.dt.float32, mybir.dt.bfloat16, mybir.dt.float16
    i32, u32 = mybir.dt.int32, mybir.dt.uint32
    ALU, ACT = mybir.AluOpType, mybir.ActivationFunctionType
    AXX = mybir.AxisListType.X
    RMAX = bass.bass_isa.ReduceOp.max

    P = 128
    N, D = x.shape
    E = src.shape[0]
    KD = D // P
    NT = -(-N // P)
    TAIL = N - (NT - 1) * P

    def sz(t):
        return P if t < NT - 1 else TAIL

    HEADS = 8
    DH = D // HEADS
    PAIRS = HEADS // 2
    M = proj.shape[0]
    SEQ = 256
    NQ = SEQ // P
    WO_BANKS = (0, 1, 6, 7)
    EPS, KEPS = 1e-5, 1e-6
    NEXP, _, F = w1.shape
    TOPK, CAP = 2, 2 * (N * 2 // NEXP)
    EMPTY = 65536
    BN = [(0, 417), (417, 834), (834, N)]
    COLS = [(c, min(c + 512, N)) for c in range(0, N, 512)]

    ROWS = E // P
    LEFT = E - ROWS * P
    PADC = 4
    WT = 50
    WN = N // WT
    WK = NT * WT
    WIN = 18
    PAIRC = 2 * WT * E // N // P
    FIRST = 3
    ODD = PAIRC // 2 + 1
    MG = 5
    ECOLS = PADC + 384
    NB = WIN
    NBG = 6
    CREDIT = 4 * WIN
    EXACT = 256
    U = 2 * NT
    PTS = 3 * U + 2
    FULL = 318

    NG = NT // 2

    def pair(g):
        return range(2 * g, 2 * g + 2)

    def turn(n, g):
        return (0, 1 + max(2 * g - 1, 0), 1 + min(2 * g + 2, 2 * NG - 1), 1 + 2 * NG + g)[n]

    ctx = ExitStack()
    with ctx:
        def sb(name, shape, dt=f32):
            return ctx.enter_context(nc.sbuf_tensor(name, shape, dt))

        def sem(name):
            return ctx.enter_context(nc.semaphore(name))

        xr = sb("xr", [P, NT, D])
        r2 = sb("r2", [P, NT, D])
        tA = sb("tA", [P, KD, N])
        tB = sb("tB", [P, 4 * N])
        arena = sb("arena", [P, 12500 + 8 * 2048])
        iota16 = sb("iota16", [P, 512], f16)
        identf = sb("identf", [P, P])
        tri = sb("tri", [P, P], bf16)
        onesb = sb("onesb", [P, P], bf16)
        onesf = sb("onesf", [P, 1])
        halfblk = sb("halfblk", [P, 2])
        iota64 = sb("iota64", [P, NEXP])
        choice = sb("choice", [P, NT, TOPK])
        par = sb("par", [P, 28])
        b1T = sb("b1T", [P, P])
        wr_s = sb("wr_s", [P, KD, NEXP])
        b2_s = sb("b2_s", [NEXP, D])
        st = sb("st", [P, NT, 6])
        mv = sb("mv", [P, NT, 2])
        rs = sb("rs", [P, NT])
        nmr = sb("nmr", [P, NT])
        bst = sb("bst", [P, KD, 3, 6])
        bmv = sb("bmv", [P, KD, 2])
        ab = sb("ab", [P, 3, KD])
        tot = sb("tot", [P, 2])
        flag = sb("flag", [1, 1], i32)
        v8 = sb("v8", [P, NT, 8])
        i8 = sb("i8", [P, NT, 8], u32)
        gk = sb("gk", [P, 8, NT, 2])
        ssum = sb("ssum", [P, NT])
        tabc = sb("tabc", [CAP, NEXP], i32)
        tabT = sb("tabT", [CAP, NEXP], i32)
        nmx = sb("nmx", [P, 2])
        esum = sb("esum", [P, 2])
        resum = sb("resum", [P, 4])
        arow = sb("arow", [P, 2, P])
        ps = ctx.enter_context(nc.psum_tensor("ps", [P, 8, 512], f32))
        psf = ps[:, :, :].rearrange("p b c -> p (b c)")

        def view(t, off, *dims):
            n = int(np.prod(dims))
            v = t[:, off:off + n]
            if len(dims) == 2:
                v = v.rearrange("p (a b) -> p a b", a=dims[0])
            if len(dims) == 3:
                v = v.rearrange("p (a b c) -> p a b c", a=dims[0], b=dims[1])
            return v

        er_i = arena[:, 0:1024].bitcast(i32).rearrange("p (s b c) -> p s b c", s=2, b=4)
        er_f = view(arena, 1024, 2, 4, P)
        pj = view(arena, 2048, 2, 2, DH)
        b1r = arena[:, 2304:2432]
        prow = arena[0:28, 2432:2560]
        projblk = view(arena, 11400, 2, M)
        qk = view(arena, 0, 2, PAIRS, SEQ)
        vaug = view(arena, 2048, NQ, HEADS, DH + 1)
        qf = view(arena, 3100, NQ, HEADS, M)
        kf = view(arena, 7200, NQ, HEADS, M)
        sq = view(arena, 7200, 2, PAIRS, SEQ)
        qfT = view(tB, 0, 2, M // P, SEQ)
        kv = view(tB, 1024, HEADS, M // P, DH + 1)
        attnrow = view(tB, 2064, NQ, D)
        attnTg = view(tB, 0, KD, SEQ)
        hatt = view(tB, 3088, KD, SEQ)
        dg = view(arena, 22400, 2, NQ, HEADS)
        mk = view(arena, 22440, NQ, HEADS)
        mk8 = arena[:, 22456:22464]
        gmk = arena[:, 22464:22472]
        bk = view(arena, 22472, NQ, HEADS)
        bq = view(arena, 22488, NQ, HEADS)
        zr = view(arena, 22504, 2, 2)
        gw = [view(arena, 12500 + 2048 * i, KD, D) for i in range(4)]
        AT = [arena[:, 6250 * i:6250 * i + 6250].bitcast(bf16).rearrange("p (a n) -> p a n", a=NT) for i in range(2)]
        xs = [arena[:, 12500 + 2560 * i:12500 + 2560 * (i + 1)].bitcast(bf16).rearrange("p (t d) -> p t d", t=NT) for i in range(3)]
        key = arena[:, 20692:20692 + WN * WIN]
        efa = arena[:, 21142:21142 + ECOLS]
        tk = arena[:, 21530:21530 + WN * WIN]
        wfirst = arena[:, 21980:21980 + WN]
        wc = view(arena, 22740, KD, D)
        ohm = arena[:, 24788:24788 + 2 * PAIRC * 64].bitcast(bf16).rearrange("p (b c) -> p b c", b=2 * PAIRC)
        rdegB = arena[:, 24788:24788 + N]
        ef = view(arena, 24788 + 2 * PAIRC * 64, 2, ECOLS)
        nm = arena[:, 22010:22010 + ECOLS]
        ei = [arena[:, 26788 + 400 * i:26788 + 400 * i + ECOLS].bitcast(i32) for i in range(3)]
        ohs = arena[:, 7200:7200 + NB * WK // 2].bitcast(bf16).rearrange("p (b c) -> p b c", b=NB)
        ohg = tB[:, 1536:1536 + NBG * WK // 2].bitcast(bf16).rearrange("p (b c) -> p b c", b=NBG)
        aggT = view(tB, 0, KD, 512)
        rl = view(tB, 2048, 2, 512)
        nrow = view(arena, 0, NT, D)
        QT = view(arena, 0, 2, N)
        KT = arena[:, 2500:2500 + N]
        V = view(arena, 3750, NT, P)
        Pb = view(arena, 5030, 2, N)
        PT = view(arena, 7530, 2, NT, P)
        wst = view(arena, 10090, 3, KD, P)
        g2row = view(arena, 9024, 2, D)
        wo_s = view(arena, 10090, KD, D)
        attnT = view(tB, 0, KD, N)
        x2T = view(arena, 5120, 2, KD, P)
        lg = view(arena, 6144, NT, NEXP)
        ex = view(arena, 6784, NT, NEXP)
        ohk = [view(arena, 7424 + 640 * k, NT, NEXP) for k in range(2)]
        O = arena[:, 8704:9024].bitcast(bf16).rearrange("p (t e) -> p t e", t=NT)
        posm = view(arena, 9024, NT, NEXP)
        tmp = view(arena, 9664, NT, NEXP)
        G = view(arena, 10304, NT, NEXP)
        GT = tB[0:NEXP, 0:N]
        pid = view(tB, N, 2 * NT, CAP)
        RW = 8
        ring = [view(arena, 12500 + 2048 * i, 2048) for i in range(RW)]
        ring1 = [r[:, 0:1024].rearrange("p (k f) -> p k f", k=KD) for r in ring]
        ring2 = [r[:, 1024:2048].rearrange("p (k f) -> p k f", k=F // P) for r in ring]
        tAf = tA[:, :, :].rearrange("p k n -> p (k n)")
        XB = 4
        xb = view(tAf, 0, XB, D)
        xT = view(tAf, 2048, 2, KD, CAP)
        hT = view(tAf, 2048 + 624, 2, F // P, CAP)
        ys = view(tAf, 2048 + 624 + 312, 2, D)
        YG = 4
        ygat = view(arena, 0, YG, TOPK, D)

        x2d = nc.dram_tensor("x2d", [N, D], f32).ap()
        yd = nc.dram_tensor("yd", [TOPK * N, D], f32).ap()

        names = """x_in edges_in params_in gw_in wc_in wst_in wo_in route_in ln2_in x2_out
            out_stored consts pool_link dve_link raw_ready raw_T ef_ready par_T par_ready
            var_ready sd_ready shift_ready y_rows h_ready h_T hT_ready bvar_ready bsd_ready xnT_ready xn_T xn_ready
            qk_mm qk_ready v_mm v_ready sq_ready dg_mm u_mm uk_copied uk_maxed uq_bias uq_exp mk_ready gmk_ready
            bk_ready kexp_done kf_ready qf_ready kv_mm kv_ready qfT_mm qfT_ready ga_mm ga_ready ga_T gaT_ready
            ho_mm hatt_ready wbase_ready abs_ready ohm_act ohm_dve oh_ready oh_used cnt_ready gcnt_oh_ready gcnt_oh_used gcnt_hi gcnt_link gcnt_ready
            xs_hi xs_rest xs_mid xs_ready deg_mm flag_ready rdeg_ready agg_mm agg_ready conv_mm rl_ready z_ready
            w_ready w_T x1_ready n1_ready n1_T n1T_raw x1T_ready qpad_ready proj_done
            q_mm k_mm qkv_act qkv_dve s_mm negmax exp_done p_T pt_dve pt_act
            wo_mm xx_ready x2_ready x2_T x2T_ready lg_mm lg_read exs_ready exp_ready O_ready pos_mm pid_ready tab_mm tabT_ready y_zeroed G_ready G_T GT_ready
            xT_mm xT_ready l1_mm gelu_done l2_mm y_ready
            b2_mm loop_link acc_ready""".split()
        S = {n: sem(n) for n in names}
        w_in = [sem(f"w_in{i}") for i in range(RW)]
        xb_in = [sem(f"xb_in{i}") for i in range(XB)]
        y_stored = [sem(f"y_stored{i}") for i in range(2)]
        yg_in = [sem(f"yg_in{i}") for i in range(4)]

        block = ctx.enter_context(nc.Block())

        @block.sync
        def _(sp):
            full = (NT - 1) * P
            sp.dma_start(xr[:, 0:NT - 1, :], x[0:full, :].rearrange("(t p) d -> p t d", p=P)).then_inc(S["x_in"], 16)
            sp.dma_start(xr[0:TAIL, NT - 1, :], x[full:N, :]).then_inc(S["x_in"], 16)
            for i, v in enumerate((src, dst)):
                rows = v[0:ROWS * P].rearrange("(r c) -> r c", c=P)
                sp.dma_start(er_i[:, i, 0:2, :], rows[0:2 * P, :].rearrange("(b p) c -> p b c", p=P)).then_inc(S["edges_in"], 16)
                sp.dma_start(er_i[0:ROWS - 2 * P, i, 2, :], rows[2 * P:ROWS, :]).then_inc(S["edges_in"], 16)
                sp.dma_start(er_i[0:1, i, 3, 0:LEFT], v[ROWS * P:E].rearrange("(a n) -> a n", a=1)).then_inc(S["edges_in"], 16)
            for i, v in enumerate((n1g, n1b, n2g, n2b, b_conv, l1g, l1b)):
                sp.dma_start(prow[KD * i:KD * i + KD, :], v.rearrange("(k p) -> k p", p=P)).then_inc(S["params_in"], 16)
            sp.dma_start(b1r[:, :], b1.rearrange("e (h p) -> (e h) p", p=P)).then_inc(S["params_in"], 16)
            for dup in range(2):
                sp.dma_start(pj[:, :, dup, :], proj.rearrange("(t p) d -> p t d", p=P)).then_inc(S["params_in"], 16)
            for i, w in enumerate((gwq, gwk, gwv, gwo)):
                sp.dma_start(gw[i], w.rearrange("(k p) n -> p k n", p=P)).then_inc(S["gw_in"], 16)
            sp.dma_start(wc, w_conv.rearrange("(k p) n -> p k n", p=P)).then_inc(S["wc_in"], 16)
            sp.dma_start(wr_s[:, :, :], wr.rearrange("(k p) n -> p k n", p=P)).then_inc(S["route_in"], 16)
            sp.dma_start(b2_s[:, :], b2).then_inc(S["route_in"], 16)
            sp.wait_ge(S["conv_mm"], 3 * KD)

            def load_expert(slot, w1e, w2e):
                sp.dma_start(ring1[slot], w1e).then_inc(w_in[slot], 16)
                sp.dma_start(ring2[slot], w2e).then_inc(w_in[slot], 16)

            w1v = w1.rearrange("e (k p) f -> e p k f", p=P)
            w2v = w2.rearrange("e (k p) n -> e p k n", p=P)
            qv, kvv, vv = (w.rearrange("(k p) n -> p k n", p=P) for w in (fwq, fwk, fwv))
            for e in range(RW):
                load_expert(e, w1v[e], w2v[e])
            with sp.Fori(0, PAIRS) as pr:
                sp.wait_ge(S["proj_done"], pr + 1)
                for i, w in enumerate((qv, kvv, vv)):
                    sp.dma_start(wst[:, i, :, :], w[:, :, bass.ds(pr * P, P)]).then_inc(S["wst_in"], 16)

            sp.wait_ge(S["qpad_ready"], 1)
            reps = TOPK * N // DH
            sp.dma_start(yd[0:reps * DH, :].rearrange("(r p) d -> p r d", p=DH),
                         QT[DH:P, 0, 0:D].rearrange("p (a d) -> p a d", a=1).to_broadcast([DH, reps, D])).then_inc(S["y_zeroed"], 16)
            sp.dma_start(yd[reps * DH:TOPK * N, :], QT[DH:DH + TOPK * N - reps * DH, 0, 0:D]).then_inc(S["y_zeroed"], 16)
            sp.wait_ge(S["proj_done"], PAIRS + 1)
            sp.dma_start(wo_s, fwo.rearrange("(k p) n -> p k n", p=P)).then_inc(S["wo_in"], 16)
            sp.wait_ge(S["pt_dve"], PAIRS * (2 * U + 2) + 1)
            sp.dma_start(g2row[:, 0, :], l2g.rearrange("(a n) -> a n", a=1).to_broadcast([P, D])).then_inc(S["ln2_in"], 16)
            sp.dma_start(g2row[:, 1, :], l2b.rearrange("(a n) -> a n", a=1).to_broadcast([P, D])).then_inc(S["ln2_in"], 16)
            for t in range(NT):
                sp.wait_ge(S["x2_ready"], t + 1)
                sp.dma_start(x2d[t * P:t * P + sz(t), :], nrow[0:sz(t), t, :]).then_inc(S["x2_out"], 16)

            with sp.Fori(0, NEXP // RW - 1) as it:
                for j in range(RW):
                    sp.wait_ge(S["l2_mm"], it * RW + (j + 3))
                    load_expert(j, w1v[bass.ds(it * RW + (j + RW), 1)].rearrange("e p k f -> p (e k) f"),
                                w2v[bass.ds(it * RW + (j + RW), 1)].rearrange("e p k f -> p (e k) f"))
            for k in range(2):
                sp.wait_ge(y_stored[k], 16 * (NEXP // 2))

            def load_choices(t):
                sp.dma_start(ygat[0:sz(t), t % YG, :, :], yd[TOPK * t * P:TOPK * (t * P + sz(t)), :]
                             .rearrange("(p k) d -> p k d", k=TOPK)).then_inc(yg_in[t % YG], 16)

            for t in range(YG):
                load_choices(t)
            for t in range(NT):
                sp.wait_ge(S["acc_ready"], t + 1)
                if t + YG < NT:
                    load_choices(t + YG)
                sp.dma_start(out[t * P:t * P + sz(t), :], xr[0:sz(t), t, :]).then_inc(S["out_stored"], 16)
            sp.wait_ge(S["out_stored"], 16 * NT)

        @block.gpsimd
        def _(pool):
            link = Link(pool, S["pool_link"])
            nc.gpsimd.iota(tk, pattern=[[WT, WN], [0, WIN]], base=0, channel_multiplier=0,
                           allow_small_or_imprecise_dtypes=True)
            nc.gpsimd.iota(wfirst, pattern=[[WT, WN]], base=0, channel_multiplier=0,
                           allow_small_or_imprecise_dtypes=True).then_inc(S["wbase_ready"], 1)
            nc.gpsimd.iota(iota16[:, :], pattern=[[1, 512]], base=0, channel_multiplier=0,
                           allow_small_or_imprecise_dtypes=True)
            nc.gpsimd.iota(iota64[:, :], pattern=[[1, NEXP]], base=0, channel_multiplier=0,
                           allow_small_or_imprecise_dtypes=True)
            nc.gpsimd.iota(choice[:, :, :], pattern=[[TOPK * P, NT], [1, TOPK]], base=-EMPTY, channel_multiplier=TOPK,
                           allow_small_or_imprecise_dtypes=True)
            nc.gpsimd.memset(onesb[:, :], 1.0)
            nc.gpsimd.memset(tri[:, :], 1.0)
            link(nc.gpsimd.memset(identf[:, :], 0.0))
            nc.gpsimd.affine_select(out=identf[:, :], in_=identf[:, :], compare_op=ALU.not_equal, fill=1.0, base=0,
                                    pattern=[[-1, P]], channel_multiplier=1)
            nc.gpsimd.affine_select(out=tri[:, :], in_=tri[:, :], compare_op=ALU.is_gt, fill=0.0, base=0,
                                    pattern=[[1, P]], channel_multiplier=-1).then_inc(S["consts"], 1)
            pool.wait_ge(S["mk_ready"], 1)
            nc.gpsimd.partition_all_reduce(gmk, mk8, P, RMAX).then_inc(S["gmk_ready"], 1)

            def split_tile(t, part):
                x = r2[0:sz(t), t, :]
                if part == 0:
                    pool.wait_ge(S["xs_hi"], t + 1)
                    nc.gpsimd.tensor_tensor(x, x, xs[0][0:sz(t), t, :], ALU.subtract).then_inc(S["xs_rest"], 1)
                else:
                    pool.wait_ge(S["xs_mid"], t + 1)
                    nc.gpsimd.tensor_tensor(xs[2][0:sz(t), t, :], x, xs[1][0:sz(t), t, :], ALU.subtract).then_inc(S["xs_ready"], 1)

            for part in range(2):
                for t in range(NT):
                    split_tile(t, part)
            pool.wait_ge(S["n1_T"], NT)
            nc.gpsimd.memset(QT[64:128, 0, :], 0.0)
            nc.gpsimd.memset(QT[0:64, 1, :], 0.0).then_inc(S["qpad_ready"], 1)
            pool.wait_ge(S["tabT_ready"], 1)
            pool.wait_ge(S["x2_out"], 16 * NT)
            pool.wait_ge(S["y_zeroed"], 32)

            def store_rows(e):
                pool.wait_ge(S["y_ready"], e + 3)
                nc.gpsimd.indirect_dma_start(
                    out=yd, out_offset=bass.IndirectOffsetOnAxis(ap=tabc[:, e:e + 1], axis=0),
                    in_=ys[0:CAP, e % 2, :], in_offset=None,
                    bounds_check=TOPK * N - 1, oob_is_err=False).then_inc(y_stored[e % 2], 16)

            BEHIND = XB + 2
            for e in range(NEXP + BEHIND):
                if e < NEXP:
                    if e >= XB:
                        pool.wait_ge(S["xT_mm"], e - XB + 1)
                    nc.gpsimd.indirect_dma_start(
                        out=xb[0:CAP, e % XB, :], out_offset=None, in_=x2d,
                        in_offset=bass.IndirectOffsetOnAxis(ap=tabT[:, e:e + 1], axis=0),
                        bounds_check=N - 1, oob_is_err=False).then_inc(xb_in[e % XB], 16)
                if e >= BEHIND:
                    store_rows(e - BEHIND)

        @block.scalar
        def _(act):
            act_ = nc.scalar.activation

            def root(n, g, cols):
                act.wait_ge(S["var_ready"], turn(n, g) + 1)
                act_(rs[:, cols], rs[:, cols], ACT.Sqrt).then_inc(S["sd_ready"], 1)

            def norm_rows(out, rows, n, g, done):
                act.wait_ge(S["shift_ready"], turn(n, g))
                for t in pair(g):
                    act_(out[0:sz(t), t, :], rows[0:sz(t), t, :], ACT.Identity, bias=nmr[0:sz(t), t:t + 1],
                         scale=rs[0:sz(t), t:t + 1]).then_inc(S[done], 1)

            root(0, 0, slice(0, NT))
            for t in range(NT):
                act.wait_ge(S["h_T"], t + 1)
                act_(tA[:, :, t * P:t * P + sz(t)], ps[:, 2 + t % 2, :].rearrange("p (k c) -> p k c", k=KD)[:, :, 0:sz(t)],
                     ACT.Copy).then_inc(S["hT_ready"], 1)
            act.wait_ge(S["bvar_ready"], 1)
            act_(ab[:, 0, :], ab[:, 0, :], ACT.Sqrt).then_inc(S["bsd_ready"], 1)

            for p in range(PAIRS):
                act.wait_ge(S["qk_mm"], p + 1)
                act_(qk[:, :, p, :], ps[:, p % 2, :].rearrange("p (s c) -> p s c", s=2), ACT.Copy,
                     scale=float(DH) ** -0.25).then_inc(S["qk_ready"], 1)
            act.wait_ge(S["qk_ready"], PAIRS)
            act_(sq, qk, ACT.Square).then_inc(S["sq_ready"], 1)
            act.wait_ge(S["dg_mm"], 1)
            for u in range(NQ * PAIRS):
                nt, p = divmod(u, PAIRS)
                act.wait_ge(S["u_mm"], u + 1)
                act_(kf[:, nt, 2 * p:2 * p + 2, :], ps[:, 5 + u % 3, :].rearrange("p (h m) -> p h m", h=2),
                     ACT.Copy).then_inc(S["uk_copied"], 1)
            for u in range(NQ * PAIRS):
                nt, p = divmod(u, PAIRS)
                act.wait_ge(S["uq_bias"], u + 1)
                for h in range(2):
                    act_(qf[:, nt, 2 * p + h, :], ps[:, 5 + (u + 8) % 3, h * M:(h + 1) * M], ACT.Exp,
                         bias=bq[:, nt, 2 * p + h:2 * p + h + 1]).then_inc(S["uq_exp"], 1)
            act.wait_ge(S["bk_ready"], 1)
            act.wait_ge(S["uk_copied"], NQ * PAIRS)
            for nt in range(NQ):
                for h in range(HEADS):
                    act_(kf[:, nt, h, :], kf[:, nt, h, :], ACT.Exp, bias=bk[:, nt, h:h + 1]).then_inc(S["kexp_done"], 1)
            for t in range(NT):
                act.wait_ge(S["xn_ready"], t + 1)
                act_(xs[0][0:sz(t), t, :], r2[0:sz(t), t, :], ACT.Copy).then_inc(S["xs_hi"], 1)
            for h in range(HEADS):
                act.wait_ge(S["qfT_mm"], h + 1)
                if h >= 2:
                    act.wait_ge(S["ga_mm"], h - 1)
                act_(qfT[:, h % 2, :, :], ps[:, 4 + h % 2, :].rearrange("p (m n) -> p m n", m=M // P),
                     ACT.Copy).then_inc(S["qfT_ready"], 1)
            for b in range(2):
                act.wait_ge(S["ga_T"], b + 1)
                act_(attnTg[:, 2 * b:2 * b + 2, :], ps[:, b, :].rearrange("p (k n) -> p k n", k=2), ACT.Copy).then_inc(S["gaT_ready"], 1)
            for b in range(2):
                act.wait_ge(S["ho_mm"], b + 1)
                act_(hatt[:, 2 * b:2 * b + 2, :], ps[:, 2 + b, :].rearrange("p (k n) -> p k n", k=2), ACT.Copy).then_inc(S["hatt_ready"], 1)

            for t in range(NT):
                act.wait_ge(S["xs_rest"], t + 1)
                act_(xs[1][0:sz(t), t, :], r2[0:sz(t), t, :], ACT.Copy).then_inc(S["xs_mid"], 1)

            def m_onehots(block, g, col, n):
                for j in range(g * MG, (g + 2) * MG):
                    last = act_(ohm[:, block * PAIRC + j, :], iota16[:, 0:P], ACT.Abs, bias=nm[:, bass.ds(col + j, 1)])
                last.then_inc(S["abs_ready"], 1)
                act.wait_ge(S["abs_ready"], n + 1)
                part = ohm[:, block * PAIRC + g * MG:block * PAIRC + (g + 2) * MG, :]
                act_(part, part, ACT.Relu, bias=onesf[:, 0:1], scale=-1.0).then_inc(S["ohm_act"], 2)

            with act.Fori(0, WN // 4) as it:
                for w in range(4):
                    block, odd = divmod(w, 2)

                    act.wait_ge(S["oh_used"], it * (4 * WIN) + ((w + 1) * WIN + CREDIT))
                    act_(AT[0][:, :, bass.ds(it * (4 * WT) + w * WT, WT)], ps[:, 4 + w, 0:WK].rearrange("p (a n) -> p a n", a=NT),
                         ACT.Copy).then_inc(S["cnt_ready"], 1)
                    m_onehots(block, 2 * odd, it * (2 * PAIRC) + ((block + 2) * PAIRC + PADC - FIRST), it * 4 + w)
            act.wait_ge(S["oh_used"], WN * WIN + CREDIT)
            act_(AT[0][:, :, N - WT:N], ps[:, 4, 0:WK].rearrange("p (a n) -> p a n", a=NT), ACT.Copy).then_inc(S["cnt_ready"], 1)
            act.wait_ge(S["flag_ready"], 1)
            total = act.value_load(flag[0:1, 0:1], min_val=0, max_val=E)
            with act.If(total < E):
                with act.Fori(0, WN) as w:
                    act.wait_ge(S["gcnt_oh_used"], w * FULL + (NBG + FULL))
                    act_(AT[0][:, :, bass.ds(w * WT, WT)], ps[:, 4, 0:WK].rearrange("p (a n) -> p a n", a=NT),
                         ACT.Copy).then_inc(S["gcnt_hi"], 1)
            for c, (c0, c1) in enumerate(COLS):
                cn = c1 - c0
                for fo in range(KD):
                    n = c * KD + fo
                    act.wait_ge(S["conv_mm"], n + 1)
                    if n >= 2:
                        act.wait_ge(S["z_ready"], n - 1)
                    act_(rl[:, n % 2, 0:cn], ps[:, 7 - 7 * (n % 2), 0:cn], ACT.Relu,
                         bias=par[:, 4 * KD + fo:4 * KD + fo + 1]).then_inc(S["rl_ready"], 1)
            act.wait_ge(S["bvar_ready"], 2)
            act_(ab[:, 0, :], ab[:, 0, :], ACT.Sqrt).then_inc(S["bsd_ready"], 1)
            def n1_copy(t):
                act.wait_ge(S["n1_T"], t + 1)
                act_(tA[:, :, t * P:t * P + sz(t)], ps[:, 2 + t % 2, :].rearrange("p (k c) -> p k c", k=KD)[:, :, 0:sz(t)],
                     ACT.Copy).then_inc(S["n1T_raw"], 1)

            for g in range(NG + 2):
                if g < NG:
                    root(1, g, slice(2 * g, 2 * g + 2))
                if 1 <= g <= NG:
                    root(2, g - 1, slice(2 * g - 2, 2 * g))
                if g < NG:
                    norm_rows(r2, xr, 1, g, "y_rows")
                if 1 <= g <= NG:
                    norm_rows(nrow, r2, 2, g - 1, "n1_ready")
                if g >= 2:
                    for t in pair(g - 2):
                        n1_copy(t)

            with act.Fori(0, PAIRS) as pr:
                act.wait_ge(S["q_mm"], pr + 1)
                for h in range(2):
                    half = slice(h * DH, (h + 1) * DH)
                    act_(QT[half, h, :], psf[half, 0:N], ACT.Copy, scale=float(DH) ** -0.5).then_inc(S["qkv_act"], 1)
                act.wait_ge(S["proj_done"], pr + 2)
                act_(V[:, 0:4, :], ps[:, 6, :].rearrange("p (t c) -> p t c", t=4), ACT.Copy).then_inc(S["qkv_act"], 1)

                def exp_unit(i):
                    qt = sz(i // 2)
                    act.wait_ge(S["negmax"], pr * U + (i + 1))
                    if i >= 2:
                        act.wait_ge(S["p_T"], pr * PTS + 3 * (i - 1))
                    act_(Pb[0:qt, i % 2, :], psf[0:qt, 1536 * (i % 2):1536 * (i % 2) + N], ACT.Exp,
                         bias=nmx[0:qt, i % 2:i % 2 + 1],
                         accum_out=esum[0:qt, i % 2:i % 2 + 1]).then_inc(S["exp_done"], 1)

                exp_unit(0)
                for i in range(U):
                    if i + 1 < U:
                        exp_unit(i + 1)
                    act.wait_ge(S["p_T"], pr * PTS + 3 * i + 2)
                    act_(PT[:, i % 2, 4:8, 0:sz(i // 2)],
                         ps[:, 6 + (3 * i + 1) % 2, :].rearrange("p (t c) -> p t c", t=4)[:, :, 0:sz(i // 2)],
                         ACT.Copy).then_inc(S["pt_act"], 1)

            def x2T_copy(r):
                act.wait_ge(S["x2_T"], r + 1)
                if r >= 2:
                    act.wait_ge(S["lg_mm"], r - 1)
                act_(x2T[:, r % 2, :, 0:sz(r)], ps[:, 2 + r % 2, :].rearrange("p (k c) -> p k c", k=KD)[:, :, 0:sz(r)],
                     ACT.Copy).then_inc(S["x2T_ready"], 1)

            for g in range(NG + 2):
                if g < NG:
                    root(3, g, slice(2 * g, 2 * g + 2))
                if g >= 2:
                    for t in pair(g - 2):
                        x2T_copy(t)
            act.wait_ge(S["exs_ready"], NT)
            act_(ex, ex, ACT.Exp)
            act_(gk[:, 0, :, :], gk[:, 0, :, :], ACT.Exp).then_inc(S["exp_ready"], 1)
            with act.Fori(0, NEXP // 2) as it:
                for j in range(2):
                    act.wait_ge(S["l1_mm"], it * 2 + (j + 1))
                    act.wait_ge(S["l2_mm"], it * 2 + (j + 1))
                    for f in range(F // P):
                        last = act_(hT[:, j, f, :], ps[:, 2 + j, f * P:f * P + CAP], ACT.Gelu_apprx_tanh,
                                    bias=b1T[:, bass.ds(it * 4 + (2 * j + f), 1)])
                    last.then_inc(S["gelu_done"], 1)
            for c, (c0, c1) in enumerate(COLS):
                act.wait_ge(S["G_T"], c + 1)
                act_(GT[:, c0:c1], ps[0:NEXP, c, 0:c1 - c0], ACT.Copy).then_inc(S["GT_ready"], 1)

        @block.vector
        def _(dve):
            V_ = nc.vector
            link = Link(dve, S["dve_link"])
            V_.memset(mv[:, :, :], 1.0)
            V_.memset(er_f, -1.0)
            V_.memset(ef[:, :, 0:PADC], -1.0)
            V_.memset(onesf[:, :], 1.0)
            link(V_.memset(halfblk[:, :], 0.0))
            V_.memset(halfblk[0:64, 0:1], 0.5)
            V_.memset(halfblk[64:128, 1:2], 0.5)
            V_.memset(projblk, 0.0)
            dve.wait_ge(S["edges_in"], 96)
            V_.tensor_copy(er_f[:, :, 0:2, :], er_i[:, :, 0:2, :])
            V_.tensor_copy(er_f[0:ROWS - 2 * P, :, 2, :], er_i[0:ROWS - 2 * P, :, 2, :])
            V_.tensor_copy(er_f[0:1, :, 3, 0:LEFT], er_i[0:1, :, 3, 0:LEFT]).then_inc(S["raw_ready"], 1)

            def moments(tiles, rows, made, count):
                dve.wait_ge(S[made], count)
                for t in tiles:
                    last = V_.bn_stats(st[0:sz(t), t, :], rows[0:sz(t), t, :])
                link(last)
                for t in tiles:
                    last = V_.bn_aggr(mv[0:sz(t), t, :], st[0:sz(t), t, :])
                link(last)
                cols = slice(tiles[0], tiles[-1] + 1)
                V_.tensor_scalar(rs[:, cols], mv[:, cols, 1], EPS, None, ALU.add).then_inc(S["var_ready"], 1)

            def inverse(n, g, cols):
                dve.wait_ge(S["sd_ready"], turn(n, g) + 1)
                link(V_.reciprocal(rs[:, cols], rs[:, cols]))

            def shift(n, g):
                cols = slice(2 * g, 2 * g + 2)
                inverse(n, g, cols)
                V_.scalar_tensor_tensor(nmr[:, cols], mv[:, cols, 0], -1.0, rs[:, cols], ALU.mult, ALU.mult)\
                  .then_inc(S["shift_ready"], 1)

            def batch_norm_stats(k, i):
                c0, c1 = BN[i]
                return V_.bn_stats(bst[:, k, i, :], tA[:, k, c0:c1])

            def batch_norm_affine(first, g0, b0):
                for k in range(KD):
                    last = V_.bn_aggr(bmv[:, k, :], bst[:, k, :, :].rearrange("p a b -> p (a b)"))
                link(last)
                V_.tensor_scalar(ab[:, 0, :], bmv[:, :, 1], EPS, None, ALU.add).then_inc(S["bvar_ready"], 1)
                dve.wait_ge(S["bsd_ready"], first)
                link(V_.reciprocal(ab[:, 0, :], ab[:, 0, :]))
                link(V_.tensor_tensor(ab[:, 1, :], ab[:, 0, :], par[:, g0:g0 + KD], ALU.mult))
                link(V_.tensor_tensor(ab[:, 2, :], bmv[:, :, 0], ab[:, 1, :], ALU.mult))
                link(V_.tensor_tensor(ab[:, 2, :], par[:, b0:b0 + KD], ab[:, 2, :], ALU.subtract))

            dve.wait_ge(S["x_in"], 32)
            moments(range(NT), xr, "x_in", 32)
            inverse(0, 0, slice(0, NT))
            for t in range(NT):
                V_.tensor_scalar(r2[0:sz(t), t, :], xr[0:sz(t), t, :], mv[0:sz(t), t, 0:1], rs[0:sz(t), t:t + 1],
                                 ALU.subtract, ALU.mult).then_inc(S["h_ready"], 1)
            dve.wait_ge(S["raw_T"], 1)
            link(V_.tensor_copy(ef[:, :, PADC:PADC + 384], ps[:, 0:2, 0:384]))
            V_.tensor_copy(ef[:, :, PADC + ROWS:PADC + ROWS + 1], ps[:, 0:2, 384:385]).then_inc(S["ef_ready"], 1)
            dve.wait_ge(S["par_T"], 1)
            V_.tensor_copy(par[:, :], ps[:, 4, 0:28])
            V_.tensor_copy(b1T[:, :], ps[:, 4, 128:256])
            V_.tensor_copy(projblk[0:64, 0, :], ps[0:64, 5, 0:M])
            V_.tensor_copy(projblk[64:128, 1, :], ps[64:128, 5, 0:M]).then_inc(S["par_ready"], 1)
            for i, (c0, c1) in enumerate(BN):
                dve.wait_ge(S["hT_ready"], -(-c1 // P))
                for k in range(KD):
                    last = batch_norm_stats(k, i)
            link(last)
            batch_norm_affine(1, 0, KD)
            for k in range(KD):
                V_.tensor_scalar(tB[:, k * N:(k + 1) * N], tA[:, k, :], ab[:, 1, k:k + 1], ab[:, 2, k:k + 1],
                                 ALU.mult, ALU.add).then_inc(S["xnT_ready"], 1)
            V_.memset(vaug[:, :, :, DH:DH + 1], 1.0)
            for nt in range(NQ):
                dve.wait_ge(S["v_mm"], nt + 1)
                V_.tensor_copy(vaug[:, nt, :, 0:DH], ps[:, 2 + nt, :].rearrange("p (h d) -> p h d", h=HEADS)).then_inc(S["v_ready"], 1)
            dve.wait_ge(S["dg_mm"], 1)
            link(V_.tensor_copy(dg, ps[:, 4, 0:2 * NQ * HEADS].rearrange("p (s n h) -> p s n h", s=2, n=NQ)))
            for u in range(NQ * PAIRS):
                nt, p = divmod(u, PAIRS)
                dve.wait_ge(S["uk_copied"], u + 1)
                V_.tensor_reduce(mk[:, nt, 2 * p:2 * p + 2], kf[:, nt, 2 * p:2 * p + 2, :], AXX, ALU.max).then_inc(S["uk_maxed"], 1)
            dve.wait_ge(S["uk_maxed"], NQ * PAIRS)
            V_.tensor_tensor(mk8, mk[:, 0, :], mk[:, 1, :], ALU.max).then_inc(S["mk_ready"], 1)
            for u in range(NQ * PAIRS):
                nt, p = divmod(u, PAIRS)
                dve.wait_ge(S["u_mm"], NQ * PAIRS + u + 1)
                link(V_.tensor_reduce(bq[:, nt, 2 * p:2 * p + 2], ps[:, 5 + (u + 8) % 3, :].rearrange("p (h m) -> p h m", h=2),
                                      AXX, ALU.max))
                V_.scalar_tensor_tensor(bq[:, nt, 2 * p:2 * p + 2], bq[:, nt, 2 * p:2 * p + 2], -1.0, dg[:, 0, nt, 2 * p:2 * p + 2],
                                        ALU.mult, ALU.subtract).then_inc(S["uq_bias"], 1)
            dve.wait_ge(S["gmk_ready"], 1)
            for nt in range(NQ):
                last = V_.scalar_tensor_tensor(bk[:, nt, :], gmk, -1.0, dg[:, 1, nt, :], ALU.mult, ALU.subtract)
            last.then_inc(S["bk_ready"], 1)
            dve.wait_ge(S["uq_exp"], NQ * HEADS)
            V_.tensor_scalar(qf, qf, 1.0 / float(np.sqrt(M)), KEPS, ALU.mult, ALU.add).then_inc(S["qf_ready"], 1)
            for t in range(NT):
                dve.wait_ge(S["xn_T"], t + 1)
                V_.tensor_copy(r2[0:sz(t), t, :], ps[0:sz(t), 3 + t % 2, :]).then_inc(S["xn_ready"], 1)
            dve.wait_ge(S["kexp_done"], NQ * HEADS)
            V_.tensor_scalar(kf, kf, 1.0 / float(np.sqrt(M)), KEPS, ALU.mult, ALU.add).then_inc(S["kf_ready"], 1)
            dve.wait_ge(S["ef_ready"], 1)
            link(V_.tensor_copy(ei[0], ef[:, 0, :]))
            V_.tensor_scalar(ei[1], ei[0], 7, None, ALU.arith_shift_right)
            link(V_.tensor_scalar(ei[2], ei[0], 127, None, ALU.bitwise_and))
            V_.tensor_copy(efa, ei[1])
            link(V_.tensor_copy(ef[:, 0, :], ei[2]))
            V_.tensor_scalar(nm, ef[:, 0, :], -1.0, None, ALU.mult)
            link(V_.scalar_tensor_tensor(efa, efa, float(WT), ef[:, 1, :], ALU.mult, ALU.add))
            dve.wait_ge(S["wbase_ready"], 1)

            def windows(v, odd):
                c = PADC - FIRST + (ODD if odd else 0)
                n = (WN + 1 - odd) // 2
                return v[:, c:c + PAIRC * n].rearrange("p (w c) -> p w c", w=n)[:, :, 0:WIN]

            def outside(k, t, link, base=0):
                link(V_.tensor_scalar(t, t, (WT - 1) / 2.0, None, ALU.subtract), base)
                link(V_.tensor_tensor(t, t, t, ALU.mult), base)
                link(V_.tensor_scalar(t, t, WT * WT / 4.0, 4096.0, ALU.is_gt, ALU.mult), base)
                return V_.tensor_tensor(k, k, t, ALU.add)

            keyv, tkv = (v.rearrange("p (w c) -> p w c", w=WN) for v in (key, tk))
            for q in range(2):
                last = V_.tensor_tensor(keyv[:, q::2, :], windows(efa, q), tkv[:, q::2, :], ALU.subtract)
            link(last)
            for q in range(2):
                last = V_.tensor_tensor(tkv[:, q::2, :], windows(ef[:, 1, :], q), tkv[:, q::2, :], ALU.subtract)
            link(last)
            link(outside(key, tk, link))
            for g in range(2 * PAIRC - MG):
                last = V_.tensor_scalar(ohm[:, g, :], iota16[:, 0:P], ef[:, 0, g + PADC - FIRST:g + PADC - FIRST + 1], None, ALU.is_equal)
            last.then_inc(S["ohm_dve"], 1)
            for b in range(4):
                dve.wait_ge(S["kv_mm"], b + 1)
                V_.tensor_copy(kv[:, 2 * b:2 * b + 2, :, :], ps[:, b, :].rearrange("p (h m c) -> p h m c", h=2, m=2)[:, :, :, 0:DH + 1])\
                  .then_inc(S["kv_ready"], 1)
            for h in range(HEADS):
                dve.wait_ge(S["ga_mm"], h + 1)
                o = ps[:, 6 + h % 2, 0:256].rearrange("p (n c) -> p n c", n=NQ)
                link(V_.tensor_scalar(zr[:, h % 2, :], o[:, :, DH], KEPS, None, ALU.add))
                link(V_.reciprocal(zr[:, h % 2, :], zr[:, h % 2, :]))
                for nt in range(NQ):
                    last = V_.tensor_scalar(attnrow[:, nt, h * DH:(h + 1) * DH], o[:, nt, 0:DH], zr[:, h % 2, nt:nt + 1],
                                            None, ALU.mult)
                last.then_inc(S["ga_ready"], 1)



            def window_onehots(step, block=None, col=None):
                for i in range(WIN):
                    dve.wait_ge(S["oh_used"], step + (i + 1 - NB + CREDIT))
                    V_.tensor_scalar(ohs[:, i % NB, :], iota16[:, 0:WK], key[:, bass.ds(step + i, 1)], None,
                                     ALU.is_equal).then_inc(S["oh_ready"], 1)
                    if block is not None and WIN - 1 - MG <= i < WIN - 1:
                        j = PAIRC - WIN + 1 + i
                        last = V_.tensor_scalar(ohm[:, block * PAIRC + j, :], iota16[:, 0:P],
                                                ef[:, 0, bass.ds(col + j, 1)], None, ALU.is_equal)
                        if j == PAIRC - 1:
                            last.then_inc(S["ohm_dve"], 1)

            with dve.Fori(0, WN // 4) as it:
                for w in range(4):
                    if w % 2:
                        window_onehots(it * (4 * WIN) + w * WIN)
                    else:
                        window_onehots(it * (4 * WIN) + w * WIN, 1 - w // 2,
                                       it * (2 * PAIRC) + ((w // 2 + 1) * PAIRC + PADC - FIRST))
            window_onehots((WN - 1) * WIN)
            dve.wait_ge(S["deg_mm"], 2)
            V_.tensor_reduce(tot[:, 0:1], psf[:, 0:N], AXX, ALU.add)
            link(V_.tensor_reduce(tot[:, 1:2], psf[:, 0:N], AXX, ALU.max))
            V_.scalar_tensor_tensor(flag[0:1, 0:1], tot[0:1, 1:2], float(EXACT), tot[0:1, 0:1], ALU.is_lt, ALU.mult)\
              .then_inc(S["flag_ready"], 1)
            dve.wait_ge(S["flag_ready"], 1)
            total = dve.value_load(flag[0:1, 0:1], min_val=0, max_val=E)
            with dve.If(total < E):
                glink = Link(dve, S["gcnt_link"])
                with dve.Fori(0, WN) as w:
                    for v, o in ((efa, key), (ef[:, 1, :], tk)):
                        last = V_.tensor_scalar(o[:, 0:FULL], v[:, PADC:PADC + FULL], wfirst[:, bass.ds(w, 1)], None, ALU.subtract)
                    glink(last, base=w * 5)
                    glink(outside(key[:, 0:FULL], tk[:, 0:FULL], glink, base=w * 5), base=w * 5)

                    def one_hots(g):
                        for j in range(NBG):
                            dve.wait_ge(S["gcnt_oh_used"], w * FULL + g * NBG + (j + 1))
                            V_.tensor_scalar(ohm[:, j, :], iota16[:, 0:P], ef[:, 0, bass.ds(g * NBG + (PADC + j), 1)], None, ALU.is_equal)
                            V_.tensor_scalar(ohg[:, j, :], iota16[:, 0:WK], key[:, bass.ds(g * NBG + j, 1)],
                                             None, ALU.is_equal).then_inc(S["gcnt_oh_ready"], 1)

                    one_hots(0)
                    with dve.Fori(1, FULL // NBG) as g:
                        one_hots(g)
                    dve.wait_ge(S["gcnt_hi"], w + 1)
                    V_.tensor_tensor(AT[1][:, :, bass.ds(w * WT, WT)], ps[:, 4, 0:WK].rearrange("p (a n) -> p a n", a=NT),
                                     AT[0][:, :, bass.ds(w * WT, WT)], ALU.subtract).then_inc(S["gcnt_ready"], 1)
                dve.wait_ge(S["deg_mm"], 3)
            V_.tensor_scalar(rdegB, psf[:, 0:N], 1.0, None, ALU.max).then_inc(S["rdeg_ready"], 1)
            dve.wait_ge(S["rdeg_ready"], 1)
            V_.reciprocal(rdegB, rdegB).then_inc(S["rdeg_ready"], 1)
            dve.wait_ge(S["rdeg_ready"], 2)
            for c, (c0, c1) in enumerate(COLS):
                cn = c1 - c0
                for k in range(KD):
                    dve.wait_ge(S["agg_mm"], c * KD + k + 1)
                    if c >= 1 and k == 0:
                        dve.wait_ge(S["conv_mm"], c * KD)
                    V_.tensor_tensor(aggT[:, k, 0:cn], ps[:, 3 + k, 0:cn], rdegB[:, c0:c1], ALU.mult).then_inc(S["agg_ready"], 1)
                for fo in range(KD):
                    n = c * KD + fo
                    dve.wait_ge(S["rl_ready"], n + 1)
                    a0 = SEQ if c == 0 else 0
                    if c == 0:
                        dve.wait_ge(S["hatt_ready"], 2)
                        link(V_.tensor_tensor(rl[:, n % 2, 0:SEQ], rl[:, n % 2, 0:SEQ], hatt[:, fo, :], ALU.add))
                        V_.tensor_tensor(tA[:, fo, 0:SEQ], rl[:, n % 2, 0:SEQ], tA[:, fo, 0:SEQ], ALU.add)
                    V_.scalar_tensor_tensor(tA[:, fo, c0 + a0:c1], rl[:, n % 2, a0:cn], hatt[:, fo, SEQ - 1:SEQ],
                                            tA[:, fo, c0 + a0:c1], ALU.add, ALU.add).then_inc(S["z_ready"], 1)
                    if c >= 1:
                        dve.wait_ge(S["z_ready"], c * KD)
                        batch_norm_stats(fo, c - 1)
            dve.wait_ge(S["z_ready"], 3 * KD)
            for k in range(KD):
                last = batch_norm_stats(k, 2)
            link(last)
            batch_norm_affine(2, 2 * KD, 3 * KD)
            for k in range(KD):
                V_.tensor_scalar(tA[:, k, :], tA[:, k, :], ab[:, 1, k:k + 1], ab[:, 2, k:k + 1],
                                 ALU.mult, ALU.add).then_inc(S["w_ready"], 1)
            for g in range(NG + 1):
                if g < NG:
                    for t in pair(g):
                        dve.wait_ge(S["w_T"], t + 1)
                        V_.tensor_tensor(xr[0:sz(t), t, :], xr[0:sz(t), t, :], ps[0:sz(t), t % 2, :], ALU.add).then_inc(S["x1_ready"], 1)
                    moments(pair(g), xr, "x1_ready", 2 * g + 2)
                if g >= 1:
                    moments(pair(g - 1), r2, "y_rows", 2 * g)
                if g < NG:
                    shift(1, g)
                if g >= 1:
                    shift(2, g - 1)
            dve.wait_ge(S["n1T_raw"], NT)
            for k in range(KD):
                V_.tensor_scalar(tA[:, k, :], tA[:, k, :], par[:, 5 * KD + k:5 * KD + k + 1], par[:, 6 * KD + k:6 * KD + k + 1],
                                 ALU.mult, ALU.add).then_inc(S["x1T_ready"], 1)

            with dve.Fori(0, PAIRS) as pr:
                dve.wait_ge(S["k_mm"], pr + 1)
                V_.tensor_copy(KT, psf[:, 1536:1536 + N]).then_inc(S["qkv_dve"], 1)
                dve.wait_ge(S["proj_done"], pr + 2)
                V_.tensor_copy(V[:, 8, :], ps[:, 5, 256:384]).then_inc(S["qkv_dve"], 1)
                V_.tensor_copy(V[0:TAIL, 9, :], ps[0:TAIL, 5, 384:512]).then_inc(S["qkv_dve"], 1)
                V_.tensor_copy(V[:, 4:8, :], ps[:, 7, :].rearrange("p (t c) -> p t c", t=4)).then_inc(S["qkv_dve"], 1)

                def neg_max(i):
                    qt = sz(i // 2)
                    dve.wait_ge(S["s_mm"], pr * U + (i + 1))
                    if i >= 2:
                        dve.wait_ge(S["exp_done"], pr * U + (i - 1))
                    V_.tensor_reduce(nmx[0:qt, i % 2:i % 2 + 1], psf[0:qt, 1536 * (i % 2):1536 * (i % 2) + N], AXX, ALU.max,
                                     negate=True).then_inc(S["negmax"], 1)

                def last_bank(i):
                    dve.wait_ge(S["p_T"], pr * PTS + (3 * i + 3 if i < U else 2 * U + i + 1))
                    bank = 6 + (3 * i + 2 if i < U else 2 * U + i) % 2
                    last = None
                    if i < U:
                        qt = sz(i // 2)
                        V_.tensor_copy(PT[:, i % 2, 8, 0:qt], ps[:, bank, 0:qt])
                        last = V_.tensor_copy(PT[0:TAIL, i % 2, 9, 0:qt], ps[0:TAIL, bank, P:P + qt])
                    if 1 <= i <= U:
                        n = i - 1
                        qt = sz(n // 2)
                        dve.wait_ge(S["loop_link"], pr * U + i)
                        last = V_.tensor_scalar(arow[0:qt, (n // 2) % 2, (n % 2) * DH:(n % 2 + 1) * DH],
                                                ps[0:qt, bank, 256:256 + DH], resum[0:qt, n % 4:n % 4 + 1], None, ALU.mult)
                    if i >= 3 and i % 2:
                        t = (i - 3) // 2
                        last = V_.tensor_copy(attnT[:, bass.ds(pr, 1), t * P:t * P + sz(t)].rearrange("p a n -> p (a n)"),
                                              ps[:, bank, 320:320 + sz(t)])
                    last.then_inc(S["pt_dve"], 1)

                neg_max(0)
                neg_max(1)
                for i in range(U + 3):
                    if i >= 1:
                        last_bank(i - 1)
                    if i < U:
                        qt = sz(i // 2)
                        dve.wait_ge(S["p_T"], pr * PTS + (3 * i + 1))
                        V_.tensor_copy(PT[:, i % 2, 0:4, 0:qt],
                                       ps[:, 6 + i % 2, :].rearrange("p (t c) -> p t c", t=4)[:, :, 0:qt]).then_inc(S["pt_dve"], 1)
                        dve.wait_ge(S["exp_done"], pr * U + (i + 1))
                        V_.reciprocal(resum[0:qt, i % 4:i % 4 + 1], esum[0:qt, i % 2:i % 2 + 1]).then_inc(S["loop_link"], 1)
                    if i + 2 < U:
                        neg_max(i + 2)

            def logits_pair(g):
                for t in pair(g):
                    dve.wait_ge(S["lg_mm"], t + 1)
                    last = V_.tensor_copy(lg[0:sz(t), t, :], ps[0:sz(t), 4 + t % 2, 0:NEXP])
                    last.then_inc(S["lg_read"], 1)
                dve.wait_ge(S["lg_read"], 2 * g + 2)
                for t in pair(g):
                    last = V_.max(v8[:, t, :], lg[:, t, :])
                link(last)
                for t in pair(g):
                    last = V_.max_index(i8[:, t, :], v8[:, t, :], lg[:, t, :])
                link(last)
                link(V_.tensor_copy(gk[:, 1, 2 * g:2 * g + 2, :], i8[:, 2 * g:2 * g + 2, 0:2]))
                for t in pair(g):
                    for k in range(2):
                        V_.tensor_scalar(ohk[k][:, t, :], iota64[:, :], gk[:, 1, t, k:k + 1], None, ALU.is_equal)
                    V_.tensor_scalar(ex[:, t, :], lg[:, t, :], v8[:, t, 0:1], None, ALU.subtract)
                    V_.tensor_scalar(gk[:, 0, t, :], v8[:, t, 0:2], v8[:, t, 0:1], None, ALU.subtract).then_inc(S["exs_ready"], 1)

            V_.memset(lg[:, NT - 1, :], 0.0)
            dve.wait_ge(S["ln2_in"], 32)
            dve.wait_ge(S["y_zeroed"], 32)
            def residual(g):
                for t in pair(g):
                    last = V_.tensor_tensor(xr[0:sz(t), t, :], xr[0:sz(t), t, :], r2[0:sz(t), t, :], ALU.add)
                link(last)

            for g in range(NG + 3):
                for done in {2: (0, 1), NG + 1: (2,), NG + 2: (3,)}.get(g, ()):
                    residual(done)
                if g < NG:
                    for t in pair(g):
                        dve.wait_ge(S["wo_mm"], t + 1)
                        V_.tensor_tensor(r2[0:sz(t), t, :], r2[0:sz(t), t, :], ps[0:sz(t), WO_BANKS[t % 4], :], ALU.add).then_inc(S["xx_ready"], 1)
                    moments(pair(g), r2, "xx_ready", 2 * g + 2)
                if g >= 3:
                    logits_pair(g - 3)
                if g < NG:
                    for t in pair(g):
                        last = V_.scalar_tensor_tensor(nrow[0:sz(t), t, :], r2[0:sz(t), t, :], mv[0:sz(t), t, 0:1],
                                                       g2row[0:sz(t), 0, :], ALU.subtract, ALU.mult)
                    link(last)
                    inverse(3, g, slice(2 * g, 2 * g + 2))
                    for t in pair(g):
                        n = nrow[0:sz(t), t, :]
                        V_.scalar_tensor_tensor(n, n, rs[0:sz(t), t:t + 1], g2row[0:sz(t), 1, :], ALU.mult, ALU.add)\
                          .then_inc(S["x2_ready"], 1)
            dve.wait_ge(S["exs_ready"], NT)
            V_.tensor_tensor(O, ohk[0], ohk[1], ALU.add).then_inc(S["O_ready"], 1)
            dve.wait_ge(S["exp_ready"], 1)
            link(V_.tensor_reduce(ssum[:, :], ex, AXX, ALU.add))
            link(V_.reciprocal(ssum[:, :], ssum[:, :]))
            for k in range(2):
                last = V_.tensor_tensor(gk[:, 2, :, k], gk[:, 0, :, k], ssum[:, :], ALU.mult)
            link(last)
            link(V_.tensor_tensor(gk[:, 3, :, 0], gk[:, 2, :, 0], gk[:, 2, :, 1], ALU.add))
            link(V_.reciprocal(gk[:, 3, :, 0], gk[:, 3, :, 0]))
            for k in range(2):
                last = V_.tensor_tensor(gk[:, 4, :, k], gk[:, 2, :, k], gk[:, 3, :, 0], ALU.mult)
            link(last)
            dve.wait_ge(S["pos_mm"], 1)
            V_.tensor_copy(posm[:, 0:8, :], ps[:, 6, :].rearrange("p (t e) -> p t e", t=8))
            V_.tensor_copy(posm[:, 8, :], ps[:, 7, 0:NEXP])
            link(V_.tensor_copy(posm[:, 9, :], ps[:, 7, NEXP:2 * NEXP]))
            for k in range(2):
                link(V_.tensor_tensor(tmp, posm, ohk[k], ALU.mult))
                link(V_.tensor_reduce(gk[:, 7, :, k], tmp, AXX, ALU.add))
            for t in range(NT):
                for k in range(2):
                    last = V_.tensor_scalar(pid[:, 2 * t + k, :], iota16[:, 0:CAP], gk[:, 7, t, k:k + 1], choice[:, t, k:k + 1],
                                            ALU.is_equal, ALU.mult)
                last.then_inc(S["pid_ready"], 1)
            V_.tensor_scalar(gk[:, 6, :, :], gk[:, 7, :, :], float(CAP), None, ALU.is_lt)
            residual(4)
            dve.wait_ge(S["tab_mm"], 1)
            link(V_.tensor_scalar(tabc[:, :], ps[0:CAP, 3, 0:NEXP], float(EMPTY), None, ALU.add))
            V_.tensor_scalar(tabT[:, :], tabc[:, :], 1, None, ALU.arith_shift_right).then_inc(S["tabT_ready"], 1)
            link(V_.tensor_tensor(gk[:, 4, :, :], gk[:, 4, :, :], gk[:, 6, :, :], ALU.mult))
            for t in range(NT):
                last = V_.tensor_scalar(tmp[:, t, :], ohk[0][:, t, :], gk[:, 4, t, 0:1], None, ALU.mult)
            link(last)
            for t in range(NT):
                last = V_.scalar_tensor_tensor(G[:, t, :], ohk[1][:, t, :], gk[:, 4, t, 1:2], tmp[:, t, :], ALU.mult, ALU.add)
            last.then_inc(S["G_ready"], 1)

            def xT_copy(j, n):
                dve.wait_ge(S["xT_mm"], n)
                V_.tensor_copy(xT[:, j, :, :], ps[:, j, :].rearrange("p (k c) -> p k c", k=KD)[:, :, 0:CAP]).then_inc(S["xT_ready"], 1)

            def y_copy(j, n, stored):
                dve.wait_ge(S["l2_mm"], n + 2)
                if stored is not None:
                    dve.wait_ge(y_stored[j], stored)
                V_.tensor_copy(ys[0:CAP, j, :], ps[0:CAP, 4 + j, :]).then_inc(S["y_ready"], 1)

            xT_copy(0, 1)
            xT_copy(1, 2)
            for j in range(2):
                xT_copy(j, j + 3)
                y_copy(j, j + 1, None)
            with dve.Fori(1, NEXP // 2 - 1) as it:
                for j in range(2):
                    xT_copy(j, it * 2 + (j + 3))
                    y_copy(j, it * 2 + (j + 1), it * 16)
            for j in range(2):
                y_copy(j, NEXP - 1 + j, 16 * (NEXP // 2 - 1))
            for t in range(NT):
                dve.wait_ge(S["b2_mm"], t + 1)
                xo = xr[0:sz(t), t, :]
                link(V_.tensor_tensor(xo, xo, ps[0:sz(t), 6 + t % 2, :], ALU.add))
                for k in range(2):
                    dve.wait_ge(yg_in[t % YG], 16 * (t // YG + 1))
                    last = V_.scalar_tensor_tensor(xo, ygat[0:sz(t), t % YG, k, :], gk[0:sz(t), 4, t, k:k + 1], xo, ALU.mult, ALU.add)
                    if k == 0:
                        link(last)
                last.then_inc(S["acc_ready"], 1)

        @block.tensor
        def _(pe):
            mm, tr = nc.tensor.matmul, nc.tensor.transpose
            pe.sem_inc(S["oh_used"], CREDIT)
            pe.sem_inc(S["proj_done"], 1)
            pe.sem_inc(S["pt_dve"], 1)
            pe.sem_inc(S["cnt_ready"], 4)
            pe.sem_inc(S["ohm_act"], 8)
            pe.sem_inc(S["gcnt_ready"], 1)
            pe.sem_inc(S["gcnt_oh_used"], NBG)
            pe.sem_inc(S["l2_mm"], 2)
            pe.sem_inc(S["y_ready"], 2)
            pe.wait_ge(S["consts"], 1)
            pe.wait_ge(S["raw_ready"], 1)
            for s in range(2):
                for b in range(3):
                    tr(ps[:, s, b * P:(b + 1) * P], er_f[:, s, b, :], identf[:, :])
                last = tr(ps[:, s, 384:385], er_f[0:1, s, 3, :], identf[0:1, 0:1])
            last.then_inc(S["raw_T"], 1)
            pe.wait_ge(S["params_in"], 160)
            tr(ps[:, 4, 0:28], prow[:, :], identf[0:28, 0:28])
            tr(ps[:, 4, 128:256], b1r[:, :], identf[:, :])
            for t in range(2):
                last = tr(ps[:, 5, t * P:(t + 1) * P], pj[:, t, :, :].rearrange("p a d -> p (a d)"), identf[:, :])
            last.then_inc(S["par_T"], 1)

            def rows_to_T(rows, ready, done, freed, bank, tiles=range(NT)):
                for t in tiles:
                    pe.wait_ge(S[ready], t + 1)
                    if t >= 2:
                        pe.wait_ge(S[freed], t - 1)
                    for k in range(KD):
                        last = tr(ps[:, bank + t % 2, k * P:k * P + sz(t)], rows[0:sz(t), t, k * P:(k + 1) * P],
                                  identf[0:sz(t), 0:sz(t)])
                    last.then_inc(S[done], 1)

            def T_to_rows(cols, done, freed, bank, tiles=range(NT)):
                for t in tiles:
                    if t >= 2:
                        pe.wait_ge(S[freed], t - 1)
                    for k in range(KD):
                        last = tr(ps[0:sz(t), bank + t % 2, k * P:(k + 1) * P], cols(k, t), identf[:, :])
                    last.then_inc(S[done], 1)

            rows_to_T(r2, "h_ready", "h_T", "hT_ready", 2)
            pe.wait_ge(S["hT_ready"], NT)

            pe.wait_ge(S["ef_ready"], 1)
            pe.wait_ge(S["par_ready"], 1)
            pe.wait_ge(S["gw_in"], 64)
            for p in range(PAIRS):
                if p >= 2:
                    pe.wait_ge(S["qk_ready"], p - 1)
                for s in range(2):
                    for k in range(KD):
                        last = mm(ps[:, p % 2, s * SEQ:(s + 1) * SEQ], gw[s][:, k, p * P:(p + 1) * P], tA[:, k, 0:SEQ],
                                  start=(k == 0), stop=(k == KD - 1))
                last.then_inc(S["qk_mm"], 1)
            for nt in range(NQ):
                for k in range(KD):
                    last = mm(ps[:, 2 + nt, :], tA[:, k, nt * P:(nt + 1) * P], gw[2][:, k, :], start=(k == 0), stop=(k == KD - 1))
                last.then_inc(S["v_mm"], 1)
            pe.wait_ge(S["sq_ready"], 1)
            for s in range(2):
                for nt in range(NQ):
                    for p in range(PAIRS):
                        c = (s * NQ + nt) * HEADS + 2 * p
                        last = mm(ps[:, 4, c:c + 2], sq[:, s, p, nt * P:(nt + 1) * P], halfblk[:, :], start=True, stop=True)
            last.then_inc(S["dg_mm"], 1)
            for u in range(2 * NQ * PAIRS):
                s, r = divmod(u, NQ * PAIRS)
                nt, p = divmod(r, PAIRS)
                if u >= 3:
                    v = u - 3
                    if v < NQ * PAIRS:
                        pe.wait_ge(S["uk_copied"], v + 1)
                    else:
                        pe.wait_ge(S["uq_exp"], 2 * (v - NQ * PAIRS + 1))
                mm(ps[:, 5 + u % 3, :], qk[:, 1 - s, p, nt * P:(nt + 1) * P], projblk.rearrange("p a m -> p (a m)"),
                   start=True, stop=True).then_inc(S["u_mm"], 1)
            pe.wait_ge(S["v_ready"], NQ)
            pe.wait_ge(S["xnT_ready"], KD)
            T_to_rows(lambda k, t: tB[:, k * N + t * P:k * N + t * P + sz(t)], "xn_T", "xn_ready", 3)
            pe.wait_ge(S["kf_ready"], 1)
            for h in range(HEADS):
                for m in range(M // P):
                    c = ((h % 2) * 2 + m) * P
                    for nt in range(NQ):
                        last = mm(ps[:, h // 2, c:c + DH + 1], kf[:, nt, h, m * P:(m + 1) * P], vaug[:, nt, h, :],
                                  start=(nt == 0), stop=(nt == NQ - 1))
                if h % 2:
                    last.then_inc(S["kv_mm"], 1)
            pe.wait_ge(S["qf_ready"], 1)

            def q_features_T(h):
                if h >= 2:
                    pe.wait_ge(S["qfT_ready"], h - 1)
                for m in range(M // P):
                    for nt in range(NQ):
                        last = tr(ps[:, 4 + h % 2, m * SEQ + nt * P:m * SEQ + (nt + 1) * P], qf[:, nt, h, m * P:(m + 1) * P],
                                  identf[:, :])
                last.then_inc(S["qfT_mm"], 1)

            pe.wait_ge(S["uq_exp"], 2 * NQ * PAIRS)
            q_features_T(0)
            for h in range(HEADS):
                if h + 1 < HEADS:
                    q_features_T(h + 1)
                pe.wait_ge(S["qfT_ready"], h + 1)
                pe.wait_ge(S["kv_ready"], h // 2 + 1)
                if h >= 2:
                    pe.wait_ge(S["ga_ready"], h - 1)
                for nt in range(NQ):
                    for m in range(M // P):
                        last = mm(ps[:, 6 + h % 2, nt * P:nt * P + DH + 1], qfT[:, h % 2, m, nt * P:(nt + 1) * P], kv[:, h, m, :],
                                  start=(m == 0), stop=(m == M // P - 1))
                last.then_inc(S["ga_mm"], 1)
            pe.wait_ge(S["kv_ready"], 4)
            pe.wait_ge(S["ga_ready"], HEADS)
            for k in range(KD):
                for nt in range(NQ):
                    last = tr(ps[:, k // 2, (k % 2) * SEQ + nt * P:(k % 2) * SEQ + (nt + 1) * P], attnrow[:, nt, k * P:(k + 1) * P],
                              identf[:, :])
                if k % 2:
                    last.then_inc(S["ga_T"], 1)
            pe.wait_ge(S["gaT_ready"], 2)
            for fo in range(KD):
                for k in range(KD):
                    last = mm(ps[:, 2 + fo // 2, (fo % 2) * SEQ:(fo % 2 + 1) * SEQ], gw[3][:, k, fo * P:(fo + 1) * P],
                              attnTg[:, k, :], start=(k == 0), stop=(k == KD - 1))
                if fo % 2:
                    last.then_inc(S["ho_mm"], 1)
            pe.wait_ge(S["hatt_ready"], 2)

            def window(odd, block, pair, step, number):
                pe.wait_ge(S["cnt_ready"], number + 1)
                for i in range(WIN):
                    j = i + ODD * odd
                    g = j // MG
                    if j % MG == 0 and g % 5 == 4:
                        pe.wait_ge(S["ohm_dve"], pair + 1)
                    elif j % MG == 0:
                        pe.wait_ge(S["ohm_act"], pair * 4 + (g + 1 if g < 5 else g))
                    pe.wait_ge(S["oh_ready"], step + (i + 1))
                    mm(ps[:, 4 + 2 * block + odd, 0:WK], ohm[:, (block * PAIRC + j) % (2 * PAIRC), :], ohs[:, i % NB, :],
                       start=(i == 0), stop=(i == WIN - 1)).then_inc(S["oh_used"], 1)

            def degrees(parts, cols):
                for c0, c1 in cols:
                    n = len(parts) * NT
                    for i in range(n):
                        last = mm(ps[:, c0 // 512, 0:c1 - c0], onesb[:, :], parts[i // NT][:, i % NT, c0:c1],
                                  start=(i == 0), stop=(i == n - 1))
                last.then_inc(S["deg_mm"], 1)

            with pe.Fori(0, WN // 4) as it:
                for w in range(4):
                    window(w % 2, w // 2, it * 2 + w // 2, it * (4 * WIN) + w * WIN, it * 4 + w)
            pe.wait_ge(S["cnt_ready"], COLS[1][1] // WT + 1 + 4)
            degrees(AT[0:1], COLS[0:2])
            window(0, 0, WN // 2, (WN - 1) * WIN, WN - 1)

            pe.wait_ge(S["cnt_ready"], WN + 4)
            degrees(AT[0:1], COLS[2:3])
            pe.wait_ge(S["flag_ready"], 1)
            total = pe.value_load(flag[0:1, 0:1], min_val=0, max_val=E)

            def aggregate(parts):
                steps = [(a, x, kt) for a in parts for x in xs for kt in range(NT)]
                for c, (c0, c1) in enumerate(COLS):
                    cn = c1 - c0
                    for k in range(KD):
                        if c >= 1:
                            pe.wait_ge(S["agg_ready"], (c - 1) * KD + k + 1)
                        for i, (a, x, kt) in enumerate(steps):
                            last = mm(ps[:, 3 + k, 0:cn], x[0:sz(kt), kt, k * P:(k + 1) * P], a[0:sz(kt), kt, c0:c1],
                                      start=(i == 0), stop=(i == len(steps) - 1))
                        last.then_inc(S["agg_mm"], 1)
                    pe.wait_ge(S["agg_ready"], (c + 1) * KD)
                    for fo in range(KD):
                        n = c * KD + fo
                        if n >= 2:
                            pe.wait_ge(S["rl_ready"], n - 1)
                        for k in range(KD):
                            last = mm(ps[:, 7 - 7 * (n % 2), 0:cn], wc[:, k, fo * P:(fo + 1) * P], aggT[:, k, 0:cn],
                                      start=(k == 0), stop=(k == KD - 1))
                        last.then_inc(S["conv_mm"], 1)

            pe.wait_ge(S["xs_ready"], NT)
            pe.wait_ge(S["wc_in"], 16)
            with pe.If(total >= E):
                aggregate(AT[0:1])
            with pe.If(total < E):
                with pe.Fori(0, WN) as w:
                    pe.wait_ge(S["gcnt_ready"], w + 1)

                    def group(done, first=False, final=False):
                        for j in range(NBG):
                            pe.wait_ge(S["gcnt_oh_ready"], done + (j + 1))
                            mm(ps[:, 4, 0:WK], ohm[:, j, :], ohg[:, j, :], start=first and j == 0,
                               stop=final and j == NBG - 1).then_inc(S["gcnt_oh_used"], 1)

                    start = w * FULL
                    group(start, first=True)
                    with pe.Fori(1, FULL // NBG - 1) as g:
                        group(start + g * NBG)
                    group(start + (FULL - NBG), final=True)
                pe.wait_ge(S["gcnt_ready"], WN + 1)
                degrees(AT, COLS)
                aggregate(AT)
            pe.wait_ge(S["w_ready"], KD)
            for t in range(NT + 6):
                if t < NT:
                    T_to_rows(lambda k, t: tA[:, k, t * P:t * P + sz(t)], "w_T", "x1_ready", 0, [t])
                if t >= 6:
                    rows_to_T(nrow, "n1_ready", "n1_T", "n1T_raw", 2, [t - 6])
            pe.wait_ge(S["x1T_ready"], KD)
            pe.wait_ge(S["rl_ready"], 3 * KD)

            pe.wait_ge(S["qpad_ready"], 1)
            def project(i):
                for c, (c0, c1) in enumerate(COLS):
                    for k in range(KD):
                        last = mm(ps[:, 3 * i + c, 0:c1 - c0], wst[:, i, k, :], tA[:, k, c0:c1], start=(k == 0), stop=(k == KD - 1))
                last.then_inc(S["k_mm" if i else "q_mm"], 1)

            def attend(pr, more):
                pe.wait_ge(S["pt_dve"], pr * (2 * U + 2) + 1)
                for t in range(NT):
                    bank, col = (6 + t // 4, (t % 4) * P) if t < 8 else (5, 256 + (t - 8) * P)
                    if t == 8:
                        pe.wait_ge(S["qkv_dve"], pr * 4 + 1)
                    for k in range(KD):
                        last = mm(ps[0:sz(t), bank, col:col + P], tA[:, k, t * P:t * P + sz(t)], wst[:, 2, k, :],
                                  start=(k == 0), stop=(k == KD - 1))
                last.then_inc(S["proj_done"], 1)

                def scores(i):
                    t, h = divmod(i, 2)
                    if i >= 2:
                        pe.wait_ge(S["exp_done"], pr * U + (i - 1))
                    for c, (c0, c1) in enumerate(COLS):
                        last = mm(ps[0:sz(t), 3 * (i % 2) + c, 0:c1 - c0], QT[:, h, t * P:t * P + sz(t)], KT[:, c0:c1], start=True, stop=True)
                    last.then_inc(S["s_mm"], 1)

                def bank_free(n):
                    n -= 2
                    if n >= 0:
                        m, r = divmod(n, 3)
                        if n >= 3 * U:
                            pe.wait_ge(S["pt_dve"], pr * (2 * U + 2) + (2 * U + 2 + n - 3 * U))
                        elif r == 1:
                            pe.wait_ge(S["pt_act"], pr * U + (m + 1))
                        else:
                            pe.wait_ge(S["pt_dve"], pr * (2 * U + 2) + (2 * m + r // 2 + 2))

                def weights_T(i, parts):
                    t = i // 2
                    if i < U:
                        pe.wait_ge(S["exp_done"], pr * U + (i + 1))
                    for g in parts:
                        n = 3 * i + g if i < U else 2 * U + i
                        bank_free(n)
                        if i < U:
                            for kt in range(4 * g, min(4 * g + 4, NT)):
                                last = tr(ps[0:sz(kt), 6 + n % 2, (kt % 4) * P:(kt % 4) * P + sz(t)],
                                          Pb[0:sz(t), i % 2, kt * P:kt * P + sz(kt)], identf[0:sz(t), 0:sz(t)])
                        if g == 2 and 1 <= i <= U:
                            m, h = divmod(i - 1, 2)
                            pe.wait_ge(S["pt_dve"], pr * (2 * U + 2) + (2 * i + 1))
                            pe.wait_ge(S["pt_act"], pr * U + i)
                            for kt in range(NT):
                                last = mm(ps[0:sz(m), 6 + n % 2, 256:256 + DH], PT[0:sz(kt), (i - 1) % 2, kt, 0:sz(m)],
                                          V[0:sz(kt), kt, h * DH:(h + 1) * DH], start=(kt == 0), stop=(kt == NT - 1))
                        if g == 2 and i >= 3 and i % 2:
                            r = (i - 3) // 2
                            pe.wait_ge(S["pt_dve"], pr * (2 * U + 2) + (2 * i + 1 if i <= U else 2 * U + 2))
                            last = tr(ps[:, 6 + n % 2, 320:320 + sz(r)], arow[0:sz(r), r % 2, :], identf[0:sz(r), 0:sz(r)])
                        last.then_inc(S["p_T"], 1)

                pe.wait_ge(S["qkv_act"], pr * 3 + 2)
                scores(0)
                pe.wait_ge(S["qkv_dve"], pr * 4 + 3)
                scores(1)
                pe.wait_ge(S["qkv_act"], pr * 3 + 3)
                pe.wait_ge(S["qkv_dve"], pr * 4 + 4)
                for i in range(U + 2):
                    if i < U:
                        weights_T(i, (0,))
                    if i + 2 < U:
                        scores(i + 2)
                    elif more and i < U:
                        if i == U - 2:
                            pe.wait_ge(S["wst_in"], pr * 48 + 96)
                        project(i - (U - 2))
                    weights_T(i, (1, 2) if i < U else (2,))

            pe.wait_ge(S["wst_in"], 48)
            project(0)
            project(1)
            with pe.Fori(0, PAIRS - 1) as pr:
                attend(pr, True)
            attend(PAIRS - 1, False)

            pe.wait_ge(S["wo_in"], 16)
            pe.wait_ge(S["pt_dve"], PAIRS * (2 * U + 2) + 1)
            pe.wait_ge(S["route_in"], 32)
            for t in range(NT + 6):
                if t < NT:
                    if t >= 4:
                        pe.wait_ge(S["xx_ready"], t - 3)
                    for k in range(KD):
                        last = mm(ps[0:sz(t), WO_BANKS[t % 4], :], attnT[:, k, t * P:t * P + sz(t)], wo_s[:, k, :],
                                  start=(k == 0), stop=(k == KD - 1))
                    last.then_inc(S["wo_mm"], 1)
                if 5 <= t < NT + 5:
                    r = t - 5
                    pe.wait_ge(S["x2_ready"], r + 1)
                    if r >= 2:
                        pe.wait_ge(S["x2T_ready"], r - 1)
                    for k in range(KD):
                        last = tr(ps[:, 2 + r % 2, k * P:k * P + sz(r)], nrow[0:sz(r), r, k * P:(k + 1) * P],
                                  identf[0:sz(r), 0:sz(r)])
                    last.then_inc(S["x2_T"], 1)
                if t >= 6:
                    r = t - 6
                    pe.wait_ge(S["x2T_ready"], r + 1)
                    if r >= 2:
                        pe.wait_ge(S["lg_read"], r - 1)
                    for k in range(KD):
                        last = mm(ps[0:sz(r), 4 + r % 2, 0:NEXP], x2T[:, r % 2, k, 0:sz(r)], wr_s[:, k, :],
                                  start=(k == 0), stop=(k == KD - 1))
                    last.then_inc(S["lg_mm"], 1)
            pe.wait_ge(S["O_ready"], 1)
            for t in range(NT):
                o = ps[:, 6 + t // 8, (t % 8) * NEXP:(t % 8 + 1) * NEXP]
                for r in range(t):
                    mm(o, onesb[:, :], O[:, r, :], start=(r == 0), stop=False)
                last = mm(o, tri[:, :], O[:, t, :], start=(t == 0), stop=True)
            last.then_inc(S["pos_mm"], 1)
            for n in range(2 * NT):
                t, k = divmod(n, 2)
                pe.wait_ge(S["pid_ready"], t + 1)
                last = mm(ps[0:CAP, 3, 0:NEXP], pid[0:sz(t), n, :], ohk[k][0:sz(t), t, :], start=(n == 0), stop=(n == 2 * NT - 1))
            last.then_inc(S["tab_mm"], 1)
            pe.wait_ge(S["tabT_ready"], 1)


            def gathered_T(j, arrived, jj):
                pe.wait_ge(xb_in[j], arrived)
                for k in range(KD):
                    last = tr(ps[:, jj, k * P:k * P + CAP], xb[0:CAP, j, k * P:(k + 1) * P], identf[0:CAP, 0:CAP])
                last.then_inc(S["xT_mm"], 1)

            def layer1(slot, arrived, n):
                pe.wait_ge(w_in[slot], arrived)
                pe.wait_ge(S["xT_ready"], n)
                for f in range(F // P):
                    for k in range(KD):
                        last = mm(ps[:, 2 + slot % 2, f * P:f * P + CAP], ring1[slot][:, k, f * P:(f + 1) * P], xT[:, slot % 2, k, :],
                                  start=(k == 0), stop=(k == KD - 1))
                last.then_inc(S["l1_mm"], 1)

            def layer2(slot, n):
                pe.wait_ge(S["gelu_done"], n)
                for f in range(F // P):
                    last = mm(ps[0:CAP, 4 + slot % 2, :], hT[:, slot % 2, f, :], ring2[slot][:, f, :],
                              start=(f == 0), stop=(f == F // P - 1))
                last.then_inc(S["l2_mm"], 1)

            gathered_T(0, 16, 0)
            layer1(0, 32, 1)
            gathered_T(1, 16, 1)
            with pe.Fori(0, NEXP // RW - 1) as it:
                for j in range(RW):
                    layer1((j + 1) % RW, it * 32 + (32 if j + 1 < RW else 64), it * RW + (j + 2))
                    gathered_T((j + 2) % XB, it * 32 + 16 * ((j + 2) // XB + 1), j % 2)
                    pe.wait_ge(S["y_ready"], it * RW + (j + 1))
                    layer2(j, it * RW + (j + 1))
            for s in range(NEXP - RW, NEXP):
                if s + 1 < NEXP:
                    layer1((s + 1) % RW, 32 * ((s + 1) // RW + 1), s + 2)
                if s + 2 < NEXP:
                    gathered_T((s + 2) % XB, 16 * ((s + 2) // XB + 1), s % 2)
                pe.wait_ge(S["y_ready"], s + 1)
                layer2(s % RW, s + 1)
            pe.wait_ge(S["G_ready"], 1)
            for t in range(NT):
                last = tr(ps[0:NEXP, t // 4, (t % 4) * P:(t % 4) * P + sz(t)], G[0:sz(t), t, :], identf[0:sz(t), 0:sz(t)])
                if t % 4 == 3 or t == NT - 1:
                    last.then_inc(S["G_T"], 1)
            pe.wait_ge(S["GT_ready"], 3)
            for t in range(NT):
                if t >= 2:
                    pe.wait_ge(S["acc_ready"], t - 1)
                mm(ps[0:sz(t), 6 + t % 2, :], GT[:, t * P:t * P + sz(t)], b2_s[:, :], start=True, stop=True).then_inc(S["b2_mm"], 1)


_INS = ["x", "src", "dst", "L0_gnn_norm1_g", "L0_gnn_norm1_b", "L0_gnn_norm2_g", "L0_gnn_norm2_b", "L0_gnn_W_conv",
        "L0_gnn_b_conv", "L0_gnn_Wq", "L0_gnn_Wk", "L0_gnn_Wv", "L0_gnn_Wo", "L0_gnn_proj", "L0_ffn_ln1_g", "L0_ffn_ln1_b",
        "L0_ffn_wq", "L0_ffn_wk", "L0_ffn_wv", "L0_ffn_wo", "L0_ffn_ln2_g", "L0_ffn_ln2_b", "L0_ffn_wr", "L0_ffn_w1",
        "L0_ffn_b1", "L0_ffn_w2", "L0_ffn_b2"]


def kernel(**inputs):
    import numpy as _np
    import concourse.bacc as _bacc
    from concourse import mybir as _mybir
    from concourse.bass_utils import run_bass_kernel_spmd as _run

    nc = _bacc.Bacc("TRN2", target_bir_lowering=False, num_devices=1)
    arrays, args = {}, []
    for name in _INS:
        a = _np.ascontiguousarray(inputs[name])
        arrays[f"in_{name}"] = a
        args.append(nc.dram_tensor(f"in_{name}", a.shape, _mybir.dt.from_np(a.dtype), kind="ExternalInput").ap())
    args.append(nc.dram_tensor("out_0", (1250, 512), _mybir.dt.float32, kind="ExternalOutput").ap())
    build(nc, *args)
    r = _run(nc, [arrays], core_ids=[0])
    return r.results[0]["out_0"]
```
